# Optimizing a Trainium2 kernel written in Bass

```python
import numpy as np
import jax
import jax.numpy as jnp

def _softmax(x, axis=-1):
    return jax.nn.softmax(x, axis=axis)

def _gelu(x):
    return jax.nn.gelu(x, approximate=True)

def _silu(x):
    return jax.nn.silu(x)

def _sigmoid(x):
    return jax.nn.sigmoid(x)

def _layernorm(x, axis=-1, eps=1e-05):
    m = jnp.mean(x, axis=axis, keepdims=True)
    v = jnp.var(x, axis=axis, keepdims=True)
    return (x - m) / jnp.sqrt(v + eps)

def _scatter_add(tgt, idx, src, axis=0):
    return tgt.at[idx].add(src)

def _segment_sum(src, seg, n):
    return jax.ops.segment_sum(src, seg, n)
kernel_name = 'mk_seq_postln_d2_jaxref_r4_e419bf'

def setup_inputs(seed: int=0):
    np.random.seed(seed)
    _w = jnp.asarray

    def _L0_attn_setup():
        import math
        import jax, jax.numpy as jnp
        import numpy as np
        D_MODEL = 512
        EXPAND = 2
        D_INNER = EXPAND * D_MODEL
        HEADDIM = 64
        NHEADS = D_INNER // HEADDIM
        D_STATE = 128
        CHUNK = 64
        D_CONV = 4
        NGROUPS = 1
        X_PROJ_DIM = D_INNER + NHEADS + 2 * NGROUPS * D_STATE
        BATCH, SEQLEN = (2, 1024)

        def segsum(x):
            T = x.shape[-1]
            cs = jnp.cumsum(x, axis=-1)
            ss = cs[..., :, None] - cs[..., None, :]
            mask = jnp.tril(jnp.ones((T, T), dtype=bool))
            return jnp.where(mask, ss, -jnp.inf)

        def ssd(X, A, B, C, block_len):
            b, l = (X.shape[0], X.shape[1])
            g = B.shape[2]
            h = X.shape[2] // g
            c = l // block_len
            X = X.astype(jnp.float32).reshape(b, c, block_len, g, h, HEADDIM)
            B = B.astype(jnp.float32).reshape(b, c, block_len, g, D_STATE)
            C = C.astype(jnp.float32).reshape(b, c, block_len, g, D_STATE)
            A = A.astype(jnp.float32).reshape(b, c, block_len, g, h)
            A = jnp.transpose(A, (0, 3, 4, 1, 2))
            A_cumsum = jnp.cumsum(A, axis=-1)
            L = jnp.exp(segsum(A))
            Y_diag = jnp.einsum('bclgn,bcsgn,bghcls,bcsghp->bclghp', C, B, L, X)
            decay_states = jnp.exp(A_cumsum[..., -1:] - A_cumsum)
            states = jnp.einsum('bclgn,bghcl,bclghp->bcghpn', B, decay_states, X)
            init = jnp.zeros_like(states[:, :1])
            states = jnp.concatenate([init, states], axis=1)
            chunk_A = jnp.pad(A_cumsum[..., -1], ((0, 0), (0, 0), (0, 0), (1, 0)))
            decay_chunk = jnp.exp(segsum(chunk_A))
            new_states = jnp.einsum('bghzc,bcghpn->bzghpn', decay_chunk, states)
            states, final_state = (new_states[:, :-1], new_states[:, -1])
            state_decay_out = jnp.exp(A_cumsum)
            Y_off = jnp.einsum('bclgn,bcghpn,bghcl->bclghp', C, states, state_decay_out)
            Y = (Y_diag + Y_off).reshape(b, l, g * h, HEADDIM)
            final_state = final_state.reshape(b, g * h, HEADDIM, D_STATE)
            return (Y, final_state)
        key = jax.random.key(seed)
        ks = jax.random.split(key, 8)
        s = 0.02
        u = jax.random.uniform(ks[6], (NHEADS,))
        dt0 = jnp.exp(u * (math.log(0.1) - math.log(0.001)) + math.log(0.001))
        inv_dt = dt0 + jnp.log(-jnp.expm1(-dt0))
        dt_std = NHEADS ** (-0.5)
        return {'x': jax.random.normal(ks[0], (BATCH, SEQLEN, D_MODEL), jnp.float32), 'in_proj_w': jax.random.normal(ks[1], (2 * D_INNER, D_MODEL), jnp.float32) * s, 'conv_w': jax.random.normal(ks[2], (D_INNER, D_CONV), jnp.float32) * s, 'conv_b': jnp.zeros((D_INNER,), jnp.float32), 'x_proj_w': jax.random.normal(ks[3], (X_PROJ_DIM, D_INNER), jnp.float32) * s, 'dt_proj_w': jax.random.uniform(ks[4], (NHEADS, NHEADS), jnp.float32, -dt_std, dt_std), 'dt_proj_b': inv_dt, 'A_log': jnp.log(jnp.arange(1, NHEADS + 1, dtype=jnp.float32)), 'D': jnp.ones((NHEADS,), jnp.float32), 'out_proj_w': jax.random.normal(ks[5], (D_MODEL, D_INNER), jnp.float32) * s}
    _L0_attn_in = _L0_attn_setup()

    def _L0_ffn_setup():
        import jax, jax.numpy as jnp
        import numpy as np
        N_BLOCKS = 16
        BLOCK_SIZE = 128
        TOP_K = N_BLOCKS // 4
        key = jax.random.key(seed)
        k1, k2, k3, k4, k5 = jax.random.split(key, 5)
        in_f, out_f = (512, 2048)
        x = jax.random.normal(k1, (2, 1024, in_f), dtype=jnp.float32)
        Wr = jax.random.normal(k2, (N_BLOCKS, in_f), dtype=jnp.float32) * in_f ** (-0.5)
        br = jnp.zeros((N_BLOCKS,), dtype=jnp.float32)
        W1 = jax.random.normal(k3, (out_f, in_f), dtype=jnp.float32) * in_f ** (-0.5)
        W2 = jax.random.normal(k4, (in_f, out_f), dtype=jnp.float32) * out_f ** (-0.5)
        return {'x': x, 'Wr': Wr, 'br': br, 'W1': W1, 'W2': W2}
    _L0_ffn_in = _L0_ffn_setup()

    def _L1_attn_setup():
        import jax, jax.numpy as jnp
        import numpy as np
        EPS = 1e-15
        HEAD_DIM = 32
        PAD_VAL = 1.0
        key = jax.random.key(seed)
        k1, k2, k3, k4 = jax.random.split(key, 4)
        B, N, C = (2, 1024, 512)
        s = 1.0 / np.sqrt(C).astype(np.float32)
        x = jax.random.normal(k1, (B, N, C), jnp.float32)
        w_qkv = jax.random.normal(k2, (3 * C, C), jnp.float32) * s
        w_proj = jax.random.normal(k3, (C, C), jnp.float32) * s
        b_proj = jax.random.normal(k4, (C,), jnp.float32) * 0.01
        return {'x': x, 'w_qkv': w_qkv, 'w_proj': w_proj, 'b_proj': b_proj}
    _L1_attn_in = _L1_attn_setup()

    def _L1_ffn_setup():
        import jax, jax.numpy as jnp
        import numpy as np
        import math
        GOLDEN_CENTER = 1.0 / math.e
        GOLDEN_LOWER = 0.5 - math.log(4.0 / 3.0)
        GOLDEN_UPPER = 0.5
        B, T, D = (4, 256, 512)
        E = 8
        F = 2048 // (E // 2)
        R = 64
        NL = 2

        def _router_weights(x, Wr, temperature):
            logits = jnp.einsum('btd,de->bte', x, Wr)
            inhibition = jax.nn.sigmoid(logits / temperature)
            in_zone = (inhibition >= GOLDEN_LOWER) & (inhibition <= GOLDEN_UPPER)
            distance = jnp.abs(inhibition - GOLDEN_CENTER)
            w = jnp.exp(-distance / 0.1) * in_zone.astype(x.dtype)
            wsum = w.sum(axis=-1, keepdims=True)
            no_expert = wsum < 1e-08
            fb = jnp.exp(-distance / 0.3)
            _, top2 = jax.lax.top_k(fb, 2)
            fb_mask = jax.nn.one_hot(top2, E, dtype=x.dtype).sum(axis=-2)
            fb_w = fb * fb_mask
            fb_w = fb_w / jnp.clip(fb_w.sum(axis=-1, keepdims=True), 1e-08)
            w = jnp.where(no_expert, fb_w, w)
            return w / jnp.clip(w.sum(axis=-1, keepdims=True), 1e-08)
        key = jax.random.key(seed)
        ks = jax.random.split(key, 13)
        s = 0.02
        x = jax.random.normal(ks[0], (B, T, D), dtype=jnp.float32)
        Wg = jax.random.normal(ks[1], (E, D, F), dtype=jnp.float32) * s
        Wu = jax.random.normal(ks[2], (E, D, F), dtype=jnp.float32) * s
        Wd = jax.random.normal(ks[3], (E, F, D), dtype=jnp.float32) * s
        Ga = jax.random.normal(ks[4], (NL, D, R), dtype=jnp.float32) * s
        Gb = jax.random.normal(ks[5], (NL, R, F), dtype=jnp.float32) * s
        Ua = jax.random.normal(ks[6], (NL, D, R), dtype=jnp.float32) * s
        Ub = jax.random.normal(ks[7], (NL, R, F), dtype=jnp.float32) * s
        Da = jax.random.normal(ks[8], (NL, F, R), dtype=jnp.float32) * s
        Db = jax.random.normal(ks[9], (NL, R, D), dtype=jnp.float32) * s
        Wr = jax.random.normal(ks[10], (D, E), dtype=jnp.float32) * s
        temperature = jnp.ones((1,), dtype=jnp.float32)
        return {'x': x, 'Wg': Wg, 'Wu': Wu, 'Wd': Wd, 'Ga': Ga, 'Gb': Gb, 'Ua': Ua, 'Ub': Ub, 'Da': Da, 'Db': Db, 'Wr': Wr, 'temperature': temperature}
    _L1_ffn_in = _L1_ffn_setup()
    _d = {'L0_attn_x': _L0_attn_in['x'], 'L0_attn_in_proj_w': _L0_attn_in['in_proj_w'], 'L0_attn_conv_w': _L0_attn_in['conv_w'], 'L0_attn_conv_b': _L0_attn_in['conv_b'], 'L0_attn_x_proj_w': _L0_attn_in['x_proj_w'], 'L0_attn_dt_proj_w': _L0_attn_in['dt_proj_w'], 'L0_attn_dt_proj_b': _L0_attn_in['dt_proj_b'], 'L0_attn_A_log': _L0_attn_in['A_log'], 'L0_attn_D': _L0_attn_in['D'], 'L0_attn_out_proj_w': _L0_attn_in['out_proj_w'], 'L0_ffn_Wr': _L0_ffn_in['Wr'], 'L0_ffn_br': _L0_ffn_in['br'], 'L0_ffn_W1': _L0_ffn_in['W1'], 'L0_ffn_W2': _L0_ffn_in['W2'], 'L1_attn_w_qkv': _L1_attn_in['w_qkv'], 'L1_attn_w_proj': _L1_attn_in['w_proj'], 'L1_attn_b_proj': _L1_attn_in['b_proj'], 'L1_ffn_Wg': _L1_ffn_in['Wg'], 'L1_ffn_Wu': _L1_ffn_in['Wu'], 'L1_ffn_Wd': _L1_ffn_in['Wd'], 'L1_ffn_Ga': _L1_ffn_in['Ga'], 'L1_ffn_Gb': _L1_ffn_in['Gb'], 'L1_ffn_Ua': _L1_ffn_in['Ua'], 'L1_ffn_Ub': _L1_ffn_in['Ub'], 'L1_ffn_Da': _L1_ffn_in['Da'], 'L1_ffn_Db': _L1_ffn_in['Db'], 'L1_ffn_Wr': _L1_ffn_in['Wr'], 'L1_ffn_temperature': _L1_ffn_in['temperature']}
    _x0 = _d['L0_attn_x']
    _d['L0_attn_x'] = jax.random.normal(jax.random.fold_in(jax.random.key(seed), 1), (4, 512, 512), dtype=_x0.dtype)
    del _x0
    return _d

def reference(L0_attn_x, L0_attn_in_proj_w, L0_attn_conv_w, L0_attn_conv_b, L0_attn_x_proj_w, L0_attn_dt_proj_w, L0_attn_dt_proj_b, L0_attn_A_log, L0_attn_D, L0_attn_out_proj_w, L0_ffn_Wr, L0_ffn_br, L0_ffn_W1, L0_ffn_W2, L1_attn_w_qkv, L1_attn_w_proj, L1_attn_b_proj, L1_ffn_Wg, L1_ffn_Wu, L1_ffn_Wd, L1_ffn_Ga, L1_ffn_Gb, L1_ffn_Ua, L1_ffn_Ub, L1_ffn_Da, L1_ffn_Db, L1_ffn_Wr, L1_ffn_temperature):

    def _L0_attn_ref(x, in_proj_w, conv_w, conv_b, x_proj_w, dt_proj_w, dt_proj_b, A_log, D, out_proj_w):
        import math
        import jax, jax.numpy as jnp
        import numpy as np
        D_MODEL = 512
        EXPAND = 2
        D_INNER = EXPAND * D_MODEL
        HEADDIM = 64
        NHEADS = D_INNER // HEADDIM
        D_STATE = 128
        CHUNK = 64
        D_CONV = 4
        NGROUPS = 1
        X_PROJ_DIM = D_INNER + NHEADS + 2 * NGROUPS * D_STATE
        BATCH, SEQLEN = (2, 1024)

        def segsum(x):
            T = x.shape[-1]
            cs = jnp.cumsum(x, axis=-1)
            ss = cs[..., :, None] - cs[..., None, :]
            mask = jnp.tril(jnp.ones((T, T), dtype=bool))
            return jnp.where(mask, ss, -jnp.inf)

        def ssd(X, A, B, C, block_len):
            b, l = (X.shape[0], X.shape[1])
            g = B.shape[2]
            h = X.shape[2] // g
            c = l // block_len
            X = X.astype(jnp.float32).reshape(b, c, block_len, g, h, HEADDIM)
            B = B.astype(jnp.float32).reshape(b, c, block_len, g, D_STATE)
            C = C.astype(jnp.float32).reshape(b, c, block_len, g, D_STATE)
            A = A.astype(jnp.float32).reshape(b, c, block_len, g, h)
            A = jnp.transpose(A, (0, 3, 4, 1, 2))
            A_cumsum = jnp.cumsum(A, axis=-1)
            L = jnp.exp(segsum(A))
            Y_diag = jnp.einsum('bclgn,bcsgn,bghcls,bcsghp->bclghp', C, B, L, X)
            decay_states = jnp.exp(A_cumsum[..., -1:] - A_cumsum)
            states = jnp.einsum('bclgn,bghcl,bclghp->bcghpn', B, decay_states, X)
            init = jnp.zeros_like(states[:, :1])
            states = jnp.concatenate([init, states], axis=1)
            chunk_A = jnp.pad(A_cumsum[..., -1], ((0, 0), (0, 0), (0, 0), (1, 0)))
            decay_chunk = jnp.exp(segsum(chunk_A))
            new_states = jnp.einsum('bghzc,bcghpn->bzghpn', decay_chunk, states)
            states, final_state = (new_states[:, :-1], new_states[:, -1])
            state_decay_out = jnp.exp(A_cumsum)
            Y_off = jnp.einsum('bclgn,bcghpn,bghcl->bclghp', C, states, state_decay_out)
            Y = (Y_diag + Y_off).reshape(b, l, g * h, HEADDIM)
            final_state = final_state.reshape(b, g * h, HEADDIM, D_STATE)
            return (Y, final_state)
        b, l, _ = x.shape
        xz = x @ in_proj_w.T
        x_branch, z_branch = jnp.split(xz, 2, axis=-1)
        xt = jnp.transpose(x_branch, (0, 2, 1))
        kern = conv_w[:, None, :]
        y = jax.lax.conv_general_dilated(xt, kern, window_strides=(1,), padding=[(D_CONV - 1, 0)], dimension_numbers=('NCH', 'OIH', 'NCH'), feature_group_count=D_INNER)
        x_branch = jnp.transpose(y + conv_b[None, :, None], (0, 2, 1))
        x_branch = jax.nn.silu(x_branch)
        proj = x_branch @ x_proj_w.T
        X = proj[..., :D_INNER].reshape(b, l, NHEADS, HEADDIM)
        dt = proj[..., D_INNER:D_INNER + NHEADS]
        Bm = proj[..., D_INNER + NHEADS:D_INNER + NHEADS + NGROUPS * D_STATE].reshape(b, l, NGROUPS, D_STATE)
        Cm = proj[..., D_INNER + NHEADS + NGROUPS * D_STATE:].reshape(b, l, NGROUPS, D_STATE)
        dt = jax.nn.softplus(dt @ dt_proj_w.T + dt_proj_b)
        A = -jnp.exp(A_log)
        X_scaled = X * dt[..., None]
        A_scaled = A[None, None, :] * dt
        Y, _ = ssd(X_scaled, A_scaled, Bm, Cm, CHUNK)
        Y = Y.astype(x.dtype)
        Y = Y + X * D[None, None, :, None]
        Y = Y.reshape(b, l, D_INNER)
        Y = Y * jax.nn.silu(z_branch)
        return Y @ out_proj_w.T

    def _L0_ffn_ref(x, Wr, br, W1, W2):
        import jax, jax.numpy as jnp
        import numpy as np
        N_BLOCKS = 16
        BLOCK_SIZE = 128
        TOP_K = N_BLOCKS // 4
        x_shape = x.shape
        in_f = x_shape[-1]
        xf = x.reshape(-1, in_f)
        n = xf.shape[0]
        prob = jax.nn.softmax(xf @ Wr.T + br, axis=-1)
        _, idx = jax.lax.top_k(prob, TOP_K)
        mask = jnp.zeros((n, N_BLOCKS), dtype=xf.dtype)
        mask = mask.at[jnp.arange(n)[:, None], idx].set(1.0)
        W1b = W1.reshape(N_BLOCKS, BLOCK_SIZE, in_f)
        h = jnp.einsum('nf,ibf->nib', xf, W1b)
        h = jax.nn.gelu(h, approximate=False) * mask[:, :, None]
        W2b = W2.reshape(in_f, N_BLOCKS, BLOCK_SIZE)
        y = jnp.einsum('nib,fib->nf', h, W2b)
        return y.reshape(x_shape)

    def _L1_attn_ref(x, w_qkv, w_proj, b_proj):
        import jax, jax.numpy as jnp
        import numpy as np
        EPS = 1e-15
        HEAD_DIM = 32
        PAD_VAL = 1.0
        B, N, C = x.shape
        d = HEAD_DIM
        h = C // d
        qkv = (x @ w_qkv.T).reshape(B, N, 3, C)
        q, k, v = (qkv[:, :, 0], qkv[:, :, 1], qkv[:, :, 2])

        def to_heads(t):
            return t.reshape(B, N, h, d).transpose(0, 2, 3, 1)
        q = jax.nn.relu(to_heads(q))
        k = jax.nn.relu(to_heads(k))
        v = to_heads(v)
        v_pad = jnp.pad(v, ((0, 0), (0, 0), (0, 1), (0, 0)), constant_values=PAD_VAL)
        vk = jnp.einsum('bhen,bhdn->bhed', v_pad, k)
        out = jnp.einsum('bhed,bhdn->bhen', vk, q)
        out = out[:, :, :-1] / (out[:, :, -1:] + EPS)
        out = out.reshape(B, C, N).transpose(0, 2, 1)
        return out @ w_proj.T + b_proj

    def _L1_ffn_ref(x, Wg, Wu, Wd, Ga, Gb, Ua, Ub, Da, Db, Wr, temperature):
        import jax, jax.numpy as jnp
        import numpy as np
        import math
        GOLDEN_CENTER = 1.0 / math.e
        GOLDEN_LOWER = 0.5 - math.log(4.0 / 3.0)
        GOLDEN_UPPER = 0.5
        B, T, D = (4, 256, 512)
        E = 8
        F = 2048 // (E // 2)
        R = 64
        NL = 2

        def _router_weights(x, Wr, temperature):
            logits = jnp.einsum('btd,de->bte', x, Wr)
            inhibition = jax.nn.sigmoid(logits / temperature)
            in_zone = (inhibition >= GOLDEN_LOWER) & (inhibition <= GOLDEN_UPPER)
            distance = jnp.abs(inhibition - GOLDEN_CENTER)
            w = jnp.exp(-distance / 0.1) * in_zone.astype(x.dtype)
            wsum = w.sum(axis=-1, keepdims=True)
            no_expert = wsum < 1e-08
            fb = jnp.exp(-distance / 0.3)
            _, top2 = jax.lax.top_k(fb, 2)
            fb_mask = jax.nn.one_hot(top2, E, dtype=x.dtype).sum(axis=-2)
            fb_w = fb * fb_mask
            fb_w = fb_w / jnp.clip(fb_w.sum(axis=-1, keepdims=True), 1e-08)
            w = jnp.where(no_expert, fb_w, w)
            return w / jnp.clip(w.sum(axis=-1, keepdims=True), 1e-08)
        weights = _router_weights(x, Wr, temperature)
        gate = jnp.einsum('btd,edf->ebtf', x, Wg)
        up = jnp.einsum('btd,edf->ebtf', x, Wu)
        gate = gate.at[:NL].add(jnp.einsum('btd,edr,erf->ebtf', x, Ga, Gb))
        up = up.at[:NL].add(jnp.einsum('btd,edr,erf->ebtf', x, Ua, Ub))
        mid = jax.nn.silu(gate) * up
        out = jnp.einsum('ebtf,efd->ebtd', mid, Wd)
        out = out.at[:NL].add(jnp.einsum('ebtf,efr,erd->ebtd', mid[:NL], Da, Db))
        return jnp.einsum('bte,ebtd->btd', weights, out)
    x = L0_attn_x
    x = _layernorm(x + _L0_attn_ref(x, L0_attn_in_proj_w, L0_attn_conv_w, L0_attn_conv_b, L0_attn_x_proj_w, L0_attn_dt_proj_w, L0_attn_dt_proj_b, L0_attn_A_log, L0_attn_D, L0_attn_out_proj_w), axis=-1)
    x = _layernorm(x + _L0_ffn_ref(x, L0_ffn_Wr, L0_ffn_br, L0_ffn_W1, L0_ffn_W2), axis=-1)
    x = _layernorm(x + _L1_attn_ref(x, L1_attn_w_qkv, L1_attn_w_proj, L1_attn_b_proj), axis=-1)
    x = _layernorm(x + _L1_ffn_ref(x, L1_ffn_Wg, L1_ffn_Wu, L1_ffn_Wd, L1_ffn_Ga, L1_ffn_Gb, L1_ffn_Ua, L1_ffn_Ub, L1_ffn_Da, L1_ffn_Db, L1_ffn_Wr, L1_ffn_temperature), axis=-1)
    return x

_drawn_inputs = setup_inputs


def setup_inputs(seed=0):
    import zlib

    import numpy as np

    out = dict(_drawn_inputs(seed))
    spreads = {'L0_attn_conv_b': (0.0, 0.1), 'L0_attn_D': (1.0, 0.6), 'L0_ffn_br': (0.0, 0.1)}
    factors = {'L0_attn_conv_w': 4.381,
     'L0_attn_dt_proj_w': 8.0,
     'L0_attn_dt_proj_b': 8.0,
     'L0_attn_A_log': 8.0,
     'L1_attn_b_proj': 6.003,
     'L1_ffn_Ga': 8.0,
     'L1_ffn_Gb': 8.0,
     'L1_ffn_Ua': 8.0,
     'L1_ffn_Ub': 8.0,
     'L1_ffn_Da': 8.0,
     'L1_ffn_Db': 8.0}
    for name, (base, spread) in spreads.items():
        noise = np.random.default_rng([zlib.crc32(name.encode()), seed]).standard_normal(out[name].shape)
        drawn = base * np.exp(spread * noise) if base else spread * noise
        out[name] = jnp.asarray(drawn.astype(out[name].dtype))
    for name, factor in factors.items():
        out[name] = (out[name] * factor).astype(out[name].dtype)
    return out
```

```python
from contextlib import ExitStack

import concourse.bass as bass
from concourse import mybir

F32 = mybir.dt.float32
F32R = mybir.dt.float32r
ALU = mybir.AluOpType
ACT = mybir.ActivationFunctionType
AX_X = mybir.AxisListType.X

P = 128
NB, SEQ, DM = 4, 512, 512
TOK = NB * SEQ
NCH = TOK // P
CPB = SEQ // P
KT = DM // P
DI = 2 * DM
IT = DI // P
NH, HD = 16, 64
NS = 128
TAPS = 4
EPS = 1e-5


class Kit:

    def __init__(self, nc, ctx, tag):
        self.nc, self.ctx, self.tag, self.sems = nc, ctx, tag, []
        ctx.callback(self.close)

    def sb(self, name, shape, dt=F32):
        return self.ctx.enter_context(self.nc.sbuf_tensor(f"{self.tag}_{name}", shape, dt))

    def ps(self, name, shape):
        return self.ctx.enter_context(self.nc.psum_tensor(f"{self.tag}_{name}", shape, F32))

    def sem(self, name):
        self.sems.append(self.nc.alloc_semaphore(f"{self.tag}_{name}"))
        return self.sems[-1]

    def close(self):
        self.nc.clear_and_free_semaphores(self.sems)
        self.nc.all_engine_barrier()

    def block(self):
        return self.ctx.enter_context(self.nc.Block())


class Chain:

    def __init__(self, eng, sem, per):
        self.eng, self.sem, self.per, self.base, self.k = eng, sem, per, 0, 0

    def round(self, g):
        self.base, self.k = g * self.per, 0

    def link(self, ins):
        self.k += 1
        ins.then_inc(self.sem, 1)
        self.eng.wait_ge(self.sem, self.base + self.k)

    def close(self):
        assert self.k <= self.per, (self.k, self.per)
        if self.k < self.per:
            self.eng.sem_inc(self.sem, self.per - self.k)
            self.k = self.per


def raw(ap):
    return ap.bitcast(F32)


def product(pe, out, lhs, rhs, first=True, last=True):
    (lh, ll), (rh, rl) = lhs, rhs
    pe.matmul(out, lh, rh, start=first, stop=False)
    pe.matmul(out, lh, rl, start=False, stop=False)
    return pe.matmul(out, ll, rh, start=False, stop=last)


def in_proj(nc, t):
    with ExitStack() as ctx:
        k = Kit(nc, ctx, "in")
        MT = 2 * IT
        GRP = 4
        TPG = MT // GRP
        x_tok = k.sb("x_tok", [P, NB, CPB, DM])
        x_hi, x_lo = k.sb("x_hi", [P, KT, TOK], F32R), k.sb("x_lo", [P, KT, TOK], F32R)
        w_raw = k.sb("w_raw", [P, 2, KT, TPG * P])
        w_hi, w_lo = (k.sb(n, [P, GRP, KT, TPG * P], F32R) for n in ("w_hi", "w_lo"))
        conv = k.sb("conv", [P, 2, SEQ])
        out = k.sb("out", [P, 4, SEQ])
        cw = k.sb("cw", [P, IT, TAPS])
        cb = k.sb("cb", [P, IT])
        ident = k.sb("ident", [P, P])
        tp = k.ps("tp", [P, 4, 512])
        acc = k.ps("acc", [P, 4, 512])

        s_x = [k.sem(f"x_loaded{b}") for b in range(NB)]
        s_w = [k.sem(f"w_loaded{g}") for g in range(2)]
        s_small = k.sem("conv_params_loaded")
        s_ident = k.sem("ident_ready")
        s_xT = k.sem("x_transposed")
        s_xhi, s_xlo = k.sem("x_hi_ready"), k.sem("x_lo_ready")
        s_whi, s_wlo = k.sem("w_hi_ready"), k.sem("w_lo_ready")
        s_xacc, s_zacc = k.sem("x_tile_summed"), k.sem("z_tile_summed")
        s_taps = k.sem("conv_taps_added")
        s_c = k.sem("conv_tile_started")
        s_xo, s_zo = k.sem("x_tile_out"), k.sem("z_tile_out")
        s_st = [k.sem(f"stored{i}") for i in range(4)]
        block = k.block()

        @block.sync
        def _(sp):
            for b in range(NB):
                sp.dma_start(x_tok[:, b], t["x"][b].rearrange("(c p) d -> p c d", p=P)).then_inc(s_x[b], 16)
                if b == 0:
                    sp.dma_start(cw[:], t["conv_w"]).then_inc(s_small, 16)
                    sp.dma_start(cb[:], t["conv_b"]).then_inc(s_small, 16)
                if b >= 2:
                    sp.wait_ge(s_wlo, b - 1)
                sp.dma_start(w_raw[:, b % 2], t["in_w"][:, b]).then_inc(s_w[b % 2], 16)
            for i in range(4):
                sp.sem_inc(s_st[i], 16)
            with sp.Fori(0, NB) as b:
                for j in range(IT):
                    sp.wait_ge(s_xo, b * IT + j + 1 + 2)
                    sp.dma_start(t["xb"][j][:, bass.ts(b, SEQ)], out[:, 2 * j % 4]).then_inc(s_st[2 * j % 4], 16)
                    sp.wait_ge(s_zo, b * IT + j + 1 + 2)
                    sp.dma_start(t["zs"][j][:, bass.ts(b, SEQ)], out[:, (2 * j + 1) % 4]).then_inc(s_st[(2 * j + 1) % 4], 16)
            for i in range(4):
                sp.wait_ge(s_st[i], 16 * (NB * MT // 4 + 1))

        @block.gpsimd
        def _(pool):
            nc.gpsimd.memset(ident[:], 0.0).then_inc(s_ident, 1)
            pool.wait_ge(s_ident, 1)
            nc.gpsimd.affine_select(out=ident[:], in_=ident[:], compare_op=ALU.not_equal, fill=1.0, base=0,
                                    pattern=[[-1, P]], channel_multiplier=1).then_inc(s_ident, 1)

        @block.tensor
        def _(pe):
            pe.wait_ge(s_ident, 2)
            for b in range(NB):
                pe.wait_ge(s_x[b], 16)
                for kt in range(KT):
                    n = b * KT + kt
                    if n >= 4:
                        pe.wait_ge(s_xlo, n - 3)
                    for c in range(CPB):
                        ins = pe.transpose(tp[:, n % 4, bass.ts(c, P)], x_tok[:, b, c, bass.ts(kt, P)], ident[:])
                    ins.then_inc(s_xT, 1)
            with pe.Fori(0, NB) as b:
                pe.wait_ge(s_xlo, b * KT + KT)
                for m in range(MT):
                    if m % TPG == 0:
                        pe.wait_ge(s_wlo, m // TPG + 1)
                    n = b * IT + m // 2
                    if m % 2:
                        pe.wait_ge(s_zo, n - 1 + 2)
                    else:
                        pe.wait_ge(s_taps, 3 * (n - 1) + 6)
                    col = bass.ts(m % TPG, P)
                    for kt in range(KT):
                        ins = product(pe, acc[:, m % 4],
                                      (w_hi[:, m // TPG, kt, col], w_lo[:, m // TPG, kt, col]),
                                      (x_hi[:, kt, bass.ts(b, SEQ)], x_lo[:, kt, bass.ts(b, SEQ)]),
                                      kt == 0, kt == KT - 1)
                    ins.then_inc(s_zacc if m % 2 else s_xacc, 1)

        @block.scalar
        def _(act):
            act.sem_inc(s_xo, 2)
            act.sem_inc(s_zo, 2)

            def hi_of_x(b):
                for kt in range(KT):
                    n = b * KT + kt
                    act.wait_ge(s_xT, n + 1)
                    nc.scalar.activation(x_hi[:, kt, bass.ts(b, SEQ)], tp[:, n % 4], ACT.Copy).then_inc(s_xhi, 1)

            def hi_of_w(g):
                act.wait_ge(s_w[g % 2], 16 * (g // 2 + 1))
                nc.scalar.activation(w_hi[:, g], w_raw[:, g % 2], ACT.Copy).then_inc(s_whi, 1)

            for b in range(NB):
                hi_of_x(b)
                hi_of_w(b)
            act.wait_ge(s_small, 32)
            with act.Fori(0, NB) as b:
                for j in range(IT):
                    n = b * IT + j
                    act.wait_ge(s_xacc, n + 1)
                    act.wait_ge(s_xo, n - 1 + 2)
                    nc.scalar.activation(conv[:, j % 2], acc[:, 2 * j % 4], ACT.Identity,
                                         bias=cb[:, j:j + 1], scale=cw[:, j, TAPS - 1:TAPS]).then_inc(s_c, 1)
                    slot, turn = 2 * j % 4, 16 * (b * (MT // 4) + 2 * j // 4 + 1)
                    act.wait_ge(s_taps, 3 * (n + 1) + 6)
                    act.wait_ge(s_st[slot], turn)
                    nc.scalar.activation(out[:, slot], conv[:, j % 2], ACT.Silu).then_inc(s_xo, 1)
                    act.wait_ge(s_zacc, n + 1)
                    act.wait_ge(s_st[slot + 1], turn)
                    nc.scalar.activation(out[:, slot + 1], acc[:, slot + 1], ACT.Silu).then_inc(s_zo, 1)

        @block.vector
        def _(dve):
            dve.sem_inc(s_taps, 6)
            for b in range(NB):
                for kt in range(KT):
                    n = b * KT + kt
                    dve.wait_ge(s_xhi, n + 1)
                    x = bass.ts(b, SEQ)
                    nc.vector.tensor_tensor(x_lo[:, kt, x], tp[:, n % 4], raw(x_hi[:, kt, x]),
                                            ALU.subtract).then_inc(s_xlo, 1)
                dve.wait_ge(s_whi, b + 1)
                nc.vector.tensor_tensor(w_lo[:, b], w_raw[:, b % 2], raw(w_hi[:, b]), ALU.subtract).then_inc(s_wlo, 1)
            with dve.Fori(0, NB) as b:
                for j in range(IT):
                    n = b * IT + j
                    dve.wait_ge(s_c, n + 1)
                    for d in range(1, TAPS):
                        dve.wait_ge(s_taps, 3 * n + d - 1 + 6)
                        nc.vector.scalar_tensor_tensor(
                            out=conv[:, j % 2, d:SEQ], in0=acc[:, 2 * j % 4, 0:SEQ - d],
                            scalar=cw[:, j, TAPS - 1 - d:TAPS - d], in1=conv[:, j % 2, d:SEQ],
                            op0=ALU.mult, op1=ALU.add).then_inc(s_taps, 1)


def layer_norm_stats(nc, dve, x, stats, mv, s_bn, sem, n, met):
    n = n if isinstance(n, int) else dve.snap(n)
    nc.vector.bn_stats(stats, x).then_inc(s_bn, 1)
    dve.wait_ge(met, 1)
    dve.wait_ge(s_bn, n)
    nc.vector.bn_aggr(mv, stats).then_inc(sem, 1)


def inverse_deviation(nc, pool, mv, rstd, const, s_mv, s_eps, s_rstd, n):
    pool.wait_ge(s_mv, n)
    nc.gpsimd.tensor_tensor(rstd, mv[:, 1:2], const[:, 0:1], ALU.add).then_inc(s_eps, 1)
    pool.wait_ge(s_eps, n)
    nc.gpsimd.tensor_tensor(rstd, rstd, const[:, 1:2], ALU.pow).then_inc(s_rstd, 1)


def make_identity(nc, pool, ident, sem):
    nc.gpsimd.memset(ident, 0.0).then_inc(sem, 1)
    pool.wait_ge(sem, 1)
    nc.gpsimd.affine_select(out=ident, in_=ident, compare_op=ALU.not_equal, fill=1.0, base=0,
                            pattern=[[-1, P]], channel_multiplier=1).then_inc(sem, 1)


def ssd_phase(nc, t):
    with ExitStack() as ctx:
        k = Kit(nc, ctx, "ssd")
        XC = DI + NH + 2 * NS
        BC = NH + 2 * NS
        wx_hi, wx_lo = (k.sb(n, [P, IT, XC], F32R) for n in ("wx_hi", "wx_lo"))
        wo_hi, wo_lo = (k.sb(n, [P, IT, DM], F32R) for n in ("wo_hi", "wo_lo"))
        x_raw = k.sb("x_raw", [P, IT, P])
        x_hi, x_lo = k.sb("x_hi", [P, IT, P], F32R), k.sb("x_lo", [P, IT, P], F32R)
        z_raw = k.sb("z_raw", [P, IT, P])
        res = k.sb("res", [P, DM])
        bcd = k.sb("bcd", [P, BC])
        bct = k.sb("bct", [P, 2 * NS])
        b_tok = k.sb("b_tok", [P, NS])
        dtT = k.sb("dtT", [NH, P])
        xf = k.sb("xf", [P, NH, HD])
        xs = k.sb("xs", [P, NH, HD])
        xd = k.sb("xd", [P, NH, HD])
        xdec = k.sb("xdec", [P, NH, HD])
        r_hi, r_lo = k.sb("r_hi", [P, NH, P], F32R), k.sb("r_lo", [P, NH, P], F32R)
        decay = k.sb("decay", [P, NH, P])
        mix = k.sb("mix", [P, NH, P])
        state = k.sb("state", [P, NH, HD])
        y = k.sb("y", [P, NH, HD])
        g_f = k.sb("g_f", [P, IT, P])
        g_hi, g_lo = k.sb("g_hi", [P, IT, P], F32R), k.sb("g_lo", [P, IT, P], F32R)
        rr = k.sb("rr", [P, DM])
        cb_m = k.sb("cb_m", [P, P])
        tri = k.sb("tri", [P, P])
        strict_r = k.sb("strict_r", [P, P], F32R)
        ones, ident = k.sb("ones", [P, P]), k.sb("ident", [P, P])
        keep = k.sb("keep", [P, NCH])
        dtw = k.sb("dtw", [NH, NH])
        dtb, a_pos, d_skip = (k.sb(n, [P, NH]) for n in ("dtb", "a_pos", "d_skip"))
        v, na, u, s2, q, dt, a = (k.sb(n, [P, NH]) for n in ("v", "na", "u", "s2", "q", "dt", "a"))
        s1 = na
        a_hi, a_lo = k.sb("a_hi", [P, NH], F32R), k.sb("a_lo", [P, NH])
        ed = k.sb("ed", [P, 3, NH])
        ek = k.sb("ek", [P, NH])
        stats, mv = k.sb("stats", [P, 6]), k.sb("mv", [P, 2])
        rstd, const = k.sb("rstd", [P, 1]), k.sb("const", [P, 2])
        pa, pb, po, psm = (k.ps(n, [P, 512]) for n in ("pa", "pb", "po", "psm"))
        pd = k.ps("pd", [P, 4, 512])
        CB, DTP, SUM = psm[:, 0:P], psm[:, 384:384 + NH], psm[:, 400:400 + 3 * NH]
        staging = (decay[:].rearrange("p h l -> p (h l)"), mix[:].rearrange("p h l -> p (h l)"))
        WG = IT + IT // 2

        s_const, s_tri, s_ident = k.sem("constants_ready"), k.sem("triangles_ready"), k.sem("ident_ready")
        s_small = k.sem("small_loaded")
        s_w = [k.sem(f"w_loaded{i}") for i in range(2)]
        s_whi, s_wlo = k.sem("w_hi_ready"), k.sem("w_lo_ready")
        s_lx, s_lz, s_lr = k.sem("x_loaded"), k.sem("z_loaded"), k.sem("residual_loaded")
        s_apos, s_strict = k.sem("a_exp_ready"), k.sem("strict_r_ready")
        s_xhi, s_xlo = k.sem("x_hi_ready"), k.sem("x_lo_ready")
        s_p0, s_p1, s_p2 = k.sem("X_left_half_summed"), k.sem("X_right_half_summed"), k.sem("BC_summed")
        s_xc, s_bc = k.sem("X_half_copied"), k.sem("BC_copied")
        s_t2, s_bct, s_btok = k.sem("BC_transposed"), k.sem("BC_turned_copied"), k.sem("B_copied")
        s_p3 = k.sem("CB_and_dt_summed")
        s_na, s_u = k.sem("minus_abs_dt_ready"), k.sem("exp_dt_ready")
        s_dt, s_a, s_al = k.sem("dt_ready"), k.sem("a_ready"), k.sem("a_lo_ready")
        s_r, s_rp = k.sem("r_by_dve"), k.sem("r_by_pool")
        s_sum, s_ed, s_ek = k.sem("a_sums_ready"), k.sem("decays_ready"), k.sem("state_decay_ready")
        s_diff, s_dec = k.sem("exponents_summed"), k.sem("decay_matrix_ready")
        s_cbm, s_mix = k.sem("CB_masked"), k.sem("mix_ready")
        s_xs, s_xd, s_xdec = k.sem("X_dt_ready"), k.sem("X_D_ready"), k.sem("X_decayed_ready")
        s_yoff, s_ydiag, s_st = k.sem("y_from_state_summed"), k.sem("y_in_chunk_summed"), k.sem("state_summed")
        s_yx, s_y = k.sem("skip_added"), k.sem("y_ready")
        s_sd, s_sa = k.sem("state_decayed"), k.sem("state_half_added")
        s_yT, s_g, s_ghi, s_glo = k.sem("y_transposed"), k.sem("gated"), k.sem("g_hi_ready"), k.sem("g_lo_ready")
        s_op, s_rr, s_mv, s_eps, s_rstd = (k.sem(n) for n in ("out_proj_summed", "residual_added", "mv_ready",
                                                             "eps_added", "rstd_ready"))
        s_bn = k.sem("bn_stats_ready")
        s_x1, s_out = k.sem("x1_ready"), k.sem("x1_stored")
        c_dve = k.sem("dve_steps")
        block = k.block()

        def chunks(eng, step):
            step(0, True, False, False)
            step(1, False, True, False)
            with eng.Fori(2, NCH - 1) as g:
                step(g, False, False, False)
            step(NCH - 1, False, False, True)

        @block.sync
        def _(sp):
            for n in ("dtw", "dtb", "a_log", "d_skip"):
                dst = {"dtw": dtw, "dtb": dtb, "a_log": a_pos, "d_skip": d_skip}[n]
                sp.dma_start(dst[:], t[n]).then_inc(s_small, 16)
            sp.dma_start(x_raw[:], t["xb"][:, :, 0:P].rearrange("j p n -> p j n")).then_inc(s_lx, 16)
            for i in range(WG):
                if i >= 2:
                    sp.wait_ge(s_wlo, i - 1)
                if i < IT:
                    sp.dma_start(staging[i % 2][:, 0:XC], t["x_w"][:, i]).then_inc(s_w[i % 2], 16)
                else:
                    sp.dma_start(staging[i % 2][:, 0:2 * DM], t["out_w"][:, i - IT]).then_inc(s_w[i % 2], 16)

            def step(g, first, second, last):
                if not last:
                    sp.wait_ge(s_small, 64)
                    sp.wait_ge(s_xlo, g + 1)
                    sp.dma_start(x_raw[:], t["xb"][:, :, bass.ds(g * P + P, P)].rearrange("j p n -> p j n")).then_inc(s_lx, 16)
                if not first:
                    sp.wait_ge(s_small, 64)
                    sp.wait_ge(s_g, g)
                sp.dma_start(z_raw[:], t["zs"][:, :, bass.ds(g * P, P)].rearrange("j p n -> p j n")).then_inc(s_lz, 16)
                if not first:
                    sp.wait_ge(s_small, 64)
                    sp.wait_ge(s_rr, g)
                sp.dma_start(res[:], t["x_rows"][bass.ds(g * P, P), :]).then_inc(s_lr, 16)
                if not first:
                    sp.wait_ge(s_small, 64)
                    sp.wait_ge(s_x1, g)
                    sp.dma_start(t["x1"][bass.ds(g * P - P, P), :], rr[:]).then_inc(s_out, 16)
            chunks(sp, step)
            sp.wait_ge(s_x1, NCH)
            sp.dma_start(t["x1"][TOK - P:TOK, :], rr[:]).then_inc(s_out, 16)
            sp.wait_ge(s_out, 16 * NCH)

        @block.gpsimd
        def _(pool):
            nc.gpsimd.memset(ones[:], 1.0).then_inc(s_const, 1)
            nc.gpsimd.memset(state[:], 0.0).then_inc(s_const, 1)
            nc.gpsimd.memset(keep[:], 1.0).then_inc(s_const, 1)
            nc.gpsimd.memset(const[:, 0:1], EPS).then_inc(s_const, 1)
            nc.gpsimd.memset(const[:, 1:2], -0.5).then_inc(s_const, 1)
            pool.wait_ge(s_const, 3)
            nc.gpsimd.memset(keep[:, CPB - 1::CPB], 0.0).then_inc(s_const, 1)
            nc.gpsimd.affine_select(out=tri[:], in_=ones[:], compare_op=ALU.is_ge, fill=0.0, base=0,
                                    pattern=[[1, P]], channel_multiplier=-1).then_inc(s_tri, 1)
            nc.gpsimd.affine_select(out=cb_m[:], in_=ones[:], compare_op=ALU.is_ge, fill=0.0, base=-1,
                                    pattern=[[-1, P]], channel_multiplier=1).then_inc(s_tri, 1)
            make_identity(nc, pool, ident[:], s_ident)
            pool.wait_ge(s_const, 6)

            def step(g, first, second, last):
                pool.wait_ge(s_al, g + 1)
                if not first:
                    pool.wait_ge(s_diff, g)
                half = NH // 2
                nc.gpsimd.tensor_tensor(r_lo[:, 0:half], tri[:].unsqueeze(1).broadcast_to([P, half, P]),
                                        a_lo[:, 0:half].unsqueeze(2).broadcast_to([P, half, P]),
                                        ALU.mult).then_inc(s_rp, 1)
                if not first:
                    low_of_gated(g - 1)
                pool.wait_ge(s_xc, 2 * g + 2)
                if not first:
                    pool.wait_ge(s_y, g)
                nc.gpsimd.tensor_tensor(xd[:], xf[:], d_skip[:].unsqueeze(2).broadcast_to([P, NH, HD]),
                                        ALU.mult).then_inc(s_xd, 1)
                pool.wait_ge(s_xs, g + 1)
                pool.wait_ge(s_ed, g + 1)
                if not first:
                    pool.wait_ge(s_st, g)
                nc.gpsimd.tensor_tensor(xdec[:], xs[:], ed[:, 1].unsqueeze(2).broadcast_to([P, NH, HD]),
                                        ALU.mult).then_inc(s_xdec, 1)
                if not first:
                    inverse_deviation(nc, pool, mv[:], rstd[:], const[:], s_mv, s_eps, s_rstd, g)
                pool.wait_ge(s_yoff, g + 1)
                pool.wait_ge(s_ek, g + 1)
                if not first:
                    pool.wait_ge(s_sa, 2 * g)
                nc.gpsimd.tensor_tensor(state[:], state[:], ek[:].unsqueeze(2).broadcast_to([P, NH, HD]),
                                        ALU.mult).then_inc(s_sd, 1)

            def low_of_gated(g):
                pool.wait_ge(s_ghi, g + 1)
                nc.gpsimd.tensor_tensor(g_lo[:], g_f[:], raw(g_hi[:]), ALU.subtract).then_inc(s_glo, 1)

            pool.wait_ge(s_small, 64)
            chunks(pool, step)
            low_of_gated(NCH - 1)
            inverse_deviation(nc, pool, mv[:], rstd[:], const[:], s_mv, s_eps, s_rstd, NCH)

        @block.scalar
        def _(act):
            act.wait_ge(s_small, 64)
            nc.scalar.activation(a_pos[:], a_pos[:], ACT.Exp).then_inc(s_apos, 1)
            act.wait_ge(s_tri, 2)
            nc.scalar.activation(strict_r[:], cb_m[:], ACT.Copy).then_inc(s_strict, 1)

            def x_high(g, first=False):
                act.wait_ge(s_lx, 16 * (g + 1))
                if not first:
                    act.wait_ge(s_p2, g)
                nc.scalar.activation(x_hi[:], x_raw[:], ACT.Copy).then_inc(s_xhi, 1)

            def x_copies(g, first=False):
                for i, (bank, sem) in enumerate(((pa, s_p0), (pb, s_p1))):
                    act.wait_ge(sem, g + 1)
                    if i == 0 and not first:
                        act.wait_ge(s_xs, g)
                        act.wait_ge(s_xd, g)
                    nc.scalar.activation(xf[:, i * NH // 2:(i + 1) * NH // 2].rearrange("p h d -> p (h d)"),
                                         bank[:], ACT.Copy).then_inc(s_xc, 1)

            def bc_copy(g, first=False):
                act.wait_ge(s_p2, g + 1)
                if not first:
                    act.wait_ge(s_t2, g)
                    act.wait_ge(s_btok, g)
                nc.scalar.activation(bcd[:], pa[:, 0:BC], ACT.Copy).then_inc(s_bc, 1)

            x_high(0, True)
            for i in range(WG):
                act.wait_ge(s_w[i % 2], 16 * (i // 2 + 1))
                if i < IT:
                    nc.scalar.activation(wx_hi[:, i], staging[i % 2][:, 0:XC], ACT.Copy).then_inc(s_whi, 1)
                else:
                    o = 2 * (i - IT)
                    nc.scalar.activation(wo_hi[:, o:o + 2].rearrange("p k n -> p (k n)"),
                                         staging[i % 2][:, 0:2 * DM], ACT.Copy).then_inc(s_whi, 1)
            x_copies(0, True)
            bc_copy(0, True)

            def g_high(g, first):
                act.wait_ge(s_g, g + 1)
                if not first:
                    act.wait_ge(s_op, g)
                nc.scalar.activation(g_hi[:], g_f[:], ACT.Copy).then_inc(s_ghi, 1)

            def step(g, first, second, last):
                if not last:
                    x_high(g + 1)
                act.wait_ge(s_t2, g + 1)
                if not first:
                    act.wait_ge(s_st, g)
                nc.scalar.activation(bct[:], psm[:, 0:2 * NS], ACT.Copy).then_inc(s_bct, 1)
                nc.scalar.activation(dtT[:], psm[0:NH, 2 * NS:3 * NS], ACT.Copy).then_inc(s_bct, 1)
                act.wait_ge(s_bc, g + 1)
                nc.scalar.activation(b_tok[:], bcd[:, NH:NH + NS], ACT.Copy).then_inc(s_btok, 1)
                act.wait_ge(s_na, g + 1)
                nc.scalar.activation(u[:], na[:], ACT.Exp).then_inc(s_u, 1)
                if not first:
                    g_high(g - 1, second)
                if not last:
                    x_copies(g + 1)
                act.wait_ge(s_sum, g + 1)
                if not first:
                    act.wait_ge(s_sd, g)
                    act.wait_ge(s_y, g)
                    act.wait_ge(s_ek, g)
                nc.scalar.activation(ed[:].rearrange("p k h -> p (k h)"), SUM, ACT.Exp).then_inc(s_ed, 1)
                act.wait_ge(s_diff, g + 1)
                if not first:
                    act.wait_ge(s_mix, g)
                nc.scalar.activation(decay[:].rearrange("p h l -> p (h l)"),
                                     pd[:].rearrange("p q n -> p (q n)"), ACT.Exp).then_inc(s_dec, 1)
                if not last:
                    bc_copy(g + 1)
            chunks(act, step)
            g_high(NCH - 1, False)

        @block.tensor
        def _(pe):
            def x_proj(g, piece, first=False, second=False):
                bank, lo, n, sem = ((pa, 0, 512, s_p0), (pb, 512, 512, s_p1), (pa, 2 * 512, BC, s_p2))[piece]
                if piece == 0:
                    pe.wait_ge(s_xlo, g + 1)
                if piece == 2:
                    pe.wait_ge(s_xc, 2 * g + 1)
                elif not first:
                    pe.wait_ge(s_bc, g)
                    if not second:
                        pe.wait_ge(s_sa, 2 * (g - 2) + 1 + piece)
                for kt in range(IT):
                    if first:
                        pe.wait_ge(s_wlo, kt + 1)
                    ins = product(pe, bank[:, 0:n], (x_hi[:, kt], x_lo[:, kt]),
                                  (wx_hi[:, kt, lo:lo + n], wx_lo[:, kt, lo:lo + n]), kt == 0, kt == IT - 1)
                ins.then_inc(sem, 1)

            def turn_y(g):
                pe.wait_ge(s_y, g + 1)
                for j in range(IT):
                    ins = pe.transpose(pd[:, j // 4, bass.ts(j % 4, P)],
                                       y[:, 2 * j:2 * j + 2].rearrange("p h d -> p (h d)"), ident[:])
                ins.then_inc(s_yT, 1)

            def out_proj(g, first):
                pe.wait_ge(s_glo, g + 1)
                if not first:
                    pe.wait_ge(s_rr, g)
                for kt in range(IT):
                    ins = product(pe, po[:], (g_hi[:, kt], g_lo[:, kt]), (wo_hi[:, kt], wo_lo[:, kt]),
                                  kt == 0, kt == IT - 1)
                ins.then_inc(s_op, 1)

            def step(g, first, second, last):
                pe.wait_ge(s_bc, g + 1)
                if not first:
                    pe.wait_ge(s_ed, g)
                pe.transpose(psm[:, 0:NS], bcd[:, NH:NH + NS], ident[:])
                pe.transpose(psm[:, NS:2 * NS], bcd[:, NH + NS:BC], ident[:])
                pe.transpose(psm[0:NH, 2 * NS:3 * NS], bcd[:, 0:NH], ident[:]).then_inc(s_t2, 1)
                if not last:
                    x_proj(g + 1, 0, second=first)
                if not first:
                    turn_y(g - 1)
                pe.wait_ge(s_bct, 2 * g + 2)
                pe.matmul(CB, bct[:, 0:NS], bct[:, NS:2 * NS], start=True, stop=True)
                pe.matmul(DTP, dtT[:], dtw[:], start=True, stop=True).then_inc(s_p3, 1)
                if not last:
                    x_proj(g + 1, 1, second=first)
                pe.wait_ge(s_a, g + 1)
                pe.wait_ge(s_cbm, g + 1)
                for i, m in enumerate((tri[:], raw(strict_r[:]), ones[:])):
                    ins = pe.matmul(SUM[:, i * NH:(i + 1) * NH], m, a[:], start=True, stop=True)
                ins.then_inc(s_sum, 1)
                pe.wait_ge(s_r, g + 1)
                pe.wait_ge(s_rp, g + 1)
                if not first:
                    pe.wait_ge(s_g, g)
                for i in range(4):
                    heads = slice(4 * i, 4 * i + 4)
                    pe.matmul(pd[:, i], strict_r[:], r_hi[:, heads].rearrange("p h l -> p (h l)"),
                              start=True, stop=False)
                    ins = pe.matmul(pd[:, i], strict_r[:], r_lo[:, heads].rearrange("p h l -> p (h l)"),
                                    start=False, stop=True)
                ins.then_inc(s_diff, 1)
                if not last:
                    x_proj(g + 1, 2)
                if not first:
                    out_proj(g - 1, second)
                pe.wait_ge(s_dec, g + 1)
                if not first:
                    pe.wait_ge(s_sa, 2 * g)
                for i in range(2):
                    ins = pe.matmul(pd[:, i], bct[:, NS:2 * NS],
                                    state[:, i * NH // 2:(i + 1) * NH // 2].rearrange("p h d -> p (h d)"),
                                    start=True, stop=True)
                ins.then_inc(s_yoff, 1)
                pe.wait_ge(s_mix, g + 1)
                pe.wait_ge(s_xs, g + 1)
                for h in range(NH):
                    ins = pe.matmul(pd[:, 2 + h // 8, bass.ts(h % 8, HD)], mix[:, h], xs[:, h],
                                    start=True, stop=True)
                ins.then_inc(s_ydiag, 1)
                pe.wait_ge(s_xdec, g + 1)
                if not last:
                    pe.wait_ge(s_xc, 2 * g + 4)
                    pe.wait_ge(s_bc, g + 2)
                for i, bank in enumerate((pa, pb)):
                    ins = pe.matmul(bank[:], b_tok[:],
                                    xdec[:, i * NH // 2:(i + 1) * NH // 2].rearrange("p h d -> p (h d)"),
                                    start=True, stop=True)
                ins.then_inc(s_st, 1)

            pe.wait_ge(s_const, 6)
            pe.wait_ge(s_tri, 2)
            pe.wait_ge(s_ident, 2)
            pe.wait_ge(s_strict, 1)
            pe.wait_ge(s_small, 64)
            for piece in range(3):
                x_proj(0, piece, True)
            pe.wait_ge(s_wlo, WG)
            chunks(pe, step)
            turn_y(NCH - 1)
            out_proj(NCH - 1, False)

        @block.vector
        def _(dve):
            chain = Chain(dve, c_dve, 17)
            tt, stt, ts = nc.vector.tensor_tensor, nc.vector.scalar_tensor_tensor, nc.vector.tensor_scalar
            heads = lambda ap, n: ap.unsqueeze(2).broadcast_to([P, ap.shape[1], n])
            flat = lambda ap: ap.rearrange("p h d -> p (h d)")

            def x_low(g):
                dve.wait_ge(s_xhi, g + 1)
                tt(x_lo[:], x_raw[:], raw(x_hi[:]), ALU.subtract).then_inc(s_xlo, 1)

            x_low(0)
            for i in range(WG):
                dve.wait_ge(s_whi, i + 1)
                if i < IT:
                    tt(wx_lo[:, i], staging[i % 2][:, 0:XC], raw(wx_hi[:, i]), ALU.subtract).then_inc(s_wlo, 1)
                else:
                    o = 2 * (i - IT)
                    tt(flat(wo_lo[:, o:o + 2]), staging[i % 2][:, 0:2 * DM], raw(flat(wo_hi[:, o:o + 2])),
                       ALU.subtract).then_inc(s_wlo, 1)
            dve.wait_ge(s_wlo, WG)
            dve.wait_ge(s_small, 64)
            dve.wait_ge(s_apos, 1)
            dve.wait_ge(s_tri, 2)
            dve.wait_ge(s_const, 6)

            def gate(g, first):
                dve.wait_ge(s_yT, g + 1)
                dve.wait_ge(s_lz, 16 * (g + 1))
                if not first:
                    dve.wait_ge(s_glo, g)
                tt(g_f[:].rearrange("p k n -> p (k n)"), pd[:, 0:2].rearrange("p q n -> p (q n)"),
                   z_raw[:].rearrange("p k n -> p (k n)"), ALU.mult).then_inc(s_g, 1)

            def residual(g, first=False):
                if not first:
                    dve.wait_ge(s_out, 16 * g)
                dve.wait_ge(s_op, g + 1)
                dve.wait_ge(s_lr, 16 * (g + 1))
                tt(rr[:], po[:], res[:], ALU.add).then_inc(s_rr, 1)
                dve.wait_ge(s_rr, g + 1)
                layer_norm_stats(nc, dve, rr[:], stats[:], mv[:], s_bn, s_mv, g + 1, s_tri)

            def normalize(g):
                dve.wait_ge(s_rstd, g + 1)
                ts(rr[:], rr[:], mv[:, 0:1], rstd[:], ALU.subtract, ALU.mult).then_inc(s_x1, 1)
                dve.wait_ge(s_x1, g + 1)

            def step(g, first, second, last):
                chain.round(g)
                if not last:
                    x_low(g + 1)
                if not first:
                    gate(g - 1, second)
                dve.wait_ge(s_p3, g + 1)
                tt(cb_m[:], CB, tri[:], ALU.mult).then_inc(s_cbm, 1)
                chain.link(tt(v[:], DTP, dtb[:], ALU.add))
                chain.link(ts(na[:], v[:], -1.0, None, ALU.mult))
                tt(na[:], na[:], v[:], ALU.min).then_inc(s_na, 1)
                dve.wait_ge(s_u, g + 1)
                chain.link(ts(s1[:], u[:], 2.0, None, ALU.add))
                chain.link(nc.vector.reciprocal(s1[:], s1[:]))
                chain.link(tt(s1[:], u[:], s1[:], ALU.mult))
                chain.link(tt(q[:], s1[:], s1[:], ALU.mult))
                chain.link(ts(s2[:], q[:], 1.0 / 13, None, ALU.mult))
                for n in (11, 9, 7, 5, 3):
                    chain.link(stt(out=s2[:], in0=s2[:], scalar=1.0 / n, in1=q[:], op0=ALU.add, op1=ALU.mult))
                chain.link(stt(out=s2[:], in0=s2[:], scalar=1.0, in1=s1[:], op0=ALU.add, op1=ALU.mult))
                chain.link(ts(v[:], v[:], 0.0, None, ALU.max))
                stt(out=dt[:], in0=s2[:], scalar=2.0, in1=v[:], op0=ALU.mult, op1=ALU.add).then_inc(s_dt, 1)
                dve.wait_ge(s_dt, g + 1)
                stt(out=a[:], in0=dt[:], scalar=-1.0, in1=a_pos[:], op0=ALU.mult, op1=ALU.mult).then_inc(s_a, 1)
                dve.wait_ge(s_a, g + 1)
                chain.link(nc.vector.tensor_copy(a_hi[:], a[:]))
                tt(a_lo[:], a[:], raw(a_hi[:]), ALU.subtract).then_inc(s_al, 1)
                dve.wait_ge(s_al, g + 1)
                half = NH // 2
                tt(r_lo[:, half:NH], tri[:].unsqueeze(1).broadcast_to([P, half, P]), heads(a_lo[:, half:NH], P),
                   ALU.mult)
                tt(r_hi[:], tri[:].unsqueeze(1).broadcast_to([P, NH, P]), heads(raw(a_hi[:]), P),
                   ALU.mult).then_inc(s_r, 1)
                dve.wait_ge(s_xc, 2 * g + 2)
                tt(xs[:], xf[:], heads(dt[:], HD), ALU.mult).then_inc(s_xs, 1)
                dve.wait_ge(s_ed, g + 1)
                ts(ek[:], ed[:, 2], keep[:, bass.ds(g, 1)], None, ALU.mult).then_inc(s_ek, 1)
                dve.wait_ge(s_dec, g + 1)
                tt(mix[:], decay[:], cb_m[:].unsqueeze(1).broadcast_to([P, NH, P]), ALU.mult).then_inc(s_mix, 1)
                if not first:
                    residual(g - 1, second)
                dve.wait_ge(s_yoff, g + 1)
                chain.link(tt(y[:], pd[:, 0:2].rearrange("p q (h d) -> p (q h) d", d=HD), heads(ed[:, 0], HD), ALU.mult))
                if not first:
                    normalize(g - 1)
                dve.wait_ge(s_xd, g + 1)
                tt(flat(y[:]), flat(y[:]), flat(xd[:]), ALU.add).then_inc(s_yx, 1)
                dve.wait_ge(s_yx, g + 1)
                dve.wait_ge(s_ydiag, g + 1)
                tt(flat(y[:]), flat(y[:]), pd[:, 2:4].rearrange("p q n -> p (q n)"), ALU.add).then_inc(s_y, 1)
                dve.wait_ge(s_st, g + 1)
                dve.wait_ge(s_sd, g + 1)
                for i, bank in enumerate((pa, pb)):
                    part = flat(state[:, i * half:(i + 1) * half])
                    stt(out=part, in0=bank[:], scalar=keep[:, bass.ds(g, 1)], in1=part,
                        op0=ALU.mult, op1=ALU.add).then_inc(s_sa, 1)
                dve.wait_ge(s_sa, 2 * g + 2)
                chain.close()
            chunks(dve, step)
            chain.round(NCH)
            gate(NCH - 1, False)
            residual(NCH - 1)
            normalize(NCH - 1)


def inverse_deviations(nc, pool, mv, rstd, minus_half, s_eps, s_rstd, n):
    nc.gpsimd.tensor_scalar(rstd, mv[:, :, 1], EPS, None, ALU.add).then_inc(s_eps, 1)
    pool.wait_ge(s_eps, n)
    nc.gpsimd.tensor_tensor(rstd, rstd, minus_half, ALU.pow).then_inc(s_rstd, 1)


def ffn_phase(nc, t, acc, gated):
    with ExitStack() as ctx:
        k = Kit(nc, ctx, "moe" if gated else "ffn")
        TAG = "e_" if gated else "f_"
        UNITS = 8 if gated else 4
        NE = 8 if gated else 16
        NU = 2 if gated else 1
        F = 4
        RING = 4 // NU
        R = 64
        LORA = 2
        GOLD_C, GOLD_LO, GOLD_HI = 0.36787944117144233, 0.5 - 0.28768207245178085, 0.5

        xc_hi, xc_lo = (k.sb(n, [P, KT, TOK], F32R) for n in ("xc_hi", "xc_lo"))
        up_raw = k.sb("up_raw", [P, NU, F, KT, P])
        dn_raw = k.sb("dn_raw", [P, F, DM])
        up_hi, up_lo = (k.sb(n, [P, NU, F, KT, P], F32R) for n in ("up_hi", "up_lo"))
        dn_hi, dn_lo = (k.sb(n, [P, F, DM], F32R) for n in ("dn_hi", "dn_lo"))
        h_f = k.sb("h_f", [P, 2, SEQ])
        act_f = k.sb("act_f", [P, 2, SEQ]) if gated else None
        h_hi, h_lo = (k.sb(n, [P, F, SEQ], F32R) for n in ("h_hi", "h_lo"))
        wts = k.sb("wts", [P, NCH, NE])
        rw_raw = k.sb("rw_raw", [P, KT, NE])
        rw_hi, rw_lo = (k.sb(n, [P, KT, NE], F32R) for n in ("rw_hi", "rw_lo"))
        rb = k.sb("rb", [P, NE if not gated else 1])
        lower = k.sb("lower", [P, NE, NE])
        GRP = CPB
        lg, pr, sel = (k.sb(n, [P, GRP, NE]) for n in ("lg", "pr", "sel"))
        sum1, sum2 = k.sb("sum1", [P, GRP]), k.sb("sum2", [P, GRP])
        cmp1, cmp2 = (k.sb(n, [P, GRP, NE, NE]) for n in ("cmp1", "cmp2"))
        ident = k.sb("ident", [P, P])
        minus_half = k.sb("minus_half", [P, CPB])
        stats, mv, rstd = k.sb("stats", [P, CPB, 6]), k.sb("mv", [P, CPB, 2]), k.sb("rstd", [P, CPB])
        if gated:
            la_up, lb_up = k.sb("la_up", [2 * R, DM]), k.sb("lb_up", [2 * R, DM])
            la_dn, lb_dn = k.sb("la_dn", [R, DM]), k.sb("lb_dn", [R, DM])
        pu, pd = k.ps("pu", [P, 4, 512]), k.ps("pd", [P, 4, 512])
        LG = pu[:, 0, 0:NCH * NE]

        s_x = [k.sem(f"x_loaded{b}") for b in range(NB)]
        s_small = k.sem("small_loaded")
        s_lora = k.sem("lora_loaded")
        s_lu, s_ld = k.sem("up_loaded"), k.sem("down_loaded")
        s_ident, s_mem = k.sem("ident_ready"), k.sem("constants_ready")
        s_xT, s_xhi, s_xlo = k.sem("x_transposed"), k.sem("x_hi_ready"), k.sem("x_lo_ready")
        s_rwhi, s_rwlo = k.sem("router_hi_ready"), k.sem("router_lo_ready")
        s_lg, s_lgc = k.sem("logits_summed"), k.sem("logits_copied")
        s_z, s_e = k.sem("router_to_act"), k.sem("router_from_act")
        s_uhi, s_ulo = k.sem("up_hi_ready"), k.sem("up_lo_ready")
        s_dhi, s_dlo = k.sem("down_hi_ready"), k.sem("down_lo_ready")
        s_delta, s_merged = k.sem("lora_delta_summed"), k.sem("lora_merged")
        s_up = k.sem("hidden_summed")
        s_act, s_hf = k.sem("silu_ready"), k.sem("hidden_ready")
        s_hhi, s_hlo = k.sem("hidden_hi_ready"), k.sem("hidden_lo_ready")
        s_dn, s_acc = k.sem("down_summed"), k.sem("down_added")
        s_bn, s_mv, s_eps, s_rstd = (k.sem(n) for n in ("bn_stats_ready", "mv_ready", "eps_added", "rstd_ready"))
        s_norm, s_out = k.sem("normalized"), k.sem("stored")
        c_dve = k.sem("dve_router_steps")
        block = k.block()

        @block.sync
        def _(sp):
            if not gated:
                for b in range(NB):
                    sp.dma_start(acc[:, b * CPB:(b + 1) * CPB],
                                 t["x1"][b * SEQ:(b + 1) * SEQ, :].rearrange("(c p) d -> p c d", p=P)).then_inc(s_x[b], 16)
            sp.dma_start(rw_raw[:], t[TAG + "router"]).then_inc(s_small, 16)
            sp.dma_start(rb[:], t[TAG + "rb"]).then_inc(s_small, 16)

            def lora(e):
                if e:
                    sp.wait_ge(s_delta, 12 * e)
                for dst, n in ((la_up, "la_up"), (lb_up, "lb_up"), (la_dn, "la_dn"), (lb_dn, "lb_dn")):
                    sp.dma_start(dst[:], t[n][e]).then_inc(s_lora, 16)

            if gated:
                lora(0)
            sp.dma_start(up_raw[:], t[TAG + "up"][0]).then_inc(s_lu, 16)
            sp.dma_start(dn_raw[:], t[TAG + "dn"][0]).then_inc(s_ld, 16)
            if gated:
                lora(1)

            def unit(u):
                sp.wait_ge(s_small, 32)
                sp.wait_ge(s_ulo, NU * F * u + NU * F)
                sp.dma_start(up_raw[:], t[TAG + "up"][bass.ds(u + 1, 1)].rearrange("o p n f k c -> (o p) n f k c")).then_inc(s_lu, 16)
                sp.wait_ge(s_small, 32)
                sp.wait_ge(s_dlo, F * u + F)
                sp.dma_start(dn_raw[:], t[TAG + "dn"][bass.ds(u + 1, 1)].rearrange("o p f d -> (o p) f d")).then_inc(s_ld, 16)
            with sp.Fori(0, UNITS - 1) as u:
                unit(u)
            if gated:
                for b in range(NB):
                    sp.wait_ge(s_norm, CPB * b + CPB)
                    sp.dma_start(t["out"][b].rearrange("(c p) d -> p c d", p=P),
                                 acc[:, b * CPB:(b + 1) * CPB]).then_inc(s_out, 16)
                sp.wait_ge(s_out, 16 * NB)

        @block.gpsimd
        def _(pool):
            make_identity(nc, pool, ident[:], s_ident)
            nc.gpsimd.memset(minus_half[:], -0.5).then_inc(s_mem, 1)
            nc.gpsimd.memset(lower[:], 1.0).then_inc(s_mem, 1)
            pool.wait_ge(s_mem, 2)
            nc.gpsimd.affine_select(out=lower[:], in_=lower[:], compare_op=ALU.is_ge, fill=0.0, base=-1,
                                    pattern=[[1, NE], [-1, NE]], channel_multiplier=0).then_inc(s_mem, 1)

            def unit(u, first, last):
                for tt in range(NB):
                    for f in range(F):
                        m = F * NB * u + F * tt + f
                        pool.wait_ge(s_hhi, m + 1)
                        nc.gpsimd.tensor_tensor(h_lo[:, f], h_f[:, f % 2], raw(h_hi[:, f]),
                                                ALU.subtract).then_inc(s_hlo, 1)
                    if last and tt:
                        deviations(tt)

            def deviations(n):
                pool.wait_ge(s_mv, CPB * n)
                inverse_deviations(nc, pool, mv[:], rstd[:], minus_half[:], s_eps, s_rstd, n)

            unit(0, True, False)
            with pool.Fori(1, UNITS - 1) as u:
                unit(u, False, False)
            unit(UNITS - 1, False, True)
            deviations(NB)

        @block.scalar
        def _(act):
            act.wait_ge(s_small, 32)
            nc.scalar.activation(rw_hi[:], rw_raw[:], ACT.Copy).then_inc(s_rwhi, 1)
            for b in range(NB):
                for kt in range(KT):
                    act.wait_ge(s_xT, b * KT + kt + 1)
                    nc.scalar.activation(xc_hi[:, kt, bass.ts(b, SEQ)], pd[:, kt], ACT.Copy).then_inc(s_xhi, 1)

            def up_high(u, f, first=False):
                act.wait_ge(s_lu, 16 * u + 16)
                if first and gated:
                    act.wait_ge(s_merged, 8)
                for i in range(NU):
                    nc.scalar.activation(up_hi[:, i, f], up_raw[:, i, f], ACT.Copy).then_inc(s_uhi, 1)

            for f in range(F):
                up_high(0, f, True)

            def unit(u, first, last):
                for tt in range(NB):
                    for f in range(F):
                        m = F * NB * u + F * tt + f
                        act.wait_ge(s_up, m + 1)
                        if gated:
                            if not (first and m < 2):
                                act.wait_ge(s_hf, m - 1)
                            nc.scalar.activation(act_f[:, f % 2], pu[:, (f % RING) * NU], ACT.Silu).then_inc(s_act, 1)
                        else:
                            if not (first and m < 2):
                                act.wait_ge(s_hlo, m - 1)
                            nc.scalar.activation(h_f[:, f % 2], pu[:, f], ACT.Gelu).then_inc(s_hf, 1)
                        if tt == NB - 1 and not last:
                            if first and gated:
                                act.wait_ge(s_merged, 12 + 8)
                            up_high(u + 1, f)
                        act.wait_ge(s_hf, m + 1)
                        if not (first and tt == 0):
                            act.wait_ge(s_dn, F * (m - F) + F)
                        nc.scalar.activation(h_hi[:, f], h_f[:, f % 2], ACT.Copy).then_inc(s_hhi, 1)
                        if tt == 0:
                            act.wait_ge(s_ld, 16 * u + 16)
                            if first and gated:
                                act.wait_ge(s_merged, 12)
                            nc.scalar.activation(dn_hi[:, f], dn_raw[:, f], ACT.Copy).then_inc(s_dhi, 1)
                    if first and tt * GRP < NCH:
                        router_functions(tt)

            def router_functions(n):
                if not gated:
                    act.wait_ge(s_z, n + 1)
                    nc.scalar.activation(pr[:], lg[:], ACT.Exp).then_inc(s_e, 1)
                else:
                    act.wait_ge(s_z, 2 * n + 1)
                    nc.scalar.activation(pr[:], lg[:], ACT.Sigmoid).then_inc(s_e, 1)
                    act.wait_ge(s_z, 2 * n + 2)
                    nc.scalar.activation(sel[:], lg[:], ACT.Exp, scale=-1 / 0.1).then_inc(s_e, 1)
                    nc.scalar.activation(pr[:], lg[:], ACT.Exp, scale=-1 / 0.3).then_inc(s_e, 1)

            unit(0, True, False)
            with act.Fori(1, UNITS - 1) as u:
                unit(u, False, False)
            unit(UNITS - 1, False, True)

        @block.tensor
        def _(pe):
            pe.wait_ge(s_ident, 2)
            for b in range(NB):
                if not gated:
                    pe.wait_ge(s_x[b], 16)
                for kt in range(KT):
                    if b:
                        pe.wait_ge(s_xlo, b * KT + kt - KT + 1)
                    for c in range(CPB):
                        ins = pe.transpose(pd[:, kt, bass.ts(c, P)], acc[:, b * CPB + c, bass.ts(kt, P)], ident[:])
                    ins.then_inc(s_xT, 1)
            pe.wait_ge(s_rwlo, 1)
            pe.wait_ge(s_xlo, NB * KT)
            for g in range(NCH):
                for kt in range(KT):
                    tok = bass.ts(g, P)
                    ins = product(pe, LG[:, g * NE:(g + 1) * NE], (xc_hi[:, kt, tok], xc_lo[:, kt, tok]),
                                  (rw_hi[:, kt], rw_lo[:, kt]), kt == 0, kt == KT - 1)
            ins.then_inc(s_lg, 1)

            def merge(e):
                pe.wait_ge(s_lora, 64 * e + 64)
                for i in range(12):
                    if i >= 4:
                        pe.wait_ge(s_merged, 12 * e + i - 3)
                    if i < 8:
                        rows = slice(R * (i // 4), R * (i // 4) + R)
                        a, b = la_up[rows, bass.ts(i % 4, P)], lb_up[rows, :]
                    else:
                        a, b = la_dn[:, bass.ts(i - 8, P)], lb_dn[:]
                    pe.matmul(pd[:, i % 4], a, b, start=True, stop=True).then_inc(s_delta, 1)
                pe.wait_ge(s_merged, 12 * e + 12)

            if gated:
                merge(0)
            pe.wait_ge(s_lgc, 1)

            def down(m, f, tt, u, start):
                pe.wait_ge(s_hlo, m + 1)
                pe.wait_ge(s_dlo, F * u + f + 1)
                for c in range(CPB):
                    if not start:
                        pe.wait_ge(s_acc, CPB * (m - 1) + c + 1)
                    ins = product(pe, pd[:, c], (h_hi[:, f, bass.ts(c, P)], h_lo[:, f, bass.ts(c, P)]),
                                  (dn_hi[:, f], dn_lo[:, f]))
                    ins.then_inc(s_dn, 1)

            def unit(u, first, last):
                for tt in range(NB):
                    if first and gated and tt == 2:
                        pe.wait_ge(s_acc, CPB * F)
                        merge(1)
                    for f in range(F):
                        m = F * NB * u + F * tt + f
                        if tt == 0:
                            pe.wait_ge(s_ulo, NU * F * u + NU * f + NU)
                        if not (first and m < RING):
                            pe.wait_ge(s_hf, m - RING + 1)
                        for i in range(NU):
                            for kt in range(KT):
                                x = bass.ts(tt, SEQ)
                                ins = product(pe, pu[:, (f % RING) * NU + i], (up_hi[:, i, f, kt], up_lo[:, i, f, kt]),
                                              (xc_hi[:, kt, x], xc_lo[:, kt, x]), kt == 0, kt == KT - 1)
                        ins.then_inc(s_up, 1)
                        if not (first and tt == 0):
                            down(m - F, f, (tt - 1) % NB, u - 1 if tt == 0 else u, first and m == F)

            unit(0, True, False)
            with pe.Fori(1, UNITS - 1) as u:
                unit(u, False, False)
            unit(UNITS - 1, False, True)
            for f in range(F):
                down(F * NB * UNITS - F + f, f, NB - 1, UNITS - 1, False)

        @block.vector
        def _(dve):
            chain = Chain(dve, c_dve, 0)
            link = chain.link
            tt_, stt, ts = nc.vector.tensor_tensor, nc.vector.scalar_tensor_tensor, nc.vector.tensor_scalar
            red = nc.vector.tensor_reduce
            over = lambda ap, n: ap.unsqueeze(2).broadcast_to([P, ap.shape[1], n])

            for b in range(NB):
                for kt in range(KT):
                    dve.wait_ge(s_xhi, b * KT + kt + 1)
                    x = bass.ts(b, SEQ)
                    tt_(xc_lo[:, kt, x], pd[:, kt], raw(xc_hi[:, kt, x]), ALU.subtract).then_inc(s_xlo, 1)
                if b == 0:
                    dve.wait_ge(s_rwhi, 1)
                    tt_(rw_lo[:], rw_raw[:], raw(rw_hi[:]), ALU.subtract).then_inc(s_rwlo, 1)

            def merge(e):
                for i in range(12):
                    dve.wait_ge(s_delta, 12 * e + i + 1)
                    if i < 8:
                        dve.wait_ge(s_lu, 16 * e + 16)
                        w = up_raw[:, i // 4, :, i % 4]
                    else:
                        dve.wait_ge(s_ld, 16 * e + 16)
                        w = dn_raw[:, i - 8]
                    d = pd[:, i % 4].rearrange("p (f c) -> p f c", c=P) if i < 8 else pd[:, i % 4]
                    tt_(w, d, w, ALU.add).then_inc(s_merged, 1)

            def up_low(u, f):
                for i in range(NU):
                    dve.wait_ge(s_uhi, NU * F * u + NU * f + i + 1)
                    tt_(up_lo[:, i, f], up_raw[:, i, f], raw(up_hi[:, i, f]), ALU.subtract).then_inc(s_ulo, 1)

            if gated:
                merge(0)
            dve.wait_ge(s_lg, 1)
            link(nc.vector.tensor_copy(wts[:].rearrange("p c e -> p (c e)"), LG))
            dve.sem_inc(s_lgc, 1)
            for f in range(F):
                up_low(0, f)

            def ranks(p):
                pj = p.unsqueeze(2).broadcast_to([P, GRP, NE, NE])
                pi = p.unsqueeze(3).broadcast_to([P, GRP, NE, NE])
                link(tt_(cmp1[:], pj, pi, ALU.is_gt))
                link(tt_(cmp2[:], pj, pi, ALU.is_equal))
                link(tt_(cmp2[:], cmp2[:], lower[:].unsqueeze(1).broadcast_to([P, GRP, NE, NE]), ALU.mult))
                link(tt_(cmp1[:], cmp1[:], cmp2[:], ALU.add))

            def router_blocks(n):
                w = wts[:, n * GRP:(n + 1) * GRP]
                link(tt_(w, w, rb[:].unsqueeze(1).broadcast_to([P, GRP, NE]), ALU.add))
                link(red(sum1[:], w, AX_X, ALU.max))
                tt_(lg[:], w, over(sum1[:], NE), ALU.subtract).then_inc(s_z, 1)
                dve.wait_ge(s_e, n + 1)
                link(red(sum1[:], pr[:], AX_X, ALU.add))
                link(nc.vector.reciprocal(sum1[:], sum1[:]))
                link(tt_(pr[:], pr[:], over(sum1[:], NE), ALU.mult))
                ranks(pr[:])
                link(red(sel[:], cmp1[:], AX_X, ALU.add))
                link(ts(w, sel[:], 3.5, None, ALU.is_lt))

            def router_golden(n):
                weights = wts[:, n * GRP:(n + 1) * GRP]
                if n == 0:
                    link(nc.vector.reciprocal(rb[:], rb[:]))
                ts(lg[:], weights, rb[:], None, ALU.mult).then_inc(s_z, 1)
                dve.wait_ge(s_e, 3 * n + 1)
                link(ts(weights, pr[:], GOLD_LO, None, ALU.is_ge))
                link(ts(cmp1[:, :, 0], pr[:], GOLD_HI, None, ALU.is_le))
                link(tt_(weights, weights, cmp1[:, :, 0], ALU.mult))
                link(ts(lg[:], pr[:], GOLD_C, None, ALU.subtract))
                link(ts(cmp1[:, :, 0], lg[:], -1.0, None, ALU.mult))
                tt_(lg[:], lg[:], cmp1[:, :, 0], ALU.max).then_inc(s_z, 1)
                dve.wait_ge(s_e, 3 * n + 2)
                link(tt_(weights, weights, sel[:], ALU.mult))
                dve.wait_ge(s_e, 3 * n + 3)
                ranks(pr[:])
                link(red(sel[:], cmp1[:], AX_X, ALU.add))
                link(ts(sel[:], sel[:], 1.5, None, ALU.is_lt))
                link(tt_(sel[:], sel[:], pr[:], ALU.mult))
                for w in (sel[:], weights):
                    link(red(sum1[:], w, AX_X, ALU.add))
                    if w is weights:
                        link(ts(sum2[:], sum1[:], 1e-8, None, ALU.is_lt))
                        link(tt_(sel[:], sel[:], over(sum2[:], NE), ALU.mult))
                        link(ts(sum2[:], sum2[:], -1.0, 1.0, ALU.mult, ALU.add))
                        link(tt_(weights, weights, over(sum2[:], NE), ALU.mult))
                        link(tt_(weights, weights, sel[:], ALU.add))
                        link(red(sum1[:], weights, AX_X, ALU.add))
                    link(ts(sum1[:], sum1[:], 1e-8, None, ALU.max))
                    link(nc.vector.reciprocal(sum1[:], sum1[:]))
                    link(tt_(w, w, over(sum1[:], NE), ALU.mult))

            def add_down(m, f, tt, u):
                for c in range(CPB):
                    n = CPB * m + c
                    ch = tt * CPB + c
                    w = wts[:, ch, bass.ds(u, 1)] if gated else wts[:, ch, bass.ds(F * u + f, 1)]
                    dve.wait_ge(s_dn, n + 1)
                    if not (isinstance(m, int) and m == 0):
                        dve.wait_ge(s_acc, n - CPB + 1)
                    stt(out=acc[:, ch], in0=pd[:, c], scalar=w, in1=acc[:, ch],
                        op0=ALU.mult, op1=ALU.add).then_inc(s_acc, 1)

            def finish(n):
                dve.wait_ge(s_acc, CPB * (F * NB * (UNITS - 1) + F * n + F))
                if n:
                    dve.wait_ge(s_norm, CPB * n)
                for c in range(CPB):
                    nc.vector.bn_stats(stats[:, c], acc[:, n * CPB + c]).then_inc(s_bn, 1)
                for c in range(CPB):
                    dve.wait_ge(s_bn, CPB * n + c + 1)
                    nc.vector.bn_aggr(mv[:, c], stats[:, c]).then_inc(s_mv, 1)
                dve.wait_ge(s_rstd, n + 1)
                for c in range(CPB):
                    ch = n * CPB + c
                    ts(acc[:, ch], acc[:, ch], mv[:, c, 0:1], rstd[:, c:c + 1], ALU.subtract,
                       ALU.mult).then_inc(s_norm, 1)

            def unit(u, first, last):
                for tt in range(NB):
                    if first and gated and tt == 2:
                        merge(1)
                    for f in range(F):
                        m = F * NB * u + F * tt + f
                        if gated:
                            dve.wait_ge(s_act, m + 1)
                            if not (first and m < 2):
                                dve.wait_ge(s_hlo, m - 1)
                            tt_(h_f[:, f % 2], pu[:, (f % RING) * NU + 1], act_f[:, f % 2], ALU.mult).then_inc(s_hf, 1)
                        if tt == NB - 1 and not last:
                            up_low(u + 1, f)
                        if not (first and tt == 0):
                            add_down(m - F, f, (tt - 1) % NB, u - 1 if tt == 0 else u)
                        if tt == 0:
                            dve.wait_ge(s_dhi, F * u + f + 1)
                            tt_(dn_lo[:, f], dn_raw[:, f], raw(dn_hi[:, f]), ALU.subtract).then_inc(s_dlo, 1)
                    if first and tt * GRP < NCH:
                        if gated:
                            router_golden(tt)
                        else:
                            router_blocks(tt)
                    if last and tt:
                        finish(tt - 1)

            dve.wait_ge(s_small, 32)
            dve.wait_ge(s_mem, 3)
            unit(0, True, False)
            with dve.Fori(1, UNITS - 1) as u:
                unit(u, False, False)
            unit(UNITS - 1, False, True)
            for f in range(F):
                add_down(F * NB * UNITS - F + f, f, NB - 1, UNITS - 1)
            finish(NB - 1)
            dve.wait_ge(s_norm, NCH)


def attn_phase(nc, t, acc):
    with ExitStack() as ctx:
        k = Kit(nc, ctx, "attn")
        AH, AD = 16, 32
        G = DM // P
        HG = AH // G
        VW, OW = P + 1, P + HG
        AEPS = 1e-15
        w_raw = k.sb("w_raw", [P, 2, 4 * DM])
        wq_hi, wq_lo = (k.sb(n, [P, KT, 3 * DM], F32R) for n in ("wq_hi", "wq_lo"))
        wp_hi, wp_lo = (k.sb(n, [P, KT, DM], F32R) for n in ("wp_hi", "wp_lo"))
        bias = k.sb("bias", [P, DM])
        xt = k.sb("xt", [P, DM])
        x_hi, x_lo = (k.sb(n, [P, KT, P], F32R) for n in ("x_hi", "x_lo"))
        q, kk = k.sb("q", [P, DM]), k.sb("k", [P, DM])
        vo = k.sb("vo", [P, G, VW])
        qT = k.sb("qT", [P, CPB, G, P])
        bd = k.sb("bd", [P, G, OW])
        same = k.sb("same", [P, HG, AD])
        den = k.sb("den", [P, G, HG])
        o = k.sb("o", [P, G, HG, AD])
        o_hi, o_lo = (k.sb(n, [P, KT, P], F32R) for n in ("o_hi", "o_lo"))
        rr = k.sb("rr", [P, DM])
        ident = k.sb("ident", [P, P])
        stats, mv = k.sb("stats", [P, 6]), k.sb("mv", [P, 2])
        rstd, const = k.sb("rstd", [P, 1]), k.sb("const", [P, 2])
        pt, pq, pk, pv = (k.ps(n, [P, 512]) for n in ("pt", "pq", "pk", "pv"))
        pvk, po = k.ps("pvk", [P, 2, 512]), k.ps("po", [P, 2, 512])

        s_small = k.sem("bias_loaded")
        s_w = [k.sem(f"w_loaded{i}") for i in range(2)]
        s_whi, s_wlo = k.sem("w_hi_ready"), k.sem("w_lo_ready")
        s_ident, s_mem = k.sem("ident_ready"), k.sem("constants_ready")
        s_xt, s_xT, s_xhi, s_xlo = (k.sem(n) for n in ("x_copied", "x_transposed", "x_hi_ready", "x_lo_ready"))
        s_q, s_k, s_v = k.sem("q_summed"), k.sem("k_summed"), k.sem("v_summed")
        s_qr, s_kr, s_vr = k.sem("q_ready"), k.sem("k_ready"), k.sem("v_ready")
        s_qT, s_qTc = k.sem("q_transposed"), k.sem("q_turned_ready")
        s_vk, s_bd = k.sem("vk_summed"), k.sem("vk_ready")
        s_o, s_od = k.sem("out_summed"), k.sem("out_ready")
        s_oT, s_ohi, s_olo = k.sem("out_transposed"), k.sem("out_hi_ready"), k.sem("out_lo_ready")
        s_p, s_pa, s_rr = k.sem("projected"), k.sem("projection_taken"), k.sem("residual_added")
        s_bn, s_mv, s_eps, s_rstd, s_norm = (k.sem(n) for n in ("bn_stats_ready", "mv_ready", "eps_added",
                                                               "rstd_ready", "normalized"))
        c_dve = k.sem("dve_steps")
        block = k.block()
        WG = KT + 1

        def batches(eng, batch):
            batch(0, True)
            with eng.Fori(1, NB) as b:
                batch(b, False)

        @block.sync
        def _(sp):
            sp.dma_start(bias[:], t["proj_b"]).then_inc(s_small, 16)
            for i in range(WG):
                if i >= 2:
                    sp.wait_ge(s_wlo, i - 1)
                if i < KT:
                    sp.dma_start(w_raw[:, i % 2, 0:3 * DM], t["qkv_w"][i]).then_inc(s_w[i % 2], 16)
                else:
                    sp.dma_start(w_raw[:, i % 2], t["proj_w"].rearrange("p k n -> p (k n)")).then_inc(s_w[i % 2], 16)

        @block.gpsimd
        def _(pool):
            make_identity(nc, pool, ident[:], s_ident)
            nc.gpsimd.memset(const[:, 0:1], EPS).then_inc(s_mem, 1)
            nc.gpsimd.memset(const[:, 1:2], -0.5).then_inc(s_mem, 1)
            nc.gpsimd.memset(vo[:], 1.0).then_inc(s_mem, 1)
            nc.gpsimd.memset(same[:], 1.0).then_inc(s_mem, 1)
            pool.wait_ge(s_mem, 4)
            nc.gpsimd.affine_select(out=same[:], in_=same[:], compare_op=ALU.is_ge, fill=0.0, base=0,
                                    pattern=[[-AD, HG], [0, AD]], channel_multiplier=1).then_inc(s_mem, 1)
            pool.wait_ge(s_mem, 5)
            nc.gpsimd.affine_select(out=same[:], in_=same[:], compare_op=ALU.is_ge, fill=0.0, base=AD - 1,
                                    pattern=[[AD, HG], [0, AD]], channel_multiplier=-1).then_inc(s_mem, 1)

            def batch(b, first):
                for c in range(CPB):
                    inverse_deviation(nc, pool, mv[:], rstd[:], const[:], s_mv, s_eps, s_rstd, CPB * b + c + 1)
            batches(pool, batch)

        @block.scalar
        def _(act):
            def take_x(n, first):
                if not first:
                    act.wait_ge(s_xT, n)
                nc.scalar.activation(xt[:].unsqueeze(1), acc[:, bass.ds(n, 1)], ACT.Copy).then_inc(s_xt, 1)

            def batch(b, first):
                take_x(CPB * b, first)
                for c in range(CPB):
                    n = CPB * b + c
                    act.wait_ge(s_xT, n + 1)
                    if not (first and c == 0):
                        act.wait_ge(s_v, n)
                    nc.scalar.activation(x_hi[:].rearrange("p k n -> p (k n)"), pt[:], ACT.Copy).then_inc(s_xhi, 1)
                    if c < CPB - 1:
                        take_x(n + 1, False)
                    if first and c == 0:
                        weights()
                    act.wait_ge(s_q, n + 1)
                    if not (first and c == 0):
                        act.wait_ge(s_qT, n)
                    nc.scalar.activation(q[:], pq[:], ACT.Relu).then_inc(s_qr, 1)
                    act.wait_ge(s_k, n + 1)
                    if not (first and c == 0):
                        act.wait_ge(s_vk, n)
                    nc.scalar.activation(kk[:], pk[:], ACT.Relu).then_inc(s_kr, 1)
                    act.wait_ge(s_qT, n + 1)
                    if not first:
                        act.wait_ge(s_o, n - c)
                    nc.scalar.activation(qT[:, c].rearrange("p g n -> p (g n)"), po[:, 0], ACT.Copy).then_inc(s_qTc, 1)
                for c in range(CPB):
                    n = CPB * b + c
                    act.wait_ge(s_oT, n + 1)
                    if not (first and c == 0):
                        act.wait_ge(s_p, n)
                    nc.scalar.activation(o_hi[:].rearrange("p k n -> p (k n)"), pt[:], ACT.Copy).then_inc(s_ohi, 1)

            def weights():
                for i in range(WG):
                    act.wait_ge(s_w[i % 2], 16 * (i // 2 + 1))
                    if i < KT:
                        nc.scalar.activation(wq_hi[:, i], w_raw[:, i % 2, 0:3 * DM], ACT.Copy).then_inc(s_whi, 1)
                    else:
                        nc.scalar.activation(wp_hi[:].rearrange("p k n -> p (k n)"), w_raw[:, i % 2],
                                             ACT.Copy).then_inc(s_whi, 1)
            batches(act, batch)

        @block.tensor
        def _(pe):
            pe.wait_ge(s_ident, 2)
            pe.wait_ge(s_mem, 6)

            def turn_x(n, first):
                pe.wait_ge(s_xt, n + 1)
                if not first:
                    pe.wait_ge(s_xlo, n)
                for kt in range(KT):
                    ins = pe.transpose(pt[:, bass.ts(kt, P)], xt[:, bass.ts(kt, P)], ident[:])
                ins.then_inc(s_xT, 1)

            def sums(n):
                c = n[1]
                n = n[0]
                pe.wait_ge(s_qr, n + 1)
                if c:
                    pe.wait_ge(s_qTc, n)
                for g in range(G):
                    ins = pe.transpose(po[:, 0, bass.ts(g, P)], q[:, bass.ts(g, P)], ident[:])
                ins.then_inc(s_qT, 1)
                pe.wait_ge(s_kr, n + 1)
                pe.wait_ge(s_vr, n + 1)
                for g in range(G):
                    bank = pvk[:, g // 2, (g % 2) * 256:(g % 2) * 256 + VW]
                    ins = pe.matmul(bank, kk[:, bass.ts(g, P)], vo[:, g], start=(c == 0 and g % 2 == 0),
                                    stop=(c == CPB - 1), skip_group_check=True)
                ins.then_inc(s_vk, 1)

            def batch(b, first):
                if not first:
                    pe.wait_ge(s_olo, CPB * b)
                turn_x(CPB * b, first)
                for c in range(CPB):
                    n = CPB * b + c
                    pe.wait_ge(s_xlo, n + 1)
                    for i, (bank, sem, ready) in enumerate(((pq, s_q, s_qr), (pk, s_k, s_kr), (pv, s_v, s_vr))):
                        if not (first and c == 0):
                            pe.wait_ge(ready, n)
                            if c == 0 and i < 2:
                                pe.wait_ge(s_pa, n - i)
                        for kt in range(KT):
                            if first and c == 0 and i == 0:
                                pe.wait_ge(s_wlo, kt + 1)
                            ins = product(pe, bank[:], (x_hi[:, kt], x_lo[:, kt]),
                                          (wq_hi[:, kt, bass.ts(i, DM)], wq_lo[:, kt, bass.ts(i, DM)]),
                                          kt == 0, kt == KT - 1)
                        ins.then_inc(sem, 1)
                    if c < CPB - 1:
                        turn_x(n + 1, False)
                    if c == 0 and not first:
                        pe.wait_ge(s_bd, b)
                        pe.wait_ge(s_od, CPB * b)
                    sums((n, c))

                def attend(c):
                    n = CPB * b + c
                    if c:
                        pe.wait_ge(s_od, n)
                    for g in range(G):
                        ins = pe.matmul(po[:, g // 2, (g % 2) * 256:(g % 2) * 256 + OW], qT[:, c, g], bd[:, g],
                                        start=True, stop=True)
                    ins.then_inc(s_o, 1)

                pe.wait_ge(s_bd, b + 1)
                pe.wait_ge(s_qTc, CPB * b + CPB)
                attend(0)
                if first:
                    pe.wait_ge(s_wlo, WG)
                for c in range(CPB):
                    n = CPB * b + c
                    pe.wait_ge(s_od, n + 1)
                    if c:
                        pe.wait_ge(s_olo, n)
                    for kt in range(KT):
                        ins = pe.transpose(pt[:, bass.ts(kt, P)],
                                           o[:, kt].rearrange("p h d -> p (h d)"), ident[:])
                    ins.then_inc(s_oT, 1)
                    if c < CPB - 1:
                        attend(c + 1)
                    pe.wait_ge(s_olo, n + 1)
                    if c >= 2:
                        pe.wait_ge(s_pa, n - 1)
                    for kt in range(KT):
                        ins = product(pe, (pq, pk)[c % 2][:], (o_hi[:, kt], o_lo[:, kt]),
                                      (wp_hi[:, kt], wp_lo[:, kt]), kt == 0, kt == KT - 1)
                    ins.then_inc(s_p, 1)
            batches(pe, batch)

        @block.vector
        def _(dve):
            tt, ts = nc.vector.tensor_tensor, nc.vector.tensor_scalar
            chain = Chain(dve, c_dve, 2 * CPB)
            flat = lambda ap: ap.rearrange("p k n -> p (k n)")
            dve.wait_ge(s_mem, 6)
            dve.wait_ge(s_small, 16)

            def weights():
                for i in range(WG):
                    dve.wait_ge(s_whi, i + 1)
                    if i < KT:
                        tt(wq_lo[:, i], w_raw[:, i % 2, 0:3 * DM], raw(wq_hi[:, i]), ALU.subtract).then_inc(s_wlo, 1)
                    else:
                        tt(flat(wp_lo[:]), w_raw[:, i % 2], raw(flat(wp_hi[:])), ALU.subtract).then_inc(s_wlo, 1)

            def norm_in(c, n, first):
                dve.wait_ge(s_p, n + 1)
                if not (first and c == 0):
                    dve.wait_ge(s_norm, n)
                tt(rr[:], (pq, pk)[c % 2][:], bias[:], ALU.add).then_inc(s_pa, 1)
                dve.wait_ge(s_pa, n + 1)
                tt(rr[:].unsqueeze(1), rr[:].unsqueeze(1), acc[:, bass.ds(n, 1)], ALU.add).then_inc(s_rr, 1)
                dve.wait_ge(s_rr, n + 1)
                layer_norm_stats(nc, dve, rr[:], stats[:], mv[:], s_bn, s_mv, n + 1, s_small)

            def norm_out(n):
                dve.wait_ge(s_rstd, n + 1)
                ts(acc[:, bass.ds(n, 1)], rr[:].unsqueeze(1), mv[:, 0:1], rstd[:], ALU.subtract,
                   ALU.mult).then_inc(s_norm, 1)

            def batch(b, first):
                chain.round(b)
                for c in range(CPB):
                    n = CPB * b + c
                    dve.wait_ge(s_xhi, n + 1)
                    tt(flat(x_lo[:]), pt[:], raw(flat(x_hi[:])), ALU.subtract).then_inc(s_xlo, 1)
                    if first and c == 0:
                        weights()
                    dve.wait_ge(s_v, n + 1)
                    if not (first and c == 0):
                        dve.wait_ge(s_vk, n)
                    nc.vector.tensor_copy(vo[:, :, 0:P], pv[:].rearrange("p (g n) -> p g n", g=G)).then_inc(s_vr, 1)
                dve.wait_ge(s_vk, CPB * b + CPB)
                if not first:
                    dve.wait_ge(s_o, CPB * b)
                for i in range(2):
                    two = pvk[:, i].rearrange("p (g n) -> p g n", g=2)
                    for g in range(2):
                        sums = two[:, g, P:P + 1].broadcast_to([P, HG])
                        tt(bd[:, 2 * i + g, 0:P], two[:, g, 0:P], same[:].rearrange("p h d -> p (h d)"), ALU.mult)
                        ins = tt(bd[:, 2 * i + g, P:OW], sums, same[:, :, 0], ALU.mult)
                ins.then_inc(s_bd, 1)
                for c in range(CPB):
                    n = CPB * b + c
                    dve.wait_ge(s_o, n + 1)
                    outs = po[:].rearrange("p t (g n) -> p (t g) n", g=2)
                    chain.link(ts(den[:], outs[:, :, P:OW], AEPS, None, ALU.add))
                    chain.link(nc.vector.reciprocal(den[:], den[:]))
                    if not (first and c == 0):
                        dve.wait_ge(s_oT, n)
                    for g in range(G):
                        ins = tt(o[:, g], outs[:, g, 0:P].rearrange("p (h d) -> p h d", h=HG),
                                 den[:, g].unsqueeze(2).broadcast_to([P, HG, AD]), ALU.mult)
                    ins.then_inc(s_od, 1)
                    dve.wait_ge(s_ohi, n + 1)
                    tt(flat(o_lo[:]), pt[:], raw(flat(o_hi[:])), ALU.subtract).then_inc(s_olo, 1)
                    if c:
                        norm_in(c - 1, n - 1, first)
                        norm_out(n - 1)
                norm_in(CPB - 1, CPB * b + CPB - 1, False)
                norm_out(CPB * b + CPB - 1)
            batches(dve, batch)
            dve.wait_ge(s_norm, NCH)


def build(nc, t):
    in_proj(nc, t)
    ssd_phase(nc, t)
    with nc.sbuf_tensor("acc", [P, NCH, DM], F32) as acc:
        ffn_phase(nc, t, acc, gated=False)
        attn_phase(nc, t, acc)
        ffn_phase(nc, t, acc, gated=True)


def lay_out(inp):
    import numpy as np

    def cm(w):
        return w.T.reshape(w.shape[1] // P, P, w.shape[0]).transpose(1, 0, 2)

    def rows(v):
        return np.broadcast_to(v, (P, v.shape[0]))

    def up_tiles(w):
        u, n = w.shape[:2]
        return w.reshape(u, n, KT, P, 4, P).transpose(0, 3, 1, 4, 2, 5)

    def down_tiles(w):
        return w.reshape(w.shape[0], 4, P, DM).transpose(0, 2, 1, 3)

    a = {n: np.asarray(v) for n, v in inp.items()}
    w = a["L0_attn_in_proj_w"].reshape(2, IT, P, DM).transpose(1, 0, 2, 3).reshape(2 * DI, DM)
    laid = {
        "x": a["L0_attn_x"],
        "x_rows": a["L0_attn_x"].reshape(TOK, DM),
        "in_w": cm(w).reshape(P, KT, 4, 4 * P).transpose(0, 2, 1, 3),
        "conv_w": a["L0_attn_conv_w"].reshape(IT, P, TAPS).transpose(1, 0, 2),
        "conv_b": a["L0_attn_conv_b"].reshape(IT, P).T,
        "x_w": cm(a["L0_attn_x_proj_w"]),
        "out_w": cm(a["L0_attn_out_proj_w"]).reshape(P, IT // 2, 2 * DM),
        "dtw": a["L0_attn_dt_proj_w"].T,
        "dtb": rows(a["L0_attn_dt_proj_b"]),
        "a_log": rows(a["L0_attn_A_log"]),
        "d_skip": rows(a["L0_attn_D"]),
        "f_router": cm(a["L0_ffn_Wr"]),
        "f_rb": rows(a["L0_ffn_br"]),
        "f_up": up_tiles(a["L0_ffn_W1"].T.reshape(DM, 4, 1, DM).transpose(1, 2, 0, 3)),
        "f_dn": down_tiles(a["L0_ffn_W2"].T.reshape(4, DM, DM)),
        "qkv_w": cm(a["L1_attn_w_qkv"]).transpose(1, 0, 2),
        "proj_w": cm(a["L1_attn_w_proj"]),
        "proj_b": rows(a["L1_attn_b_proj"]),
        "e_router": a["L1_ffn_Wr"].reshape(KT, P, 8).transpose(1, 0, 2),
        "e_rb": rows(a["L1_ffn_temperature"]),
        "e_up": up_tiles(np.stack([a["L1_ffn_Wg"], a["L1_ffn_Wu"]], 1)),
        "e_dn": down_tiles(a["L1_ffn_Wd"]),
        "la_up": np.stack([a["L1_ffn_Ga"], a["L1_ffn_Ua"]], 1).transpose(0, 1, 3, 2).reshape(2, P, DM),
        "lb_up": np.stack([a["L1_ffn_Gb"], a["L1_ffn_Ub"]], 1).reshape(2, P, DM),
        "la_dn": a["L1_ffn_Da"].transpose(0, 2, 1),
        "lb_dn": a["L1_ffn_Db"],
    }
    return {n: np.ascontiguousarray(v) for n, v in laid.items()}


def kernel(**inputs):
    import concourse.bacc as bacc
    from concourse.bass_utils import run_bass_kernel_spmd as run

    laid = lay_out(inputs)
    nc = bacc.Bacc("TRN2", target_bir_lowering=False, num_devices=1)
    t = {n: nc.dram_tensor(f"in_{n}", v.shape, F32, kind="ExternalInput").ap() for n, v in laid.items()}
    for n, shape in (("xb", (IT, P, TOK)), ("zs", (IT, P, TOK)), ("x1", (TOK, DM))):
        t[n] = nc.dram_tensor(n, shape, F32, kind="Internal").ap()
    t["out"] = nc.dram_tensor("out", (NB, SEQ, DM), F32, kind="ExternalOutput").ap()
    build(nc, t)
    r = run(nc, [{f"in_{n}": v for n, v in laid.items()}], core_ids=[0])
    return r.results[0]["out"]
```

```python
from contextlib import ExitStack

import concourse.bass as bass
from concourse import mybir

F32 = mybir.dt.float32
F32R = mybir.dt.float32r
ALU = mybir.AluOpType
ACT = mybir.ActivationFunctionType
AX_X = mybir.AxisListType.X

P = 128
NB, SEQ, DM = 4, 512, 512
TOK = NB * SEQ
NCH = TOK // P
CPB = SEQ // P
KT = DM // P
DI = 2 * DM
IT = DI // P
NH, HD = 16, 64
NS = 128
TAPS = 4
EPS = 1e-5


class Kit:

    def __init__(self, nc, ctx, tag):
        self.nc, self.ctx, self.tag, self.sems = nc, ctx, tag, []
        ctx.callback(self.close)

    def sb(self, name, shape, dt=F32):
        return self.ctx.enter_context(self.nc.sbuf_tensor(f"{self.tag}_{name}", shape, dt))

    def ps(self, name, shape):
        return self.ctx.enter_context(self.nc.psum_tensor(f"{self.tag}_{name}", shape, F32))

    def sem(self, name):
        self.sems.append(self.nc.alloc_semaphore(f"{self.tag}_{name}"))
        return self.sems[-1]

    def close(self):
        self.nc.clear_and_free_semaphores(self.sems)
        self.nc.all_engine_barrier()

    def block(self):
        return self.ctx.enter_context(self.nc.Block())


class Chain:

    def __init__(self, eng, sem, per):
        self.eng, self.sem, self.per, self.base, self.k = eng, sem, per, 0, 0

    def round(self, g):
        self.base, self.k = g * self.per, 0

    def link(self, ins):
        self.k += 1
        ins.then_inc(self.sem, 1)
        self.eng.wait_ge(self.sem, self.base + self.k)

    def close(self):
        assert self.k <= self.per, (self.k, self.per)
        if self.k < self.per:
            self.eng.sem_inc(self.sem, self.per - self.k)
            self.k = self.per


def raw(ap):
    return ap.bitcast(F32)


def product(pe, out, lhs, rhs, first=True, last=True):
    (lh, ll), (rh, rl) = lhs, rhs
    pe.matmul(out, lh, rh, start=first, stop=False)
    pe.matmul(out, lh, rl, start=False, stop=False)
    return pe.matmul(out, ll, rh, start=False, stop=last)


def in_proj(nc, t):
    with ExitStack() as ctx:
        k = Kit(nc, ctx, "in")
        MT = 2 * IT
        GRP = 4
        TPG = MT // GRP
        x_tok = k.sb("x_tok", [P, NB, CPB, DM])
        x_hi, x_lo = k.sb("x_hi", [P, KT, TOK], F32R), k.sb("x_lo", [P, KT, TOK], F32R)
        w_raw = k.sb("w_raw", [P, 2, KT, TPG * P])
        w_hi, w_lo = (k.sb(n, [P, GRP, KT, TPG * P], F32R) for n in ("w_hi", "w_lo"))
        conv = k.sb("conv", [P, 2, SEQ])
        out = k.sb("out", [P, 4, SEQ])
        cw = k.sb("cw", [P, IT, TAPS])
        cb = k.sb("cb", [P, IT])
        ident = k.sb("ident", [P, P])
        tp = k.ps("tp", [P, 4, 512])
        acc = k.ps("acc", [P, 4, 512])

        s_x = [k.sem(f"x_loaded{b}") for b in range(NB)]
        s_w = [k.sem(f"w_loaded{g}") for g in range(2)]
        s_small = k.sem("conv_params_loaded")
        s_ident = k.sem("ident_ready")
        s_xT = k.sem("x_transposed")
        s_xhi, s_xlo = k.sem("x_hi_ready"), k.sem("x_lo_ready")
        s_whi, s_wlo = k.sem("w_hi_ready"), k.sem("w_lo_ready")
        s_xacc, s_zacc = k.sem("x_tile_summed"), k.sem("z_tile_summed")
        s_taps = k.sem("conv_taps_added")
        s_c = k.sem("conv_tile_started")
        s_xo, s_zo = k.sem("x_tile_out"), k.sem("z_tile_out")
        s_st = [k.sem(f"stored{i}") for i in range(4)]
        block = k.block()

        @block.sync
        def _(sp):
            for b in range(NB):
                sp.dma_start(x_tok[:, b], t["x"][b].rearrange("(c p) d -> p c d", p=P)).then_inc(s_x[b], 16)
                if b == 0:
                    sp.dma_start(cw[:], t["conv_w"]).then_inc(s_small, 16)
                    sp.dma_start(cb[:], t["conv_b"]).then_inc(s_small, 16)
                if b >= 2:
                    sp.wait_ge(s_wlo, b - 1)
                sp.dma_start(w_raw[:, b % 2], t["in_w"][:, b]).then_inc(s_w[b % 2], 16)
            for i in range(4):
                sp.sem_inc(s_st[i], 16)
            with sp.Fori(0, NB) as b:
                for j in range(IT):
                    sp.wait_ge(s_xo, b * IT + j + 1 + 2)
                    sp.dma_start(t["xb"][j][:, bass.ts(b, SEQ)], out[:, 2 * j % 4]).then_inc(s_st[2 * j % 4], 16)
                    sp.wait_ge(s_zo, b * IT + j + 1 + 2)
                    sp.dma_start(t["zs"][j][:, bass.ts(b, SEQ)], out[:, (2 * j + 1) % 4]).then_inc(s_st[(2 * j + 1) % 4], 16)
            for i in range(4):
                sp.wait_ge(s_st[i], 16 * (NB * MT // 4 + 1))

        @block.gpsimd
        def _(pool):
            nc.gpsimd.memset(ident[:], 0.0).then_inc(s_ident, 1)
            pool.wait_ge(s_ident, 1)
            nc.gpsimd.affine_select(out=ident[:], in_=ident[:], compare_op=ALU.not_equal, fill=1.0, base=0,
                                    pattern=[[-1, P]], channel_multiplier=1).then_inc(s_ident, 1)

        @block.tensor
        def _(pe):
            pe.wait_ge(s_ident, 2)
            for b in range(NB):
                pe.wait_ge(s_x[b], 16)
                for kt in range(KT):
                    n = b * KT + kt
                    if n >= 4:
                        pe.wait_ge(s_xlo, n - 3)
                    for c in range(CPB):
                        ins = pe.transpose(tp[:, n % 4, bass.ts(c, P)], x_tok[:, b, c, bass.ts(kt, P)], ident[:])
                    ins.then_inc(s_xT, 1)
            with pe.Fori(0, NB) as b:
                pe.wait_ge(s_xlo, b * KT + KT)
                for m in range(MT):
                    if m % TPG == 0:
                        pe.wait_ge(s_wlo, m // TPG + 1)
                    n = b * IT + m // 2
                    if m % 2:
                        pe.wait_ge(s_zo, n - 1 + 2)
                    else:
                        pe.wait_ge(s_taps, 3 * (n - 1) + 6)
                    col = bass.ts(m % TPG, P)
                    for kt in range(KT):
                        ins = product(pe, acc[:, m % 4],
                                      (w_hi[:, m // TPG, kt, col], w_lo[:, m // TPG, kt, col]),
                                      (x_hi[:, kt, bass.ts(b, SEQ)], x_lo[:, kt, bass.ts(b, SEQ)]),
                                      kt == 0, kt == KT - 1)
                    ins.then_inc(s_zacc if m % 2 else s_xacc, 1)

        @block.scalar
        def _(act):
            act.sem_inc(s_xo, 2)
            act.sem_inc(s_zo, 2)

            def hi_of_x(b):
                for kt in range(KT):
                    n = b * KT + kt
                    act.wait_ge(s_xT, n + 1)
                    nc.scalar.activation(x_hi[:, kt, bass.ts(b, SEQ)], tp[:, n % 4], ACT.Copy).then_inc(s_xhi, 1)

            def hi_of_w(g):
                act.wait_ge(s_w[g % 2], 16 * (g // 2 + 1))
                nc.scalar.activation(w_hi[:, g], w_raw[:, g % 2], ACT.Copy).then_inc(s_whi, 1)

            for b in range(NB):
                hi_of_x(b)
                hi_of_w(b)
            act.wait_ge(s_small, 32)
            with act.Fori(0, NB) as b:
                for j in range(IT):
                    n = b * IT + j
                    act.wait_ge(s_xacc, n + 1)
                    act.wait_ge(s_xo, n - 1 + 2)
                    nc.scalar.activation(conv[:, j % 2], acc[:, 2 * j % 4], ACT.Identity,
                                         bias=cb[:, j:j + 1], scale=cw[:, j, TAPS - 1:TAPS]).then_inc(s_c, 1)
                    slot, turn = 2 * j % 4, 16 * (b * (MT // 4) + 2 * j // 4 + 1)
                    act.wait_ge(s_taps, 3 * (n + 1) + 6)
                    act.wait_ge(s_st[slot], turn)
                    nc.scalar.activation(out[:, slot], conv[:, j % 2], ACT.Silu).then_inc(s_xo, 1)
                    act.wait_ge(s_zacc, n + 1)
                    act.wait_ge(s_st[slot + 1], turn)
                    nc.scalar.activation(out[:, slot + 1], acc[:, slot + 1], ACT.Silu).then_inc(s_zo, 1)

        @block.vector
        def _(dve):
            dve.sem_inc(s_taps, 6)
            for b in range(NB):
                for kt in range(KT):
                    n = b * KT + kt
                    dve.wait_ge(s_xhi, n + 1)
                    x = bass.ts(b, SEQ)
                    nc.vector.tensor_tensor(x_lo[:, kt, x], tp[:, n % 4], raw(x_hi[:, kt, x]),
                                            ALU.subtract).then_inc(s_xlo, 1)
                dve.wait_ge(s_whi, b + 1)
                nc.vector.tensor_tensor(w_lo[:, b], w_raw[:, b % 2], raw(w_hi[:, b]), ALU.subtract).then_inc(s_wlo, 1)
            with dve.Fori(0, NB) as b:
                for j in range(IT):
                    n = b * IT + j
                    dve.wait_ge(s_c, n + 1)
                    for d in range(1, TAPS):
                        dve.wait_ge(s_taps, 3 * n + d - 1 + 6)
                        nc.vector.scalar_tensor_tensor(
                            out=conv[:, j % 2, d:SEQ], in0=acc[:, 2 * j % 4, 0:SEQ - d],
                            scalar=cw[:, j, TAPS - 1 - d:TAPS - d], in1=conv[:, j % 2, d:SEQ],
                            op0=ALU.mult, op1=ALU.add).then_inc(s_taps, 1)


def layer_norm_stats(nc, dve, x, stats, mv, s_bn, sem, n, met):
    n = n if isinstance(n, int) else dve.snap(n)
    nc.vector.bn_stats(stats, x).then_inc(s_bn, 1)
    dve.wait_ge(met, 1)
    dve.wait_ge(s_bn, n)
    nc.vector.bn_aggr(mv, stats).then_inc(sem, 1)


def inverse_deviation(nc, pool, mv, rstd, const, s_mv, s_eps, s_rstd, n):
    pool.wait_ge(s_mv, n)
    nc.gpsimd.tensor_tensor(rstd, mv[:, 1:2], const[:, 0:1], ALU.add).then_inc(s_eps, 1)
    pool.wait_ge(s_eps, n)
    nc.gpsimd.tensor_tensor(rstd, rstd, const[:, 1:2], ALU.pow).then_inc(s_rstd, 1)


def make_identity(nc, pool, ident, sem):
    nc.gpsimd.memset(ident, 0.0).then_inc(sem, 1)
    pool.wait_ge(sem, 1)
    nc.gpsimd.affine_select(out=ident, in_=ident, compare_op=ALU.not_equal, fill=1.0, base=0,
                            pattern=[[-1, P]], channel_multiplier=1).then_inc(sem, 1)


def ssd_phase(nc, t):
    with ExitStack() as ctx:
        k = Kit(nc, ctx, "ssd")
        XC = DI + NH + 2 * NS
        BC = NH + 2 * NS
        wx_hi, wx_lo = (k.sb(n, [P, IT, XC], F32R) for n in ("wx_hi", "wx_lo"))
        wo_hi, wo_lo = (k.sb(n, [P, IT, DM], F32R) for n in ("wo_hi", "wo_lo"))
        x_raw = k.sb("x_raw", [P, IT, P])
        x_hi, x_lo = k.sb("x_hi", [P, IT, P], F32R), k.sb("x_lo", [P, IT, P], F32R)
        z_raw = k.sb("z_raw", [P, IT, P])
        res = k.sb("res", [P, DM])
        bcd = k.sb("bcd", [P, BC])
        bct = k.sb("bct", [P, 2 * NS])
        b_tok = k.sb("b_tok", [P, NS])
        dtT = k.sb("dtT", [NH, P])
        xf = k.sb("xf", [P, NH, HD])
        xs = k.sb("xs", [P, NH, HD])
        xd = k.sb("xd", [P, NH, HD])
        xdec = k.sb("xdec", [P, NH, HD])
        r_hi, r_lo = k.sb("r_hi", [P, NH, P], F32R), k.sb("r_lo", [P, NH, P], F32R)
        decay = k.sb("decay", [P, NH, P])
        mix = k.sb("mix", [P, NH, P])
        state = k.sb("state", [P, NH, HD])
        y = k.sb("y", [P, NH, HD])
        g_f = k.sb("g_f", [P, IT, P])
        g_hi, g_lo = k.sb("g_hi", [P, IT, P], F32R), k.sb("g_lo", [P, IT, P], F32R)
        rr = k.sb("rr", [P, DM])
        cb_m = k.sb("cb_m", [P, P])
        tri = k.sb("tri", [P, P])
        strict_r = k.sb("strict_r", [P, P], F32R)
        ones, ident = k.sb("ones", [P, P]), k.sb("ident", [P, P])
        keep = k.sb("keep", [P, NCH])
        dtw = k.sb("dtw", [NH, NH])
        dtb, a_pos, d_skip = (k.sb(n, [P, NH]) for n in ("dtb", "a_pos", "d_skip"))
        v, na, u, s2, q, dt, a = (k.sb(n, [P, NH]) for n in ("v", "na", "u", "s2", "q", "dt", "a"))
        s1 = na
        a_hi, a_lo = k.sb("a_hi", [P, NH], F32R), k.sb("a_lo", [P, NH])
        ed = k.sb("ed", [P, 3, NH])
        ek = k.sb("ek", [P, NH])
        stats, mv = k.sb("stats", [P, 6]), k.sb("mv", [P, 2])
        rstd, const = k.sb("rstd", [P, 1]), k.sb("const", [P, 2])
        pa, pb, po, psm = (k.ps(n, [P, 512]) for n in ("pa", "pb", "po", "psm"))
        pd = k.ps("pd", [P, 4, 512])
        CB, DTP, SUM = psm[:, 0:P], psm[:, 384:384 + NH], psm[:, 400:400 + 3 * NH]
        staging = (decay[:].rearrange("p h l -> p (h l)"), mix[:].rearrange("p h l -> p (h l)"))
        WG = IT + IT // 2

        s_const, s_tri, s_ident = k.sem("constants_ready"), k.sem("triangles_ready"), k.sem("ident_ready")
        s_small = k.sem("small_loaded")
        s_w = [k.sem(f"w_loaded{i}") for i in range(2)]
        s_whi, s_wlo = k.sem("w_hi_ready"), k.sem("w_lo_ready")
        s_lx, s_lz, s_lr = k.sem("x_loaded"), k.sem("z_loaded"), k.sem("residual_loaded")
        s_apos, s_strict = k.sem("a_exp_ready"), k.sem("strict_r_ready")
        s_xhi, s_xlo = k.sem("x_hi_ready"), k.sem("x_lo_ready")
        s_p0, s_p1, s_p2 = k.sem("X_left_half_summed"), k.sem("X_right_half_summed"), k.sem("BC_summed")
        s_xc, s_bc = k.sem("X_half_copied"), k.sem("BC_copied")
        s_t2, s_bct, s_btok = k.sem("BC_transposed"), k.sem("BC_turned_copied"), k.sem("B_copied")
        s_p3 = k.sem("CB_and_dt_summed")
        s_na, s_u = k.sem("minus_abs_dt_ready"), k.sem("exp_dt_ready")
        s_dt, s_a, s_al = k.sem("dt_ready"), k.sem("a_ready"), k.sem("a_lo_ready")
        s_r, s_rp = k.sem("r_by_dve"), k.sem("r_by_pool")
        s_sum, s_ed, s_ek = k.sem("a_sums_ready"), k.sem("decays_ready"), k.sem("state_decay_ready")
        s_diff, s_dec = k.sem("exponents_summed"), k.sem("decay_matrix_ready")
        s_cbm, s_mix = k.sem("CB_masked"), k.sem("mix_ready")
        s_xs, s_xd, s_xdec = k.sem("X_dt_ready"), k.sem("X_D_ready"), k.sem("X_decayed_ready")
        s_yoff, s_ydiag, s_st = k.sem("y_from_state_summed"), k.sem("y_in_chunk_summed"), k.sem("state_summed")
        s_yx, s_y = k.sem("skip_added"), k.sem("y_ready")
        s_sd, s_sa = k.sem("state_decayed"), k.sem("state_half_added")
        s_yT, s_g, s_ghi, s_glo = k.sem("y_transposed"), k.sem("gated"), k.sem("g_hi_ready"), k.sem("g_lo_ready")
        s_op, s_rr, s_mv, s_eps, s_rstd = (k.sem(n) for n in ("out_proj_summed", "residual_added", "mv_ready",
                                                             "eps_added", "rstd_ready"))
        s_bn = k.sem("bn_stats_ready")
        s_x1, s_out = k.sem("x1_ready"), k.sem("x1_stored")
        c_dve = k.sem("dve_steps")
        block = k.block()

        def chunks(eng, step):
            step(0, True, False, 2)
            step(1, False, True, 2)
            with eng.Fori(2, NCH - 2) as g:
                step(g, False, False, 2)
            step(NCH - 2, False, False, 1)
            step(NCH - 1, False, False, 0)

        @block.sync
        def _(sp):
            for n in ("dtw", "dtb", "a_log", "d_skip"):
                dst = {"dtw": dtw, "dtb": dtb, "a_log": a_pos, "d_skip": d_skip}[n]
                sp.dma_start(dst[:], t[n]).then_inc(s_small, 16)
            sp.dma_start(x_raw[:], t["xb"][:, :, 0:P].rearrange("j p n -> p j n")).then_inc(s_lx, 16)
            for i in range(WG):
                if i >= 2:
                    sp.wait_ge(s_wlo, i - 1)
                if i < IT:
                    sp.dma_start(staging[i % 2][:, 0:XC], t["x_w"][:, i]).then_inc(s_w[i % 2], 16)
                else:
                    sp.dma_start(staging[i % 2][:, 0:2 * DM], t["out_w"][:, i - IT]).then_inc(s_w[i % 2], 16)

            def x_load(g):
                sp.wait_ge(s_small, 64)
                sp.wait_ge(s_xlo, g)
                sp.dma_start(x_raw[:], t["xb"][:, :, bass.ds(g * P, P)].rearrange("j p n -> p j n")).then_inc(s_lx, 16)

            def step(g, first, second, left):
                if left == 2:
                    x_load(g + 2)
                if not first:
                    sp.wait_ge(s_small, 64)
                    sp.wait_ge(s_g, g)
                sp.dma_start(z_raw[:], t["zs"][:, :, bass.ds(g * P, P)].rearrange("j p n -> p j n")).then_inc(s_lz, 16)
                if not first:
                    sp.wait_ge(s_small, 64)
                    sp.wait_ge(s_rr, g)
                sp.dma_start(res[:], t["x_rows"][bass.ds(g * P, P), :]).then_inc(s_lr, 16)
                if not first:
                    sp.wait_ge(s_small, 64)
                    sp.wait_ge(s_x1, g)
                    sp.dma_start(t["x1"][bass.ds(g * P - P, P), :], rr[:]).then_inc(s_out, 16)
            x_load(1)
            chunks(sp, step)
            sp.wait_ge(s_x1, NCH)
            sp.dma_start(t["x1"][TOK - P:TOK, :], rr[:]).then_inc(s_out, 16)
            sp.wait_ge(s_out, 16 * NCH)

        @block.gpsimd
        def _(pool):
            nc.gpsimd.memset(ones[:], 1.0).then_inc(s_const, 1)
            nc.gpsimd.memset(state[:], 0.0).then_inc(s_const, 1)
            nc.gpsimd.memset(keep[:], 1.0).then_inc(s_const, 1)
            nc.gpsimd.memset(const[:, 0:1], EPS).then_inc(s_const, 1)
            nc.gpsimd.memset(const[:, 1:2], -0.5).then_inc(s_const, 1)
            pool.wait_ge(s_const, 3)
            nc.gpsimd.memset(keep[:, CPB - 1::CPB], 0.0).then_inc(s_const, 1)
            nc.gpsimd.affine_select(out=tri[:], in_=ones[:], compare_op=ALU.is_ge, fill=0.0, base=0,
                                    pattern=[[1, P]], channel_multiplier=-1).then_inc(s_tri, 1)
            nc.gpsimd.affine_select(out=cb_m[:], in_=ones[:], compare_op=ALU.is_ge, fill=0.0, base=-1,
                                    pattern=[[-1, P]], channel_multiplier=1).then_inc(s_tri, 1)
            make_identity(nc, pool, ident[:], s_ident)
            pool.wait_ge(s_const, 6)

            def step(g, first, second, left):
                if not first:
                    low_of_gated(g - 1)
                pool.wait_ge(s_al, g + 1)
                if not first:
                    pool.wait_ge(s_diff, g)
                half = NH // 2
                nc.gpsimd.tensor_tensor(r_lo[:, 0:half], tri[:].unsqueeze(1).broadcast_to([P, half, P]),
                                        a_lo[:, 0:half].unsqueeze(2).broadcast_to([P, half, P]),
                                        ALU.mult).then_inc(s_rp, 1)
                pool.wait_ge(s_xc, 2 * g + 2)
                if not first:
                    pool.wait_ge(s_y, g)
                nc.gpsimd.tensor_tensor(xd[:], xf[:], d_skip[:].unsqueeze(2).broadcast_to([P, NH, HD]),
                                        ALU.mult).then_inc(s_xd, 1)
                pool.wait_ge(s_xs, g + 1)
                pool.wait_ge(s_ed, g + 1)
                if not first:
                    pool.wait_ge(s_st, g)
                nc.gpsimd.tensor_tensor(xdec[:], xs[:], ed[:, 1].unsqueeze(2).broadcast_to([P, NH, HD]),
                                        ALU.mult).then_inc(s_xdec, 1)
                pool.wait_ge(s_yoff, g + 1)
                pool.wait_ge(s_ek, g + 1)
                if not first:
                    pool.wait_ge(s_sa, 2 * g)
                nc.gpsimd.tensor_tensor(state[:], state[:], ek[:].unsqueeze(2).broadcast_to([P, NH, HD]),
                                        ALU.mult).then_inc(s_sd, 1)
                if not first:
                    inverse_deviation(nc, pool, mv[:], rstd[:], const[:], s_mv, s_eps, s_rstd, g)

            def low_of_gated(g):
                pool.wait_ge(s_ghi, g + 1)
                nc.gpsimd.tensor_tensor(g_lo[:], g_f[:], raw(g_hi[:]), ALU.subtract).then_inc(s_glo, 1)

            pool.wait_ge(s_small, 64)
            chunks(pool, step)
            low_of_gated(NCH - 1)
            inverse_deviation(nc, pool, mv[:], rstd[:], const[:], s_mv, s_eps, s_rstd, NCH)

        @block.scalar
        def _(act):
            act.wait_ge(s_small, 64)
            nc.scalar.activation(a_pos[:], a_pos[:], ACT.Exp).then_inc(s_apos, 1)
            act.wait_ge(s_tri, 2)
            nc.scalar.activation(strict_r[:], cb_m[:], ACT.Copy).then_inc(s_strict, 1)

            def x_high(g, first=False):
                act.wait_ge(s_lx, 16 * (g + 1))
                if not first:
                    act.wait_ge(s_p2, g)
                nc.scalar.activation(x_hi[:], x_raw[:], ACT.Copy).then_inc(s_xhi, 1)

            def x_copies(g, first=False):
                for i, (bank, sem) in enumerate(((pa, s_p0), (pb, s_p1))):
                    act.wait_ge(sem, g + 1)
                    if i == 0 and not first:
                        act.wait_ge(s_xs, g)
                        act.wait_ge(s_xd, g)
                    nc.scalar.activation(xf[:, i * NH // 2:(i + 1) * NH // 2].rearrange("p h d -> p (h d)"),
                                         bank[:], ACT.Copy).then_inc(s_xc, 1)

            def bc_copy(g, first=False):
                act.wait_ge(s_p2, g + 1)
                if not first:
                    act.wait_ge(s_t2, g)
                    act.wait_ge(s_btok, g)
                nc.scalar.activation(bcd[:], pa[:, 0:BC], ACT.Copy).then_inc(s_bc, 1)

            x_high(0, True)
            for i in range(WG):
                act.wait_ge(s_w[i % 2], 16 * (i // 2 + 1))
                if i < IT:
                    nc.scalar.activation(wx_hi[:, i], staging[i % 2][:, 0:XC], ACT.Copy).then_inc(s_whi, 1)
                else:
                    o = 2 * (i - IT)
                    nc.scalar.activation(wo_hi[:, o:o + 2].rearrange("p k n -> p (k n)"),
                                         staging[i % 2][:, 0:2 * DM], ACT.Copy).then_inc(s_whi, 1)
            x_copies(0, True)
            bc_copy(0, True)
            x_high(1)

            def g_high(g, first):
                act.wait_ge(s_g, g + 1)
                if not first:
                    act.wait_ge(s_op, g)
                nc.scalar.activation(g_hi[:], g_f[:], ACT.Copy).then_inc(s_ghi, 1)

            def step(g, first, second, left):
                act.wait_ge(s_t2, g + 1)
                if not first:
                    act.wait_ge(s_st, g)
                nc.scalar.activation(bct[:], psm[:, 0:2 * NS], ACT.Copy).then_inc(s_bct, 1)
                nc.scalar.activation(dtT[:], psm[0:NH, 2 * NS:3 * NS], ACT.Copy).then_inc(s_bct, 1)
                act.wait_ge(s_bc, g + 1)
                nc.scalar.activation(b_tok[:], bcd[:, NH:NH + NS], ACT.Copy).then_inc(s_btok, 1)
                act.wait_ge(s_na, g + 1)
                nc.scalar.activation(u[:], na[:], ACT.Exp).then_inc(s_u, 1)
                if not first:
                    g_high(g - 1, second)
                if left:
                    x_copies(g + 1)
                act.wait_ge(s_sum, g + 1)
                if not first:
                    act.wait_ge(s_sd, g)
                    act.wait_ge(s_y, g)
                    act.wait_ge(s_ek, g)
                nc.scalar.activation(ed[:].rearrange("p k h -> p (k h)"), SUM, ACT.Exp).then_inc(s_ed, 1)
                act.wait_ge(s_diff, g + 1)
                if not first:
                    act.wait_ge(s_mix, g)
                nc.scalar.activation(decay[:].rearrange("p h l -> p (h l)"),
                                     pd[:].rearrange("p q n -> p (q n)"), ACT.Exp).then_inc(s_dec, 1)
                if left:
                    bc_copy(g + 1)
                if left == 2:
                    x_high(g + 2)
            chunks(act, step)
            g_high(NCH - 1, False)

        @block.tensor
        def _(pe):
            def x_proj(g, piece, first=False, second=False):
                bank, lo, n, sem = ((pa, 0, 512, s_p0), (pb, 512, 512, s_p1), (pa, 2 * 512, BC, s_p2))[piece]
                if piece == 0:
                    pe.wait_ge(s_xlo, g + 1)
                if piece == 2:
                    pe.wait_ge(s_xc, 2 * g + 1)
                elif not first:
                    pe.wait_ge(s_bc, g)
                    if not second:
                        pe.wait_ge(s_sa, 2 * (g - 2) + 1 + piece)
                for kt in range(IT):
                    if first:
                        pe.wait_ge(s_wlo, kt + 1)
                    ins = product(pe, bank[:, 0:n], (x_hi[:, kt], x_lo[:, kt]),
                                  (wx_hi[:, kt, lo:lo + n], wx_lo[:, kt, lo:lo + n]), kt == 0, kt == IT - 1)
                ins.then_inc(sem, 1)

            def turn_y(g):
                pe.wait_ge(s_y, g + 1)
                for j in range(IT):
                    ins = pe.transpose(pd[:, j // 4, bass.ts(j % 4, P)],
                                       y[:, 2 * j:2 * j + 2].rearrange("p h d -> p (h d)"), ident[:])
                ins.then_inc(s_yT, 1)

            def out_proj(g, first):
                pe.wait_ge(s_glo, g + 1)
                if not first:
                    pe.wait_ge(s_rr, g)
                for kt in range(IT):
                    ins = product(pe, po[:], (g_hi[:, kt], g_lo[:, kt]), (wo_hi[:, kt], wo_lo[:, kt]),
                                  kt == 0, kt == IT - 1)
                ins.then_inc(s_op, 1)

            def step(g, first, second, left):
                pe.wait_ge(s_bc, g + 1)
                if not first:
                    pe.wait_ge(s_ed, g)
                pe.transpose(psm[:, 0:NS], bcd[:, NH:NH + NS], ident[:])
                pe.transpose(psm[:, NS:2 * NS], bcd[:, NH + NS:BC], ident[:])
                pe.transpose(psm[0:NH, 2 * NS:3 * NS], bcd[:, 0:NH], ident[:]).then_inc(s_t2, 1)
                if left:
                    x_proj(g + 1, 0, second=first)
                if not first:
                    turn_y(g - 1)
                pe.wait_ge(s_bct, 2 * g + 2)
                pe.matmul(CB, bct[:, 0:NS], bct[:, NS:2 * NS], start=True, stop=True)
                pe.matmul(DTP, dtT[:], dtw[:], start=True, stop=True).then_inc(s_p3, 1)
                if left:
                    x_proj(g + 1, 1, second=first)
                pe.wait_ge(s_a, g + 1)
                pe.wait_ge(s_cbm, g + 1)
                for i, m in enumerate((tri[:], raw(strict_r[:]), ones[:])):
                    ins = pe.matmul(SUM[:, i * NH:(i + 1) * NH], m, a[:], start=True, stop=True)
                ins.then_inc(s_sum, 1)
                if not first:
                    out_proj(g - 1, second)
                pe.wait_ge(s_r, g + 1)
                pe.wait_ge(s_rp, g + 1)
                if not first:
                    pe.wait_ge(s_g, g)
                for i in range(4):
                    heads = slice(4 * i, 4 * i + 4)
                    pe.matmul(pd[:, i], strict_r[:], r_hi[:, heads].rearrange("p h l -> p (h l)"),
                              start=True, stop=False)
                    ins = pe.matmul(pd[:, i], strict_r[:], r_lo[:, heads].rearrange("p h l -> p (h l)"),
                                    start=False, stop=True)
                ins.then_inc(s_diff, 1)
                if left:
                    x_proj(g + 1, 2)
                pe.wait_ge(s_dec, g + 1)
                if not first:
                    pe.wait_ge(s_sa, 2 * g)
                for i in range(2):
                    ins = pe.matmul(pd[:, i], bct[:, NS:2 * NS],
                                    state[:, i * NH // 2:(i + 1) * NH // 2].rearrange("p h d -> p (h d)"),
                                    start=True, stop=True)
                ins.then_inc(s_yoff, 1)
                pe.wait_ge(s_xdec, g + 1)
                if left:
                    pe.wait_ge(s_xc, 2 * g + 4)
                    pe.wait_ge(s_bc, g + 2)
                for i, bank in enumerate((pa, pb)):
                    ins = pe.matmul(bank[:], b_tok[:],
                                    xdec[:, i * NH // 2:(i + 1) * NH // 2].rearrange("p h d -> p (h d)"),
                                    start=True, stop=True)
                ins.then_inc(s_st, 1)
                pe.wait_ge(s_mix, g + 1)
                pe.wait_ge(s_xs, g + 1)
                for h in range(NH):
                    ins = pe.matmul(pd[:, 2 + h // 8, bass.ts(h % 8, HD)], mix[:, h], xs[:, h],
                                    start=True, stop=True)
                ins.then_inc(s_ydiag, 1)

            pe.wait_ge(s_const, 6)
            pe.wait_ge(s_tri, 2)
            pe.wait_ge(s_ident, 2)
            pe.wait_ge(s_strict, 1)
            pe.wait_ge(s_small, 64)
            for piece in range(3):
                x_proj(0, piece, True)
            pe.wait_ge(s_wlo, WG)
            chunks(pe, step)
            turn_y(NCH - 1)
            out_proj(NCH - 1, False)

        @block.vector
        def _(dve):
            chain = Chain(dve, c_dve, 17)
            tt, stt, ts = nc.vector.tensor_tensor, nc.vector.scalar_tensor_tensor, nc.vector.tensor_scalar
            heads = lambda ap, n: ap.unsqueeze(2).broadcast_to([P, ap.shape[1], n])
            flat = lambda ap: ap.rearrange("p h d -> p (h d)")

            def x_low(g):
                dve.wait_ge(s_xhi, g + 1)
                tt(x_lo[:], x_raw[:], raw(x_hi[:]), ALU.subtract).then_inc(s_xlo, 1)

            x_low(0)
            for i in range(WG):
                dve.wait_ge(s_whi, i + 1)
                if i < IT:
                    tt(wx_lo[:, i], staging[i % 2][:, 0:XC], raw(wx_hi[:, i]), ALU.subtract).then_inc(s_wlo, 1)
                else:
                    o = 2 * (i - IT)
                    tt(flat(wo_lo[:, o:o + 2]), staging[i % 2][:, 0:2 * DM], raw(flat(wo_hi[:, o:o + 2])),
                       ALU.subtract).then_inc(s_wlo, 1)
            dve.wait_ge(s_wlo, WG)
            dve.wait_ge(s_small, 64)
            dve.wait_ge(s_apos, 1)
            dve.wait_ge(s_tri, 2)
            dve.wait_ge(s_const, 6)
            x_low(1)

            def gate(g, first):
                dve.wait_ge(s_yT, g + 1)
                dve.wait_ge(s_lz, 16 * (g + 1))
                if not first:
                    dve.wait_ge(s_glo, g)
                tt(g_f[:].rearrange("p k n -> p (k n)"), pd[:, 0:2].rearrange("p q n -> p (q n)"),
                   z_raw[:].rearrange("p k n -> p (k n)"), ALU.mult).then_inc(s_g, 1)

            def residual_sum(g, first=False):
                if not first:
                    dve.wait_ge(s_out, 16 * g)
                dve.wait_ge(s_op, g + 1)
                dve.wait_ge(s_lr, 16 * (g + 1))
                tt(rr[:], po[:], res[:], ALU.add).then_inc(s_rr, 1)

            def statistics(g):
                dve.wait_ge(s_rr, g + 1)
                layer_norm_stats(nc, dve, rr[:], stats[:], mv[:], s_bn, s_mv, g + 1, s_tri)

            def normalize(g):
                dve.wait_ge(s_rstd, g + 1)
                ts(rr[:], rr[:], mv[:, 0:1], rstd[:], ALU.subtract, ALU.mult).then_inc(s_x1, 1)
                dve.wait_ge(s_x1, g + 1)

            def step(g, first, second, left):
                chain.round(g)
                if not first:
                    gate(g - 1, second)
                dve.wait_ge(s_p3, g + 1)
                tt(cb_m[:], CB, tri[:], ALU.mult).then_inc(s_cbm, 1)
                chain.link(tt(v[:], DTP, dtb[:], ALU.add))
                chain.link(ts(na[:], v[:], -1.0, None, ALU.mult))
                tt(na[:], na[:], v[:], ALU.min).then_inc(s_na, 1)
                dve.wait_ge(s_u, g + 1)
                chain.link(ts(s1[:], u[:], 2.0, None, ALU.add))
                chain.link(nc.vector.reciprocal(s1[:], s1[:]))
                chain.link(tt(s1[:], u[:], s1[:], ALU.mult))
                chain.link(tt(q[:], s1[:], s1[:], ALU.mult))
                chain.link(ts(s2[:], q[:], 1.0 / 13, None, ALU.mult))
                for n in (11, 9, 7, 5, 3):
                    chain.link(stt(out=s2[:], in0=s2[:], scalar=1.0 / n, in1=q[:], op0=ALU.add, op1=ALU.mult))
                chain.link(stt(out=s2[:], in0=s2[:], scalar=1.0, in1=s1[:], op0=ALU.add, op1=ALU.mult))
                chain.link(ts(v[:], v[:], 0.0, None, ALU.max))
                stt(out=dt[:], in0=s2[:], scalar=2.0, in1=v[:], op0=ALU.mult, op1=ALU.add).then_inc(s_dt, 1)
                dve.wait_ge(s_dt, g + 1)
                stt(out=a[:], in0=dt[:], scalar=-1.0, in1=a_pos[:], op0=ALU.mult, op1=ALU.mult).then_inc(s_a, 1)
                dve.wait_ge(s_a, g + 1)
                chain.link(nc.vector.tensor_copy(a_hi[:], a[:]))
                tt(a_lo[:], a[:], raw(a_hi[:]), ALU.subtract).then_inc(s_al, 1)
                dve.wait_ge(s_al, g + 1)
                half = NH // 2
                tt(r_lo[:, half:NH], tri[:].unsqueeze(1).broadcast_to([P, half, P]), heads(a_lo[:, half:NH], P),
                   ALU.mult)
                tt(r_hi[:], tri[:].unsqueeze(1).broadcast_to([P, NH, P]), heads(raw(a_hi[:]), P),
                   ALU.mult).then_inc(s_r, 1)
                dve.wait_ge(s_xc, 2 * g + 2)
                tt(xs[:], xf[:], heads(dt[:], HD), ALU.mult).then_inc(s_xs, 1)
                dve.wait_ge(s_ed, g + 1)
                ts(ek[:], ed[:, 2], keep[:, bass.ds(g, 1)], None, ALU.mult).then_inc(s_ek, 1)
                dve.wait_ge(s_dec, g + 1)
                tt(mix[:], decay[:], cb_m[:].unsqueeze(1).broadcast_to([P, NH, P]), ALU.mult).then_inc(s_mix, 1)
                if left == 2:
                    x_low(g + 2)
                if not first:
                    residual_sum(g - 1, second)
                dve.wait_ge(s_st, g + 1)
                dve.wait_ge(s_sd, g + 1)
                for i, bank in enumerate((pa, pb)):
                    part = flat(state[:, i * half:(i + 1) * half])
                    stt(out=part, in0=bank[:], scalar=keep[:, bass.ds(g, 1)], in1=part,
                        op0=ALU.mult, op1=ALU.add).then_inc(s_sa, 1)
                if not first:
                    statistics(g - 1)
                dve.wait_ge(s_yoff, g + 1)
                chain.link(tt(y[:], pd[:, 0:2].rearrange("p q (h d) -> p (q h) d", d=HD), heads(ed[:, 0], HD), ALU.mult))
                if not first:
                    normalize(g - 1)
                dve.wait_ge(s_xd, g + 1)
                tt(flat(y[:]), flat(y[:]), flat(xd[:]), ALU.add).then_inc(s_yx, 1)
                dve.wait_ge(s_yx, g + 1)
                dve.wait_ge(s_ydiag, g + 1)
                tt(flat(y[:]), flat(y[:]), pd[:, 2:4].rearrange("p q n -> p (q n)"), ALU.add).then_inc(s_y, 1)
                dve.wait_ge(s_sa, 2 * g + 2)
                chain.close()
            chunks(dve, step)
            chain.round(NCH)
            gate(NCH - 1, False)
            residual_sum(NCH - 1)
            statistics(NCH - 1)
            normalize(NCH - 1)


def inverse_deviations(nc, pool, mv, rstd, minus_half, s_eps, s_rstd, n):
    nc.gpsimd.tensor_scalar(rstd, mv[:, :, 1], EPS, None, ALU.add).then_inc(s_eps, 1)
    pool.wait_ge(s_eps, n)
    nc.gpsimd.tensor_tensor(rstd, rstd, minus_half, ALU.pow).then_inc(s_rstd, 1)


def ffn_phase(nc, t, acc, gated):
    with ExitStack() as ctx:
        k = Kit(nc, ctx, "moe" if gated else "ffn")
        TAG = "e_" if gated else "f_"
        UNITS = 8 if gated else 4
        NE = 8 if gated else 16
        NU = 2 if gated else 1
        F = 4
        RING = 4 // NU
        R = 64
        LORA = 2
        GOLD_C, GOLD_LO, GOLD_HI = 0.36787944117144233, 0.5 - 0.28768207245178085, 0.5

        xc_hi, xc_lo = (k.sb(n, [P, KT, TOK], F32R) for n in ("xc_hi", "xc_lo"))
        up_raw = k.sb("up_raw", [P, NU, F, KT, P])
        dn_raw = k.sb("dn_raw", [P, F, DM])
        up_hi, up_lo = (k.sb(n, [P, NU, F, KT, P], F32R) for n in ("up_hi", "up_lo"))
        dn_hi, dn_lo = (k.sb(n, [P, F, DM], F32R) for n in ("dn_hi", "dn_lo"))
        h_f = k.sb("h_f", [P, 2, SEQ])
        act_f = k.sb("act_f", [P, 2, SEQ]) if gated else None
        h_hi, h_lo = (k.sb(n, [P, F, SEQ], F32R) for n in ("h_hi", "h_lo"))
        wts = k.sb("wts", [P, NCH, NE])
        rw_raw = k.sb("rw_raw", [P, KT, NE])
        rw_hi, rw_lo = (k.sb(n, [P, KT, NE], F32R) for n in ("rw_hi", "rw_lo"))
        rb = k.sb("rb", [P, NE if not gated else 1])
        lower = k.sb("lower", [P, NE, NE])
        GRP = CPB
        lg, pr, sel, gold = (k.sb(n, [P, GRP, NE]) for n in ("lg", "pr", "sel", "gold"))
        sum1, sum2 = k.sb("sum1", [P, GRP]), k.sb("sum2", [P, GRP])
        cmp1, cmp2 = (k.sb(n, [P, GRP, NE, NE]) for n in ("cmp1", "cmp2"))
        ident = k.sb("ident", [P, P])
        minus_half = k.sb("minus_half", [P, CPB])
        stats, mv, rstd = k.sb("stats", [P, CPB, 6]), k.sb("mv", [P, CPB, 2]), k.sb("rstd", [P, CPB])
        if gated:
            la_up, lb_up = k.sb("la_up", [2 * R, DM]), k.sb("lb_up", [2 * R, DM])
            la_dn, lb_dn = k.sb("la_dn", [R, DM]), k.sb("lb_dn", [R, DM])
        pu, pd = k.ps("pu", [P, 4, 512]), k.ps("pd", [P, 4, 512])
        logT = dn_raw[0:NE]
        ORDER = ((0, 2, 1), (1, 0, 2), (3, 3, NE - 3))

        s_x = [k.sem(f"x_loaded{b}") for b in range(NB)]
        s_small = k.sem("small_loaded")
        s_lora = k.sem("lora_loaded")
        s_lu, s_ld = k.sem("up_loaded"), k.sem("down_loaded")
        s_ident, s_mem = k.sem("ident_ready"), k.sem("constants_ready")
        s_xT, s_xhi, s_xlo = k.sem("x_transposed"), k.sem("x_hi_ready"), k.sem("x_lo_ready")
        s_rwhi, s_rwlo = k.sem("router_hi_ready"), k.sem("router_lo_ready")
        s_lg, s_lgc = k.sem("logits_summed"), k.sem("logits_copied")
        s_lgT, s_wts = k.sem("logits_turned"), k.sem("logits_on_tokens")
        s_z, s_e = k.sem("router_to_act"), k.sem("router_from_act")
        s_uhi, s_ulo = k.sem("up_hi_ready"), k.sem("up_lo_ready")
        s_dhi, s_dlo = k.sem("down_hi_ready"), k.sem("down_lo_ready")
        s_delta, s_merged = k.sem("lora_delta_summed"), k.sem("lora_merged")
        s_up = k.sem("hidden_summed")
        s_act, s_hf = k.sem("silu_ready"), k.sem("hidden_ready")
        s_hhi, s_hlo = k.sem("hidden_hi_ready"), k.sem("hidden_lo_ready")
        s_dn, s_acc = k.sem("down_summed"), k.sem("down_added")
        s_bn, s_mv, s_eps, s_rstd = (k.sem(n) for n in ("bn_stats_ready", "mv_ready", "eps_added", "rstd_ready"))
        s_norm, s_out = k.sem("normalized"), k.sem("stored")
        c_dve = k.sem("dve_router_steps")
        block = k.block()

        @block.sync
        def _(sp):
            def load_x(b):
                if not gated:
                    sp.dma_start(acc[:, b * CPB:(b + 1) * CPB],
                                 t["x1"][b * SEQ:(b + 1) * SEQ, :].rearrange("(c p) d -> p c d", p=P)).then_inc(s_x[b], 16)

            def lora(e):
                for dst, n in ((la_up, "la_up"), (lb_up, "lb_up"), (la_dn, "la_dn"), (lb_dn, "lb_dn")):
                    sp.dma_start(dst[:], t[n][e]).then_inc(s_lora, 16)

            load_x(0)
            sp.dma_start(rw_raw[:], t[TAG + "router"]).then_inc(s_small, 16)
            sp.dma_start(rb[:], t[TAG + "rb"]).then_inc(s_small, 16)
            load_x(1)
            load_x(2)
            sp.dma_start(up_raw[:], t[TAG + "up"][0]).then_inc(s_lu, 16)
            load_x(3)
            if gated:
                lora(0)
            sp.wait_ge(s_wts, 1)
            sp.dma_start(dn_raw[:], t[TAG + "dn"][0]).then_inc(s_ld, 16)

            def unit(u):
                sp.wait_ge(s_small, 32)
                sp.wait_ge(s_ulo, NU * F * u + NU * F)
                sp.dma_start(up_raw[:], t[TAG + "up"][bass.ds(u + 1, 1)].rearrange("o p n f k c -> (o p) n f k c")).then_inc(s_lu, 16)
                sp.wait_ge(s_small, 32)
                sp.wait_ge(s_dlo, F * u + F)
                sp.dma_start(dn_raw[:], t[TAG + "dn"][bass.ds(u + 1, 1)].rearrange("o p f d -> (o p) f d")).then_inc(s_ld, 16)
            unit(0)
            if gated:
                sp.wait_ge(s_delta, 12)
                lora(1)
            with sp.Fori(1, UNITS - 1) as u:
                unit(u)
            if gated:
                for ch in range(NCH):
                    sp.wait_ge(s_norm, ch + 1)
                    sp.dma_start(t["out"][ch // CPB, bass.ts(ch % CPB, P)], acc[:, ch]).then_inc(s_out, 16)
                sp.wait_ge(s_out, 16 * NCH)

        @block.gpsimd
        def _(pool):
            make_identity(nc, pool, ident[:], s_ident)
            nc.gpsimd.memset(minus_half[:], -0.5).then_inc(s_mem, 1)
            nc.gpsimd.memset(lower[:], 1.0).then_inc(s_mem, 1)
            pool.wait_ge(s_mem, 2)
            nc.gpsimd.affine_select(out=lower[:], in_=lower[:], compare_op=ALU.is_ge, fill=0.0, base=-1,
                                    pattern=[[1, NE], [-1, NE]], channel_multiplier=0).then_inc(s_mem, 1)

            def unit(u, first, last, second=False):
                for tt in range(NB):
                    for f in range(F):
                        m = F * NB * u + F * tt + f
                        pool.wait_ge(s_hhi, m + 1)
                        nc.gpsimd.tensor_tensor(h_lo[:, f], h_f[:, f % 2], raw(h_hi[:, f]),
                                                ALU.subtract).then_inc(s_hlo, 1)
                        if last and tt >= 2 and f == 1:
                            deviations(tt - 1)

            def deviations(n):
                pool.wait_ge(s_mv, CPB * n)
                inverse_deviations(nc, pool, mv[:], rstd[:], minus_half[:], s_eps, s_rstd, n)

            unit(0, True, False)
            unit(1, False, False, True)
            with pool.Fori(2, UNITS - 1) as u:
                unit(u, False, False)
            unit(UNITS - 1, False, True)
            deviations(NB - 1)
            deviations(NB)

        @block.scalar
        def _(act):
            act.wait_ge(s_small, 32)
            nc.scalar.activation(rw_hi[:], rw_raw[:], ACT.Copy).then_inc(s_rwhi, 1)

            def turned_logits(b):
                act.wait_ge(s_lg, b + 1)
                nc.scalar.activation(logT[:, b], pu[0:NE, b], ACT.Copy).then_inc(s_lgT, 1)

            for b in range(NB):
                for kt in range(KT):
                    act.wait_ge(s_xT, b * KT + kt + 1)
                    nc.scalar.activation(xc_hi[:, kt, bass.ts(b, SEQ)], pd[:, kt], ACT.Copy).then_inc(s_xhi, 1)
                if b:
                    turned_logits(b - 1)
            turned_logits(NB - 1)

            def up_high(u, f):
                act.wait_ge(s_lu, 16 * u + 16)
                for i in range(NU):
                    nc.scalar.activation(up_hi[:, i, f], up_raw[:, i, f], ACT.Copy).then_inc(s_uhi, 1)

            for f in range(F):
                up_high(0, f)

            def unit(u, first, last, second=False):
                for tt in range(NB):
                    for f in range(F):
                        m = F * NB * u + F * tt + f
                        act.wait_ge(s_up, m + 1)
                        if gated:
                            if not (first and m < 2):
                                act.wait_ge(s_hf, m - 1)
                            nc.scalar.activation(act_f[:, f % 2], pu[:, (f % RING) * NU], ACT.Silu).then_inc(s_act, 1)
                        else:
                            if not (first and m < 2):
                                act.wait_ge(s_hlo, m - 1)
                            nc.scalar.activation(h_f[:, f % 2], pu[:, f], ACT.Gelu).then_inc(s_hf, 1)
                        if tt == NB - 1 and not last:
                            if gated and (first or second):
                                act.wait_ge(s_merged, 12 * u + 8)
                            up_high(u + 1, f)
                        act.wait_ge(s_hf, m + 1)
                        if not (first and tt == 0):
                            act.wait_ge(s_dn, F * (m - F) + F)
                        nc.scalar.activation(h_hi[:, f], h_f[:, f % 2], ACT.Copy).then_inc(s_hhi, 1)
                        if tt == 0:
                            act.wait_ge(s_ld, 16 * u + 16)
                            if gated and second:
                                act.wait_ge(s_merged, 12)
                            elif gated and not first:
                                act.wait_ge(s_merged, 24)
                            nc.scalar.activation(dn_hi[:, f], dn_raw[:, f], ACT.Copy).then_inc(s_dhi, 1)
                        if first:
                            router_functions(tt, f)

            def router_functions(n, part):
                if not gated and part == 0:
                    act.wait_ge(s_z, n + 1)
                    nc.scalar.activation(pr[:], lg[:], ACT.Exp).then_inc(s_e, 1)
                if gated and part == 0:
                    act.wait_ge(s_z, 2 * n + 1)
                    nc.scalar.activation(pr[:], lg[:], ACT.Sigmoid).then_inc(s_e, 1)
                if gated and part == 1:
                    act.wait_ge(s_z, 2 * n + 2)
                    nc.scalar.activation(sel[:], lg[:], ACT.Exp, scale=-1 / 0.1).then_inc(s_e, 1)
                    nc.scalar.activation(pr[:], lg[:], ACT.Exp, scale=-1 / 0.3).then_inc(s_e, 1)

            unit(0, True, False)
            unit(1, False, False, True)
            with act.Fori(2, UNITS - 1) as u:
                unit(u, False, False)
            unit(UNITS - 1, False, True)

        @block.tensor
        def _(pe):
            pe.wait_ge(s_ident, 2)

            def logits(b):
                pe.wait_ge(s_rwlo, 1)
                pe.wait_ge(s_xlo, b * KT + KT)
                for kt in range(KT):
                    x = bass.ts(b, SEQ)
                    ins = product(pe, pu[0:NE, b], (rw_hi[:, kt], rw_lo[:, kt]),
                                  (xc_hi[:, kt, x], xc_lo[:, kt, x]), kt == 0, kt == KT - 1)
                ins.then_inc(s_lg, 1)

            for b in range(NB):
                if not gated:
                    pe.wait_ge(s_x[b], 16)
                for kt in range(KT):
                    if b:
                        pe.wait_ge(s_xlo, b * KT + kt - KT + 1)
                    for c in range(CPB):
                        ins = pe.transpose(pd[:, kt, bass.ts(c, P)], acc[:, b * CPB + c, bass.ts(kt, P)], ident[:])
                    ins.then_inc(s_xT, 1)
                if b:
                    logits(b - 1)
            logits(NB - 1)
            pe.wait_ge(s_lgT, NB)
            for g in range(NCH):
                ins = pe.transpose(pd[:, 0, bass.ts(g, NE)], logT[:, g // CPB, bass.ts(g % CPB, P)],
                                   ident[0:NE, 0:NE])
            ins.then_inc(s_wts, 1)

            def merge(e, i, before):
                if i == 0:
                    pe.wait_ge(s_lora, 64 * e + 64)
                    pe.wait_ge(s_lgc, 1)
                if before:
                    pe.wait_ge(s_acc, before)
                if i < 8:
                    rows = slice(R * (i // 4), R * (i // 4) + R)
                    a, b = la_up[rows, bass.ts(i % 4, P)], lb_up[rows, :]
                else:
                    a, b = la_dn[:, bass.ts(i - 8, P)], lb_dn[:]
                pe.matmul(pd[:, 0], a, b, start=True, stop=True).then_inc(s_delta, 1)

            def down(m, f, tt, u, start):
                pe.wait_ge(s_hlo, m + 1)
                pe.wait_ge(s_dlo, F * u + f + 1)
                for c in range(CPB):
                    if not start:
                        pe.wait_ge(s_acc, CPB * (m - 1) + c + 1)
                    ins = product(pe, pd[:, c], (h_hi[:, f, bass.ts(c, P)], h_lo[:, f, bass.ts(c, P)]),
                                  (dn_hi[:, f], dn_lo[:, f]))
                    ins.then_inc(s_dn, 1)

            def unit(u, first, last, second=False):
                for tt in range(NB):
                    for f in range(F):
                        m = F * NB * u + F * tt + f
                        if gated and (first or second) and tt:
                            merge(u, F * (tt - 1) + f, max(0, CPB * (m - F - 1) + 1))
                        if tt == 0:
                            pe.wait_ge(s_ulo, NU * F * u + NU * f + NU)
                        if not (first and m < RING):
                            pe.wait_ge(s_hf, m - RING + 1)
                        for i in range(NU):
                            for kt in range(KT):
                                x = bass.ts(tt, SEQ)
                                ins = product(pe, pu[:, (f % RING) * NU + i], (up_hi[:, i, f, kt], up_lo[:, i, f, kt]),
                                              (xc_hi[:, kt, x], xc_lo[:, kt, x]), kt == 0, kt == KT - 1)
                        ins.then_inc(s_up, 1)
                        if gated and (first or second) and tt:
                            pe.wait_ge(s_merged, 12 * u + F * (tt - 1) + f + 1)
                        if not (first and tt == 0):
                            down(m - F, f, (tt - 1) % NB, u - 1 if tt == 0 else u, first and m == F)

            unit(0, True, False)
            unit(1, False, False, True)
            with pe.Fori(2, UNITS - 1) as u:
                unit(u, False, False)
            unit(UNITS - 1, False, True)
            for f in range(F):
                down(F * NB * UNITS - F + f, f, NB - 1, UNITS - 1, False)

        @block.vector
        def _(dve):
            chain = Chain(dve, c_dve, 0)
            link = chain.link
            tt_, stt, ts = nc.vector.tensor_tensor, nc.vector.scalar_tensor_tensor, nc.vector.tensor_scalar
            red = nc.vector.tensor_reduce
            over = lambda ap, n: ap.unsqueeze(2).broadcast_to([P, ap.shape[1], n])

            for b in range(NB):
                for kt in range(KT):
                    dve.wait_ge(s_xhi, b * KT + kt + 1)
                    x = bass.ts(b, SEQ)
                    tt_(xc_lo[:, kt, x], pd[:, kt], raw(xc_hi[:, kt, x]), ALU.subtract).then_inc(s_xlo, 1)
                if b == 0:
                    dve.wait_ge(s_rwhi, 1)
                    tt_(rw_lo[:], rw_raw[:], raw(rw_hi[:]), ALU.subtract).then_inc(s_rwlo, 1)

            def merge(e, i):
                dve.wait_ge(s_delta, 12 * e + i + 1)
                if i < 8:
                    dve.wait_ge(s_lu, 16 * e + 32)
                    w, d = up_raw[:, i // 4, :, i % 4], pd[:, 0].rearrange("p (f c) -> p f c", c=P)
                else:
                    dve.wait_ge(s_ld, 16 * e + 32)
                    w, d = dn_raw[:, i - 8], pd[:, 0]
                tt_(w, d, w, ALU.add).then_inc(s_merged, 1)

            def up_low(u, f):
                for i in range(NU):
                    dve.wait_ge(s_uhi, NU * F * u + NU * f + i + 1)
                    tt_(up_lo[:, i, f], up_raw[:, i, f], raw(up_hi[:, i, f]), ALU.subtract).then_inc(s_ulo, 1)

            for f in range(F):
                up_low(0, f)
            dve.wait_ge(s_wts, 1)
            nc.vector.tensor_copy(wts[:].rearrange("p c e -> p (c e)"), pd[:, 0, 0:NCH * NE]).then_inc(s_lgc, 1)
            dve.wait_ge(s_lgc, 1)

            def ranks(p, part):
                pj = p.unsqueeze(2).broadcast_to([P, GRP, NE, NE])
                pi = p.unsqueeze(3).broadcast_to([P, GRP, NE, NE])
                if part == 0:
                    link(tt_(cmp1[:], pj, pi, ALU.is_gt))
                    link(tt_(cmp2[:], pj, pi, ALU.is_equal))
                else:
                    link(tt_(cmp2[:], cmp2[:], lower[:].unsqueeze(1).broadcast_to([P, GRP, NE, NE]), ALU.mult))
                    link(tt_(cmp1[:], cmp1[:], cmp2[:], ALU.add))

            def router_blocks(n, part):
                w = wts[:, n * GRP:(n + 1) * GRP]
                if part == 0:
                    link(tt_(w, w, rb[:].unsqueeze(1).broadcast_to([P, GRP, NE]), ALU.add))
                    link(red(sum1[:], w, AX_X, ALU.max))
                    tt_(lg[:], w, over(sum1[:], NE), ALU.subtract).then_inc(s_z, 1)
                if part == 1:
                    dve.wait_ge(s_e, n + 1)
                    link(red(sum1[:], pr[:], AX_X, ALU.add))
                    link(nc.vector.reciprocal(sum1[:], sum1[:]))
                    link(tt_(pr[:], pr[:], over(sum1[:], NE), ALU.mult))
                    ranks(pr[:], 0)
                if part == 2:
                    ranks(pr[:], 1)
                if part == 3:
                    link(red(sel[:], cmp1[:], AX_X, ALU.add))
                    link(ts(w, sel[:], 3.5, None, ALU.is_lt))

            def router_golden(n, part):
                w = wts[:, n * GRP:(n + 1) * GRP]
                if part == 0:
                    if n == 0:
                        link(nc.vector.reciprocal(rb[:], rb[:]))
                    ts(lg[:], w, rb[:], None, ALU.mult).then_inc(s_z, 1)
                if part == 1:
                    dve.wait_ge(s_e, 3 * n + 1)
                    link(ts(gold[:], pr[:], GOLD_LO, None, ALU.is_ge))
                    link(ts(cmp1[:, :, 0], pr[:], GOLD_HI, None, ALU.is_le))
                    link(tt_(gold[:], gold[:], cmp1[:, :, 0], ALU.mult))
                    link(ts(lg[:], pr[:], GOLD_C, None, ALU.subtract))
                    link(ts(cmp1[:, :, 0], lg[:], -1.0, None, ALU.mult))
                    tt_(lg[:], lg[:], cmp1[:, :, 0], ALU.max).then_inc(s_z, 1)
                if part == 2:
                    dve.wait_ge(s_e, 3 * n + 2)
                    link(tt_(gold[:], gold[:], sel[:], ALU.mult))
                    dve.wait_ge(s_e, 3 * n + 3)
                    ranks(pr[:], 0)
                    ranks(pr[:], 1)
                if part == 3:
                    link(red(sel[:], cmp1[:], AX_X, ALU.add))
                    link(ts(sel[:], sel[:], 1.5, None, ALU.is_lt))
                    link(tt_(sel[:], sel[:], pr[:], ALU.mult))
                    inverse_of_sum(sel[:])
                    link(tt_(sel[:], sel[:], over(sum1[:], NE), ALU.mult))
                    link(red(sum1[:], gold[:], AX_X, ALU.add))
                    link(ts(sum2[:], sum1[:], 1e-8, None, ALU.is_lt))
                    link(tt_(sel[:], sel[:], over(sum2[:], NE), ALU.mult))
                    link(ts(sum2[:], sum2[:], -1.0, 1.0, ALU.mult, ALU.add))
                    link(tt_(gold[:], gold[:], over(sum2[:], NE), ALU.mult))
                    link(tt_(gold[:], gold[:], sel[:], ALU.add))
                    inverse_of_sum(gold[:])
                    for unit_, expert, size in ORDER:
                        link(tt_(w[:, :, unit_:unit_ + size], gold[:, :, expert:expert + size],
                                 over(sum1[:], size), ALU.mult))

            def inverse_of_sum(v):
                link(red(sum1[:], v, AX_X, ALU.add))
                link(ts(sum1[:], sum1[:], 1e-8, None, ALU.max))
                link(nc.vector.reciprocal(sum1[:], sum1[:]))

            def add_down(m, f, tt, u):
                for c in range(CPB):
                    n = CPB * m + c
                    ch = tt * CPB + c
                    w = wts[:, ch, bass.ds(u, 1)] if gated else wts[:, ch, bass.ds(F * u + f, 1)]
                    dve.wait_ge(s_dn, n + 1)
                    if not (isinstance(m, int) and m == 0):
                        dve.wait_ge(s_acc, n - CPB + 1)
                    stt(out=acc[:, ch], in0=pd[:, c], scalar=w, in1=acc[:, ch],
                        op0=ALU.mult, op1=ALU.add).then_inc(s_acc, 1)

            def finish(n, part):
                if part == 0:
                    dve.wait_ge(s_acc, CPB * (F * NB * (UNITS - 1) + F * n + F))
                    if n:
                        dve.wait_ge(s_norm, CPB * n)
                    for c in range(CPB):
                        nc.vector.bn_stats(stats[:, c], acc[:, n * CPB + c]).then_inc(s_bn, 1)
                if part == 1:
                    for c in range(CPB):
                        dve.wait_ge(s_bn, CPB * n + c + 1)
                        nc.vector.bn_aggr(mv[:, c], stats[:, c]).then_inc(s_mv, 1)
                if part == 2:
                    dve.wait_ge(s_rstd, n + 1)
                if part >= 2:
                    for c in (2 * part - 4, 2 * part - 3):
                        ch = n * CPB + c
                        ts(acc[:, ch], acc[:, ch], mv[:, c, 0:1], rstd[:, c:c + 1], ALU.subtract,
                           ALU.mult).then_inc(s_norm, 1)

            def unit(u, first, last, second=False):
                for tt in range(NB):
                    for f in range(F):
                        m = F * NB * u + F * tt + f
                        if gated and (first or second) and tt:
                            merge(u, F * (tt - 1) + f)
                        if gated:
                            dve.wait_ge(s_act, m + 1)
                            if not (first and m < 2):
                                dve.wait_ge(s_hlo, m - 1)
                            tt_(h_f[:, f % 2], pu[:, (f % RING) * NU + 1], act_f[:, f % 2], ALU.mult).then_inc(s_hf, 1)
                        if tt == NB - 1 and not last:
                            up_low(u + 1, f)
                        if not (first and tt == 0):
                            add_down(m - F, f, (tt - 1) % NB, u - 1 if tt == 0 else u)
                        if tt == 0:
                            dve.wait_ge(s_dhi, F * u + f + 1)
                            tt_(dn_lo[:, f], dn_raw[:, f], raw(dn_hi[:, f]), ALU.subtract).then_inc(s_dlo, 1)
                        if first and gated:
                            router_golden(tt, f)
                        elif first:
                            router_blocks(tt, f)
                        if last and tt >= 2:
                            finish(tt - 2, f)

            dve.wait_ge(s_small, 32)
            dve.wait_ge(s_mem, 3)
            unit(0, True, False)
            unit(1, False, False, True)
            with dve.Fori(2, UNITS - 1) as u:
                unit(u, False, False)
            unit(UNITS - 1, False, True)
            for f in range(F):
                add_down(F * NB * UNITS - F + f, f, NB - 1, UNITS - 1)
                finish(NB - 2, f)
            for part in range(4):
                finish(NB - 1, part)
            dve.wait_ge(s_norm, NCH)


def attn_phase(nc, t, acc):
    with ExitStack() as ctx:
        k = Kit(nc, ctx, "attn")
        AH, AD = 16, 32
        G = DM // P
        HG = AH // G
        VW, OW = P + 1, P + HG
        AEPS = 1e-15
        w_raw = k.sb("w_raw", [P, 2, 4 * DM])
        wq_hi, wq_lo = (k.sb(n, [P, KT, 3 * DM], F32R) for n in ("wq_hi", "wq_lo"))
        wp_hi, wp_lo = (k.sb(n, [P, KT, DM], F32R) for n in ("wp_hi", "wp_lo"))
        bias = k.sb("bias", [P, DM])
        xt = k.sb("xt", [P, DM])
        x_hi, x_lo = (k.sb(n, [P, KT, P], F32R) for n in ("x_hi", "x_lo"))
        q, kk = k.sb("q", [P, DM]), k.sb("k", [P, DM])
        vo = k.sb("vo", [P, G, VW])
        qT = k.sb("qT", [P, CPB, G, P])
        bd = k.sb("bd", [P, G, OW])
        same = k.sb("same", [P, HG, AD])
        den = k.sb("den", [P, G, HG])
        o = k.sb("o", [P, G, HG, AD])
        o_hi, o_lo = (k.sb(n, [P, KT, P], F32R) for n in ("o_hi", "o_lo"))
        rr = k.sb("rr", [P, DM])
        ident = k.sb("ident", [P, P])
        stats, mv = k.sb("stats", [P, 6]), k.sb("mv", [P, 2])
        rstd, const = k.sb("rstd", [P, 1]), k.sb("const", [P, 2])
        pt, pq, pk, pv = (k.ps(n, [P, 512]) for n in ("pt", "pq", "pk", "pv"))
        pvk, po = k.ps("pvk", [P, 2, 512]), k.ps("po", [P, 2, 512])

        s_small = k.sem("bias_loaded")
        s_w = [k.sem(f"w_loaded{i}") for i in range(2)]
        s_whi, s_wlo = k.sem("w_hi_ready"), k.sem("w_lo_ready")
        s_ident, s_mem = k.sem("ident_ready"), k.sem("constants_ready")
        s_xt, s_xT, s_xhi, s_xlo = (k.sem(n) for n in ("x_copied", "x_transposed", "x_hi_ready", "x_lo_ready"))
        s_q, s_k, s_v = k.sem("q_summed"), k.sem("k_summed"), k.sem("v_summed")
        s_qr, s_kr, s_vr = k.sem("q_ready"), k.sem("k_ready"), k.sem("v_ready")
        s_qT, s_qTc = k.sem("q_transposed"), k.sem("q_turned_ready")
        s_vk, s_bd = k.sem("vk_summed"), k.sem("vk_ready")
        s_o, s_od = k.sem("out_summed"), k.sem("out_ready")
        s_oT, s_ohi, s_olo = k.sem("out_transposed"), k.sem("out_hi_ready"), k.sem("out_lo_ready")
        s_p, s_pa, s_rr = k.sem("projected"), k.sem("projection_taken"), k.sem("residual_added")
        s_bn, s_mv, s_eps, s_rstd, s_norm = (k.sem(n) for n in ("bn_stats_ready", "mv_ready", "eps_added",
                                                               "rstd_ready", "normalized"))
        c_dve = k.sem("dve_steps")
        block = k.block()
        WG = KT + 1

        def batches(eng, batch):
            batch(0, True)
            with eng.Fori(1, NB) as b:
                batch(b, False)

        @block.sync
        def _(sp):
            sp.dma_start(bias[:], t["proj_b"]).then_inc(s_small, 16)
            for i in range(WG):
                if i >= 2:
                    sp.wait_ge(s_wlo, i - 1)
                if i < KT:
                    sp.dma_start(w_raw[:, i % 2, 0:3 * DM], t["qkv_w"][i]).then_inc(s_w[i % 2], 16)
                else:
                    sp.dma_start(w_raw[:, i % 2], t["proj_w"].rearrange("p k n -> p (k n)")).then_inc(s_w[i % 2], 16)

        @block.gpsimd
        def _(pool):
            make_identity(nc, pool, ident[:], s_ident)
            nc.gpsimd.memset(const[:, 0:1], EPS).then_inc(s_mem, 1)
            nc.gpsimd.memset(const[:, 1:2], -0.5).then_inc(s_mem, 1)
            nc.gpsimd.memset(vo[:], 1.0).then_inc(s_mem, 1)
            nc.gpsimd.memset(same[:], 1.0).then_inc(s_mem, 1)
            pool.wait_ge(s_mem, 4)
            nc.gpsimd.affine_select(out=same[:], in_=same[:], compare_op=ALU.is_ge, fill=0.0, base=0,
                                    pattern=[[-AD, HG], [0, AD]], channel_multiplier=1).then_inc(s_mem, 1)
            pool.wait_ge(s_mem, 5)
            nc.gpsimd.affine_select(out=same[:], in_=same[:], compare_op=ALU.is_ge, fill=0.0, base=AD - 1,
                                    pattern=[[AD, HG], [0, AD]], channel_multiplier=-1).then_inc(s_mem, 1)

            def batch(b, first):
                for c in range(CPB):
                    inverse_deviation(nc, pool, mv[:], rstd[:], const[:], s_mv, s_eps, s_rstd, CPB * b + c + 1)
            batches(pool, batch)

        @block.scalar
        def _(act):
            def take_x(n, first):
                if not first:
                    act.wait_ge(s_xT, n)
                nc.scalar.activation(xt[:].unsqueeze(1), acc[:, bass.ds(n, 1)], ACT.Copy).then_inc(s_xt, 1)

            def batch(b, first):
                take_x(CPB * b, first)
                for c in range(CPB):
                    n = CPB * b + c
                    act.wait_ge(s_xT, n + 1)
                    if not (first and c == 0):
                        act.wait_ge(s_v, n)
                    nc.scalar.activation(x_hi[:].rearrange("p k n -> p (k n)"), pt[:], ACT.Copy).then_inc(s_xhi, 1)
                    if c < CPB - 1:
                        take_x(n + 1, False)
                    if first and c == 0:
                        weights()
                    act.wait_ge(s_q, n + 1)
                    if not (first and c == 0):
                        act.wait_ge(s_qT, n)
                    nc.scalar.activation(q[:], pq[:], ACT.Relu).then_inc(s_qr, 1)
                    act.wait_ge(s_k, n + 1)
                    if not (first and c == 0):
                        act.wait_ge(s_vk, n)
                    nc.scalar.activation(kk[:], pk[:], ACT.Relu).then_inc(s_kr, 1)
                    act.wait_ge(s_qT, n + 1)
                    if not first:
                        act.wait_ge(s_o, n - c)
                    nc.scalar.activation(qT[:, c].rearrange("p g n -> p (g n)"), po[:, 0], ACT.Copy).then_inc(s_qTc, 1)
                for c in range(CPB):
                    n = CPB * b + c
                    act.wait_ge(s_oT, n + 1)
                    if not (first and c == 0):
                        act.wait_ge(s_p, n)
                    nc.scalar.activation(o_hi[:].rearrange("p k n -> p (k n)"), pt[:], ACT.Copy).then_inc(s_ohi, 1)

            def weights():
                for i in range(WG):
                    act.wait_ge(s_w[i % 2], 16 * (i // 2 + 1))
                    if i < KT:
                        nc.scalar.activation(wq_hi[:, i], w_raw[:, i % 2, 0:3 * DM], ACT.Copy).then_inc(s_whi, 1)
                    else:
                        nc.scalar.activation(wp_hi[:].rearrange("p k n -> p (k n)"), w_raw[:, i % 2],
                                             ACT.Copy).then_inc(s_whi, 1)
            batches(act, batch)

        @block.tensor
        def _(pe):
            pe.wait_ge(s_ident, 2)
            pe.wait_ge(s_mem, 6)

            def turn_x(n, first):
                pe.wait_ge(s_xt, n + 1)
                if not first:
                    pe.wait_ge(s_xlo, n)
                for kt in range(KT):
                    ins = pe.transpose(pt[:, bass.ts(kt, P)], xt[:, bass.ts(kt, P)], ident[:])
                ins.then_inc(s_xT, 1)

            def sums(n):
                c = n[1]
                n = n[0]
                pe.wait_ge(s_qr, n + 1)
                if c:
                    pe.wait_ge(s_qTc, n)
                for g in range(G):
                    ins = pe.transpose(po[:, 0, bass.ts(g, P)], q[:, bass.ts(g, P)], ident[:])
                ins.then_inc(s_qT, 1)
                pe.wait_ge(s_kr, n + 1)
                pe.wait_ge(s_vr, n + 1)
                for g in range(G):
                    bank = pvk[:, g // 2, (g % 2) * 256:(g % 2) * 256 + VW]
                    ins = pe.matmul(bank, kk[:, bass.ts(g, P)], vo[:, g], start=(c == 0 and g % 2 == 0),
                                    stop=(c == CPB - 1), skip_group_check=True)
                ins.then_inc(s_vk, 1)

            def batch(b, first):
                if not first:
                    pe.wait_ge(s_olo, CPB * b)
                turn_x(CPB * b, first)
                for c in range(CPB):
                    n = CPB * b + c
                    pe.wait_ge(s_xlo, n + 1)
                    for i, (bank, sem, ready) in enumerate(((pq, s_q, s_qr), (pk, s_k, s_kr), (pv, s_v, s_vr))):
                        if not (first and c == 0):
                            pe.wait_ge(ready, n)
                            if c == 0 and i < 2:
                                pe.wait_ge(s_pa, n - i)
                        for kt in range(KT):
                            if first and c == 0 and i == 0:
                                pe.wait_ge(s_wlo, kt + 1)
                            ins = product(pe, bank[:], (x_hi[:, kt], x_lo[:, kt]),
                                          (wq_hi[:, kt, bass.ts(i, DM)], wq_lo[:, kt, bass.ts(i, DM)]),
                                          kt == 0, kt == KT - 1)
                        ins.then_inc(sem, 1)
                    if c < CPB - 1:
                        turn_x(n + 1, False)
                    if c == 0 and not first:
                        pe.wait_ge(s_bd, b)
                        pe.wait_ge(s_od, CPB * b)
                    sums((n, c))

                def attend(c):
                    n = CPB * b + c
                    if c:
                        pe.wait_ge(s_od, n)
                    for g in range(G):
                        ins = pe.matmul(po[:, g // 2, (g % 2) * 256:(g % 2) * 256 + OW], qT[:, c, g], bd[:, g],
                                        start=True, stop=True)
                    ins.then_inc(s_o, 1)

                pe.wait_ge(s_bd, b + 1)
                pe.wait_ge(s_qTc, CPB * b + CPB)
                attend(0)
                if first:
                    pe.wait_ge(s_wlo, WG)
                for c in range(CPB):
                    n = CPB * b + c
                    pe.wait_ge(s_od, n + 1)
                    if c:
                        pe.wait_ge(s_olo, n)
                    for kt in range(KT):
                        ins = pe.transpose(pt[:, bass.ts(kt, P)],
                                           o[:, kt].rearrange("p h d -> p (h d)"), ident[:])
                    ins.then_inc(s_oT, 1)
                    if c < CPB - 1:
                        attend(c + 1)
                    pe.wait_ge(s_olo, n + 1)
                    if c >= 2:
                        pe.wait_ge(s_pa, n - 1)
                    for kt in range(KT):
                        ins = product(pe, (pq, pk)[c % 2][:], (o_hi[:, kt], o_lo[:, kt]),
                                      (wp_hi[:, kt], wp_lo[:, kt]), kt == 0, kt == KT - 1)
                    ins.then_inc(s_p, 1)
            batches(pe, batch)

        @block.vector
        def _(dve):
            tt, ts = nc.vector.tensor_tensor, nc.vector.tensor_scalar
            chain = Chain(dve, c_dve, 2 * CPB)
            flat = lambda ap: ap.rearrange("p k n -> p (k n)")
            dve.wait_ge(s_mem, 6)
            dve.wait_ge(s_small, 16)

            def weights():
                for i in range(WG):
                    dve.wait_ge(s_whi, i + 1)
                    if i < KT:
                        tt(wq_lo[:, i], w_raw[:, i % 2, 0:3 * DM], raw(wq_hi[:, i]), ALU.subtract).then_inc(s_wlo, 1)
                    else:
                        tt(flat(wp_lo[:]), w_raw[:, i % 2], raw(flat(wp_hi[:])), ALU.subtract).then_inc(s_wlo, 1)

            def norm_in(c, n, first):
                dve.wait_ge(s_p, n + 1)
                if not (first and c == 0):
                    dve.wait_ge(s_norm, n)
                tt(rr[:], (pq, pk)[c % 2][:], bias[:], ALU.add).then_inc(s_pa, 1)
                dve.wait_ge(s_pa, n + 1)
                tt(rr[:].unsqueeze(1), rr[:].unsqueeze(1), acc[:, bass.ds(n, 1)], ALU.add).then_inc(s_rr, 1)
                dve.wait_ge(s_rr, n + 1)
                layer_norm_stats(nc, dve, rr[:], stats[:], mv[:], s_bn, s_mv, n + 1, s_small)

            def norm_out(n):
                dve.wait_ge(s_rstd, n + 1)
                ts(acc[:, bass.ds(n, 1)], rr[:].unsqueeze(1), mv[:, 0:1], rstd[:], ALU.subtract,
                   ALU.mult).then_inc(s_norm, 1)

            def batch(b, first):
                chain.round(b)
                for c in range(CPB):
                    n = CPB * b + c
                    dve.wait_ge(s_xhi, n + 1)
                    tt(flat(x_lo[:]), pt[:], raw(flat(x_hi[:])), ALU.subtract).then_inc(s_xlo, 1)
                    if first and c == 0:
                        weights()
                    dve.wait_ge(s_v, n + 1)
                    if not (first and c == 0):
                        dve.wait_ge(s_vk, n)
                    nc.vector.tensor_copy(vo[:, :, 0:P], pv[:].rearrange("p (g n) -> p g n", g=G)).then_inc(s_vr, 1)
                dve.wait_ge(s_vk, CPB * b + CPB)
                if not first:
                    dve.wait_ge(s_o, CPB * b)
                for i in range(2):
                    two = pvk[:, i].rearrange("p (g n) -> p g n", g=2)
                    for g in range(2):
                        sums = two[:, g, P:P + 1].broadcast_to([P, HG])
                        tt(bd[:, 2 * i + g, 0:P], two[:, g, 0:P], same[:].rearrange("p h d -> p (h d)"), ALU.mult)
                        ins = tt(bd[:, 2 * i + g, P:OW], sums, same[:, :, 0], ALU.mult)
                ins.then_inc(s_bd, 1)
                for c in range(CPB):
                    n = CPB * b + c
                    dve.wait_ge(s_o, n + 1)
                    outs = po[:].rearrange("p t (g n) -> p (t g) n", g=2)
                    chain.link(ts(den[:], outs[:, :, P:OW], AEPS, None, ALU.add))
                    chain.link(nc.vector.reciprocal(den[:], den[:]))
                    if not (first and c == 0):
                        dve.wait_ge(s_oT, n)
                    for g in range(G):
                        ins = tt(o[:, g], outs[:, g, 0:P].rearrange("p (h d) -> p h d", h=HG),
                                 den[:, g].unsqueeze(2).broadcast_to([P, HG, AD]), ALU.mult)
                    ins.then_inc(s_od, 1)
                    dve.wait_ge(s_ohi, n + 1)
                    tt(flat(o_lo[:]), pt[:], raw(flat(o_hi[:])), ALU.subtract).then_inc(s_olo, 1)
                    if c:
                        norm_in(c - 1, n - 1, first)
                        norm_out(n - 1)
                norm_in(CPB - 1, CPB * b + CPB - 1, False)
                norm_out(CPB * b + CPB - 1)
            batches(dve, batch)
            dve.wait_ge(s_norm, NCH)


def build(nc, t):
    in_proj(nc, t)
    ssd_phase(nc, t)
    with nc.sbuf_tensor("acc", [P, NCH, DM], F32) as acc:
        ffn_phase(nc, t, acc, gated=False)
        attn_phase(nc, t, acc)
        ffn_phase(nc, t, acc, gated=True)


def lay_out(inp):
    import numpy as np

    def cm(w):
        return w.T.reshape(w.shape[1] // P, P, w.shape[0]).transpose(1, 0, 2)

    def rows(v):
        return np.broadcast_to(v, (P, v.shape[0]))

    def up_tiles(w):
        u, n = w.shape[:2]
        return w.reshape(u, n, KT, P, 4, P).transpose(0, 3, 1, 4, 2, 5)

    def down_tiles(w):
        return w.reshape(w.shape[0], 4, P, DM).transpose(0, 2, 1, 3)

    a = {n: np.asarray(v) for n, v in inp.items()}
    w = a["L0_attn_in_proj_w"].reshape(2, IT, P, DM).transpose(1, 0, 2, 3).reshape(2 * DI, DM)
    order = [2, 0, 1] + list(range(3, 8))
    laid = {
        "x": a["L0_attn_x"],
        "x_rows": a["L0_attn_x"].reshape(TOK, DM),
        "in_w": cm(w).reshape(P, KT, 4, 4 * P).transpose(0, 2, 1, 3),
        "conv_w": a["L0_attn_conv_w"].reshape(IT, P, TAPS).transpose(1, 0, 2),
        "conv_b": a["L0_attn_conv_b"].reshape(IT, P).T,
        "x_w": cm(a["L0_attn_x_proj_w"]),
        "out_w": cm(a["L0_attn_out_proj_w"]).reshape(P, IT // 2, 2 * DM),
        "dtw": a["L0_attn_dt_proj_w"].T,
        "dtb": rows(a["L0_attn_dt_proj_b"]),
        "a_log": rows(a["L0_attn_A_log"]),
        "d_skip": rows(a["L0_attn_D"]),
        "f_router": cm(a["L0_ffn_Wr"]),
        "f_rb": rows(a["L0_ffn_br"]),
        "f_up": up_tiles(a["L0_ffn_W1"].T.reshape(DM, 4, 1, DM).transpose(1, 2, 0, 3)),
        "f_dn": down_tiles(a["L0_ffn_W2"].T.reshape(4, DM, DM)),
        "qkv_w": cm(a["L1_attn_w_qkv"]).transpose(1, 0, 2),
        "proj_w": cm(a["L1_attn_w_proj"]),
        "proj_b": rows(a["L1_attn_b_proj"]),
        "e_router": a["L1_ffn_Wr"].reshape(KT, P, 8).transpose(1, 0, 2),
        "e_rb": rows(a["L1_ffn_temperature"]),
        "e_up": up_tiles(np.stack([a["L1_ffn_Wg"], a["L1_ffn_Wu"]], 1))[order],
        "e_dn": down_tiles(a["L1_ffn_Wd"])[order],
        "la_up": np.stack([a["L1_ffn_Ga"], a["L1_ffn_Ua"]], 1).transpose(0, 1, 3, 2).reshape(2, P, DM),
        "lb_up": np.stack([a["L1_ffn_Gb"], a["L1_ffn_Ub"]], 1).reshape(2, P, DM),
        "la_dn": a["L1_ffn_Da"].transpose(0, 2, 1),
        "lb_dn": a["L1_ffn_Db"],
    }
    return {n: np.ascontiguousarray(v) for n, v in laid.items()}


def kernel(**inputs):
    import concourse.bacc as bacc
    from concourse.bass_utils import run_bass_kernel_spmd as run

    laid = lay_out(inputs)
    nc = bacc.Bacc("TRN2", target_bir_lowering=False, num_devices=1)
    t = {n: nc.dram_tensor(f"in_{n}", v.shape, F32, kind="ExternalInput").ap() for n, v in laid.items()}
    for n, shape in (("xb", (IT, P, TOK)), ("zs", (IT, P, TOK)), ("x1", (TOK, DM))):
        t[n] = nc.dram_tensor(n, shape, F32, kind="Internal").ap()
    t["out"] = nc.dram_tensor("out", (NB, SEQ, DM), F32, kind="ExternalOutput").ap()
    build(nc, t)
    r = run(nc, [{f"in_{n}": v for n, v in laid.items()}], core_ids=[0])
    return r.results[0]["out"]
```

```python
from contextlib import ExitStack

import concourse.bass as bass
from concourse import mybir

F32 = mybir.dt.float32
F32R = mybir.dt.float32r
ALU = mybir.AluOpType
ACT = mybir.ActivationFunctionType
AX_X = mybir.AxisListType.X

P = 128
NB, SEQ, DM = 4, 512, 512
TOK = NB * SEQ
NCH = TOK // P
CPB = SEQ // P
KT = DM // P
DI = 2 * DM
IT = DI // P
NH, HD = 16, 64
NS = 128
TAPS = 4
EPS = 1e-5
XC = DI + NH + 2 * NS
EARLY = 6


class Kit:

    def __init__(self, nc, ctx, tag):
        self.nc, self.ctx, self.tag, self.sems = nc, ctx, tag, []
        ctx.callback(self.close)

    def sb(self, name, shape, dt=F32):
        return self.ctx.enter_context(self.nc.sbuf_tensor(f"{self.tag}_{name}", shape, dt))

    def ps(self, name, shape):
        return self.ctx.enter_context(self.nc.psum_tensor(f"{self.tag}_{name}", shape, F32))

    def sem(self, name):
        self.sems.append(self.nc.alloc_semaphore(f"{self.tag}_{name}"))
        return self.sems[-1]

    def close(self):
        self.nc.clear_and_free_semaphores(self.sems)
        self.nc.all_engine_barrier()

    def block(self):
        return self.ctx.enter_context(self.nc.Block())


class Chain:

    def __init__(self, eng, sem, per):
        self.eng, self.sem, self.per, self.base, self.k = eng, sem, per, 0, 0

    def round(self, g):
        self.base, self.k = g * self.per, 0

    def link(self, ins):
        self.k += 1
        ins.then_inc(self.sem, 1)
        self.eng.wait_ge(self.sem, self.base + self.k)

    def close(self):
        assert self.k <= self.per, (self.k, self.per)
        if self.k < self.per:
            self.eng.sem_inc(self.sem, self.per - self.k)
            self.k = self.per


def raw(ap):
    return ap.bitcast(F32)


def product(pe, out, lhs, rhs, first=True, last=True):
    (lh, ll), (rh, rl) = lhs, rhs
    pe.matmul(out, lh, rh, start=first, stop=False)
    pe.matmul(out, lh, rl, start=False, stop=False)
    return pe.matmul(out, ll, rh, start=False, stop=last)


def in_proj(nc, t, pre, x_raw):
    with ExitStack() as ctx:
        k = Kit(nc, ctx, "in")
        MT = 2 * IT
        GRP = 4
        TPG = MT // GRP
        x_tok = pre[:].rearrange("p (b c d) -> p b c d", b=NB, c=CPB)
        x_hi, x_lo = k.sb("x_hi", [P, KT, TOK], F32R), k.sb("x_lo", [P, KT, TOK], F32R)
        w_raw = k.sb("w_raw", [P, 2, KT, TPG * P])
        w_hi, w_lo = (k.sb(n, [P, GRP, KT, TPG * P], F32R) for n in ("w_hi", "w_lo"))
        conv = k.sb("conv", [P, 2, SEQ])
        out = k.sb("out", [P, 4, SEQ])
        cw = k.sb("cw", [P, IT, TAPS])
        cb = k.sb("cb", [P, IT])
        ident = k.sb("ident", [P, P])
        tp = k.ps("tp", [P, 4, 512])
        acc = k.ps("acc", [P, 4, 512])

        s_x = [k.sem(f"x_loaded{b}") for b in range(NB)]
        s_w = [k.sem(f"w_loaded{g}") for g in range(2)]
        s_small = k.sem("conv_params_loaded")
        s_ident = k.sem("ident_ready")
        s_xT = k.sem("x_transposed")
        s_xhi, s_xlo = k.sem("x_hi_ready"), k.sem("x_lo_ready")
        s_whi, s_wlo = k.sem("w_hi_ready"), k.sem("w_lo_ready")
        s_xacc, s_zacc = k.sem("x_tile_summed"), k.sem("z_tile_summed")
        s_taps = k.sem("conv_taps_added")
        s_c = k.sem("conv_tile_started")
        s_xo, s_zo = k.sem("x_tile_out"), k.sem("z_tile_out")
        s_st = [k.sem(f"stored{i}") for i in range(4)]
        s_early = k.sem("next_phase_loaded")
        s_x0 = [k.sem(f"x_chunk_loaded{c}") for c in range(CPB)]
        block = k.block()

        @block.sync
        def _(sp):
            def load_x(b):
                sp.dma_start(x_tok[:, b], t["x"][b].rearrange("(c p) d -> p c d", p=P)).then_inc(s_x[b], 16)

            def load_w(g):
                if g >= 2:
                    sp.wait_ge(s_wlo, g - 1)
                sp.dma_start(w_raw[:, g % 2], t["in_w"][:, g]).then_inc(s_w[g % 2], 16)

            for c in range(CPB):
                sp.dma_start(x_tok[:, 0, c], t["x"][0, c * P:(c + 1) * P, :]).then_inc(s_x0[c], 16)
            load_w(0)
            sp.dma_start(cw[:], t["conv_w"]).then_inc(s_small, 16)
            sp.dma_start(cb[:], t["conv_b"]).then_inc(s_small, 16)
            load_w(1)
            for b in range(1, NB):
                load_x(b)
                if b + 1 < GRP:
                    load_w(b + 1)
            for i in range(4):
                sp.sem_inc(s_st[i], 16)

            def batch(b):
                for j in range(IT):
                    sp.wait_ge(s_xo, b * IT + j + 1 + 2)
                    sp.dma_start(t["xb"][j][:, bass.ts(b, SEQ)], out[:, 2 * j % 4]).then_inc(s_st[2 * j % 4], 16)
                    sp.wait_ge(s_zo, b * IT + j + 1 + 2)
                    sp.dma_start(t["zs"][j][:, bass.ts(b, SEQ)], out[:, (2 * j + 1) % 4]).then_inc(s_st[(2 * j + 1) % 4], 16)

            batch(0)
            sp.wait_ge(s_xT, NB * KT)
            sp.dma_start(pre[:, 0:EARLY * XC], t["x_w"][:, 0:EARLY].rearrange("p k n -> p (k n)")).then_inc(s_early, 16)
            for i in (0, 2):
                sp.wait_ge(s_st[i], 16 * (MT // 4 + 1))
            sp.dma_start(x_raw[:], t["xb"][:, :, 0:P].rearrange("j p n -> p j n")).then_inc(s_early, 16)
            with sp.Fori(1, NB) as b:
                batch(b)
            for i in range(4):
                sp.wait_ge(s_st[i], 16 * (NB * MT // 4 + 1))
            sp.wait_ge(s_early, 32)

        @block.gpsimd
        def _(pool):
            nc.gpsimd.memset(ident[:], 0.0).then_inc(s_ident, 1)
            pool.wait_ge(s_ident, 1)
            nc.gpsimd.affine_select(out=ident[:], in_=ident[:], compare_op=ALU.not_equal, fill=1.0, base=0,
                                    pattern=[[-1, P]], channel_multiplier=1).then_inc(s_ident, 1)

        @block.tensor
        def _(pe):
            pe.wait_ge(s_ident, 2)

            def turn_x(b):
                pe.wait_ge(s_x[b], 16)
                for kt in range(KT):
                    n = b * KT + kt
                    if n >= 4:
                        pe.wait_ge(s_xlo, n - 3)
                    for c in range(CPB):
                        ins = pe.transpose(tp[:, n % 4, bass.ts(c, P)], x_tok[:, b, c, bass.ts(kt, P)], ident[:])
                    ins.then_inc(s_xT, 1)

            def batch(b, first):
                pe.wait_ge(s_xlo, b * KT + KT)
                for m in range(MT):
                    if first and m % TPG == 0:
                        pe.wait_ge(s_wlo, m // TPG + 1)
                    n = b * IT + m // 2
                    if m % 2:
                        pe.wait_ge(s_zo, n - 1 + 2)
                    else:
                        pe.wait_ge(s_taps, 3 * (n - 1) + 6)
                    col = bass.ts(m % TPG, P)
                    for kt in range(KT):
                        ins = product(pe, acc[:, m % 4],
                                      (w_hi[:, m // TPG, kt, col], w_lo[:, m // TPG, kt, col]),
                                      (x_hi[:, kt, bass.ts(b, SEQ)], x_lo[:, kt, bass.ts(b, SEQ)]),
                                      kt == 0, kt == KT - 1)
                    ins.then_inc(s_zacc if m % 2 else s_xacc, 1)
                    if first and m % TPG == TPG - 1 and m // TPG + 1 < NB:
                        turn_x(m // TPG + 1)

            for c in range(CPB):
                pe.wait_ge(s_x0[c], 16)
                for kt in range(KT):
                    ins = pe.transpose(tp[:, kt, bass.ts(c, P)], x_tok[:, 0, c, bass.ts(kt, P)], ident[:])
                    if c == CPB - 1:
                        ins.then_inc(s_xT, 1)
            batch(0, True)
            with pe.Fori(1, NB) as b:
                batch(b, False)

        @block.scalar
        def _(act):
            act.sem_inc(s_xo, 2)
            act.sem_inc(s_zo, 2)

            def hi_of_x(b):
                for kt in range(KT):
                    n = b * KT + kt
                    act.wait_ge(s_xT, n + 1)
                    nc.scalar.activation(x_hi[:, kt, bass.ts(b, SEQ)], tp[:, n % 4], ACT.Copy).then_inc(s_xhi, 1)

            def hi_of_w(g):
                act.wait_ge(s_w[g % 2], 16 * (g // 2 + 1))
                nc.scalar.activation(w_hi[:, g], w_raw[:, g % 2], ACT.Copy).then_inc(s_whi, 1)

            def batch(b, first):
                for j in range(IT):
                    n = b * IT + j
                    act.wait_ge(s_xacc, n + 1)
                    act.wait_ge(s_xo, n - 1 + 2)
                    nc.scalar.activation(conv[:, j % 2], acc[:, 2 * j % 4], ACT.Identity,
                                         bias=cb[:, j:j + 1], scale=cw[:, j, TAPS - 1:TAPS]).then_inc(s_c, 1)
                    slot, turn = 2 * j % 4, 16 * (b * (MT // 4) + 2 * j // 4 + 1)
                    act.wait_ge(s_taps, 3 * (n + 1) + 6)
                    act.wait_ge(s_st[slot], turn)
                    nc.scalar.activation(out[:, slot], conv[:, j % 2], ACT.Silu).then_inc(s_xo, 1)
                    act.wait_ge(s_zacc, n + 1)
                    act.wait_ge(s_st[slot + 1], turn)
                    nc.scalar.activation(out[:, slot + 1], acc[:, slot + 1], ACT.Silu).then_inc(s_zo, 1)
                    if first and j % 2:
                        if j // 2 + 2 < GRP:
                            hi_of_w(j // 2 + 2)
                        if j // 2 + 1 < NB:
                            hi_of_x(j // 2 + 1)

            hi_of_x(0)
            hi_of_w(0)
            hi_of_w(1)
            act.wait_ge(s_small, 32)
            batch(0, True)
            with act.Fori(1, NB) as b:
                batch(b, False)

        @block.vector
        def _(dve):
            dve.sem_inc(s_taps, 6)

            def lo_of_x(b):
                for kt in range(KT):
                    n = b * KT + kt
                    dve.wait_ge(s_xhi, n + 1)
                    x = bass.ts(b, SEQ)
                    nc.vector.tensor_tensor(x_lo[:, kt, x], tp[:, n % 4], raw(x_hi[:, kt, x]),
                                            ALU.subtract).then_inc(s_xlo, 1)

            def lo_of_w(g):
                dve.wait_ge(s_whi, g + 1)
                nc.vector.tensor_tensor(w_lo[:, g], w_raw[:, g % 2], raw(w_hi[:, g]), ALU.subtract).then_inc(s_wlo, 1)

            def batch(b, first):
                for j in range(IT):
                    n = b * IT + j
                    dve.wait_ge(s_c, n + 1)
                    for d in range(1, TAPS):
                        dve.wait_ge(s_taps, 3 * n + d - 1 + 6)
                        nc.vector.scalar_tensor_tensor(
                            out=conv[:, j % 2, d:SEQ], in0=acc[:, 2 * j % 4, 0:SEQ - d],
                            scalar=cw[:, j, TAPS - 1 - d:TAPS - d], in1=conv[:, j % 2, d:SEQ],
                            op0=ALU.mult, op1=ALU.add).then_inc(s_taps, 1)
                    if first and j % 2:
                        if j // 2 + 2 < GRP:
                            lo_of_w(j // 2 + 2)
                        if j // 2 + 1 < NB:
                            lo_of_x(j // 2 + 1)

            lo_of_x(0)
            lo_of_w(0)
            lo_of_w(1)
            batch(0, True)
            with dve.Fori(1, NB) as b:
                batch(b, False)


def layer_norm_stats(nc, dve, x, stats, mv, s_bn, sem, n, met):
    n = n if isinstance(n, int) else dve.snap(n)
    nc.vector.bn_stats(stats, x).then_inc(s_bn, 1)
    dve.wait_ge(met, 1)
    dve.wait_ge(s_bn, n)
    nc.vector.bn_aggr(mv, stats).then_inc(sem, 1)


def inverse_deviation(nc, pool, mv, rstd, const, s_mv, s_eps, s_rstd, n):
    pool.wait_ge(s_mv, n)
    nc.gpsimd.tensor_tensor(rstd, mv[:, 1:2], const[:, 0:1], ALU.add).then_inc(s_eps, 1)
    pool.wait_ge(s_eps, n)
    nc.gpsimd.tensor_tensor(rstd, rstd, const[:, 1:2], ALU.pow).then_inc(s_rstd, 1)


def make_identity(nc, pool, ident, sem):
    nc.gpsimd.memset(ident, 0.0).then_inc(sem, 1)
    pool.wait_ge(sem, 1)
    nc.gpsimd.affine_select(out=ident, in_=ident, compare_op=ALU.not_equal, fill=1.0, base=0,
                            pattern=[[-1, P]], channel_multiplier=1).then_inc(sem, 1)


def ssd_phase(nc, t, pre, x_raw):
    with ExitStack() as ctx:
        k = Kit(nc, ctx, "ssd")
        BC = NH + 2 * NS
        wx_hi, wx_lo = (k.sb(n, [P, IT, XC], F32R) for n in ("wx_hi", "wx_lo"))
        wo_hi, wo_lo = (k.sb(n, [P, IT, DM], F32R) for n in ("wo_hi", "wo_lo"))
        x_hi, x_lo = k.sb("x_hi", [P, IT, P], F32R), k.sb("x_lo", [P, IT, P], F32R)
        z_raw = k.sb("z_raw", [P, IT, P])
        res = k.sb("res", [P, DM])
        bcd = k.sb("bcd", [P, BC])
        bct = k.sb("bct", [P, 2 * NS])
        b_tok = k.sb("b_tok", [P, NS])
        dtT = k.sb("dtT", [NH, P])
        xf = k.sb("xf", [P, NH, HD])
        xdec = k.sb("xdec", [P, NH, HD])
        r_hi, r_lo = k.sb("r_hi", [P, NH, P], F32R), k.sb("r_lo", [P, NH, P], F32R)
        state = k.sb("state", [P, NH, HD])
        g_hi, g_lo = k.sb("g_hi", [P, IT, P], F32R), k.sb("g_lo", [P, IT, P], F32R)
        rr = k.sb("rr", [P, DM])
        cb_m = k.sb("cb_m", [P, P])
        tri = k.sb("tri", [P, P])
        strict_r = k.sb("strict_r", [P, P], F32R)
        ones, ident = k.sb("ones", [P, P]), k.sb("ident", [P, P])
        keep = k.sb("keep", [P, NCH])
        dtw = k.sb("dtw", [NH, NH])
        dtb, a_pos, d_skip = (k.sb(n, [P, NH]) for n in ("dtb", "a_pos", "d_skip"))
        v, na, u, s2, q, dt, a = (k.sb(n, [P, NH]) for n in ("v", "na", "u", "s2", "q", "dt", "a"))
        s1 = na
        a_hi, a_lo = k.sb("a_hi", [P, NH], F32R), k.sb("a_lo", [P, NH])
        ed = k.sb("ed", [P, 3, NH])
        ek = k.sb("ek", [P, NH])
        stats, mv = k.sb("stats", [P, 6]), k.sb("mv", [P, 2])
        rstd, const = k.sb("rstd", [P, 1]), k.sb("const", [P, 2])
        pa, pb, po, psm = (k.ps(n, [P, 512]) for n in ("pa", "pb", "po", "psm"))
        pd = k.ps("pd", [P, 4, 512])
        CB, DTP, SUM = psm[:, 0:P], psm[:, 384:384 + NH], psm[:, 400:400 + 3 * NH]
        HP = NH * P
        decay, mix = (pre[:, i * HP:(i + 1) * HP].rearrange("p (h l) -> p h l", h=NH) for i in range(2))
        xs, xd, y, g_f = (pre[:, 2 * HP + i * DI:2 * HP + (i + 1) * DI].rearrange("p (h d) -> p h d", h=h)
                          for i, h in enumerate((NH, NH, NH, IT)))

        def staging(i):
            at = (i % EARLY) * XC
            return pre[:, at:at + (XC if i < IT else 2 * DM)]

        WG = IT + IT // 2

        s_const, s_tri, s_ident = k.sem("constants_ready"), k.sem("triangles_ready"), k.sem("ident_ready")
        s_small = k.sem("small_loaded")
        s_w = [k.sem(f"w_loaded{i}") for i in range(EARLY, WG)]
        s_whi, s_wlo = k.sem("w_hi_ready"), k.sem("w_lo_ready")
        s_lx, s_lz, s_lr = k.sem("x_loaded"), k.sem("z_loaded"), k.sem("residual_loaded")
        s_apos, s_strict = k.sem("a_exp_ready"), k.sem("strict_r_ready")
        s_xhi, s_xlo = k.sem("x_hi_ready"), k.sem("x_lo_ready")
        s_p0, s_p1, s_p2 = k.sem("X_left_half_summed"), k.sem("X_right_half_summed"), k.sem("BC_summed")
        s_xc, s_bc = k.sem("X_half_copied"), k.sem("BC_copied")
        s_t2, s_bct, s_btok = k.sem("BC_transposed"), k.sem("BC_turned_copied"), k.sem("B_copied")
        s_p3 = k.sem("CB_and_dt_summed")
        s_na, s_u = k.sem("minus_abs_dt_ready"), k.sem("exp_dt_ready")
        s_dt, s_a, s_al = k.sem("dt_ready"), k.sem("a_ready"), k.sem("a_lo_ready")
        s_r, s_rp = k.sem("r_by_dve"), k.sem("r_by_pool")
        s_sum, s_ed, s_ek = k.sem("a_sums_ready"), k.sem("decays_ready"), k.sem("state_decay_ready")
        s_diff, s_dec = k.sem("exponents_summed"), k.sem("decay_matrix_ready")
        s_cbm, s_mix = k.sem("CB_masked"), k.sem("mix_ready")
        s_xs, s_xd, s_xdec = k.sem("X_dt_ready"), k.sem("X_D_ready"), k.sem("X_decayed_ready")
        s_yoff, s_ydiag, s_st = k.sem("y_from_state_summed"), k.sem("y_in_chunk_summed"), k.sem("state_summed")
        s_yx, s_y = k.sem("skip_added"), k.sem("y_ready")
        s_sd, s_sa = k.sem("state_decayed"), k.sem("state_half_added")
        s_yT, s_g, s_ghi, s_glo = k.sem("y_transposed"), k.sem("gated"), k.sem("g_hi_ready"), k.sem("g_lo_ready")
        s_op, s_rr, s_mv, s_eps, s_rstd = (k.sem(n) for n in ("out_proj_summed", "residual_added", "mv_ready",
                                                             "eps_added", "rstd_ready"))
        s_bn = k.sem("bn_stats_ready")
        s_x1, s_out = k.sem("x1_ready"), k.sem("x1_stored")
        c_dve = k.sem("dve_steps")
        block = k.block()

        def chunks(eng, step):
            step(0, True, False, 2)
            step(1, False, True, 2)
            with eng.Fori(2, NCH - 2) as g:
                step(g, False, False, 2)
            step(NCH - 2, False, False, 1)
            step(NCH - 1, False, False, 0)

        @block.sync
        def _(sp):
            for n in ("dtw", "dtb", "a_log", "d_skip"):
                dst = {"dtw": dtw, "dtb": dtb, "a_log": a_pos, "d_skip": d_skip}[n]
                sp.dma_start(dst[:], t[n]).then_inc(s_small, 16)
            for i in range(EARLY, WG):
                sp.wait_ge(s_wlo, i - EARLY + 1)
                src = t["x_w"][:, i] if i < IT else t["out_w"][:, i - IT]
                sp.dma_start(staging(i), src).then_inc(s_w[i - EARLY], 16)

            def x_load(g):
                sp.wait_ge(s_small, 64)
                sp.wait_ge(s_xlo, g)
                sp.dma_start(x_raw[:], t["xb"][:, :, bass.ds(g * P, P)].rearrange("j p n -> p j n")).then_inc(s_lx, 16)

            def step(g, first, second, left):
                if left == 2:
                    x_load(g + 2)
                if not first:
                    sp.wait_ge(s_small, 64)
                    sp.wait_ge(s_g, g)
                sp.dma_start(z_raw[:], t["zs"][:, :, bass.ds(g * P, P)].rearrange("j p n -> p j n")).then_inc(s_lz, 16)
                if not first:
                    sp.wait_ge(s_small, 64)
                    sp.wait_ge(s_rr, g)
                sp.dma_start(res[:], t["x_rows"][bass.ds(g * P, P), :]).then_inc(s_lr, 16)
                if not first:
                    sp.wait_ge(s_small, 64)
                    sp.wait_ge(s_x1, g)
                    sp.dma_start(t["x1"][bass.ds(g * P - P, P), :], rr[:]).then_inc(s_out, 16)
            x_load(1)
            chunks(sp, step)
            sp.wait_ge(s_x1, NCH)
            sp.dma_start(t["x1"][TOK - P:TOK, :], rr[:]).then_inc(s_out, 16)
            sp.wait_ge(s_out, 16 * NCH)

        @block.gpsimd
        def _(pool):
            nc.gpsimd.memset(ones[:], 1.0).then_inc(s_const, 1)
            nc.gpsimd.memset(state[:], 0.0).then_inc(s_const, 1)
            nc.gpsimd.memset(keep[:], 1.0).then_inc(s_const, 1)
            nc.gpsimd.memset(const[:, 0:1], EPS).then_inc(s_const, 1)
            nc.gpsimd.memset(const[:, 1:2], -0.5).then_inc(s_const, 1)
            pool.wait_ge(s_const, 3)
            nc.gpsimd.memset(keep[:, CPB - 1::CPB], 0.0).then_inc(s_const, 1)
            nc.gpsimd.affine_select(out=tri[:], in_=ones[:], compare_op=ALU.is_ge, fill=0.0, base=0,
                                    pattern=[[1, P]], channel_multiplier=-1).then_inc(s_tri, 1)
            nc.gpsimd.affine_select(out=cb_m[:], in_=ones[:], compare_op=ALU.is_ge, fill=0.0, base=-1,
                                    pattern=[[-1, P]], channel_multiplier=1).then_inc(s_tri, 1)
            make_identity(nc, pool, ident[:], s_ident)
            pool.wait_ge(s_const, 6)

            def step(g, first, second, left):
                if not first and left:
                    low_of_gated(g - 1)
                pool.wait_ge(s_al, g + 1)
                if not first:
                    pool.wait_ge(s_diff, g)
                half = NH // 2
                nc.gpsimd.tensor_tensor(r_lo[:, 0:half], tri[:].unsqueeze(1).broadcast_to([P, half, P]),
                                        a_lo[:, 0:half].unsqueeze(2).broadcast_to([P, half, P]),
                                        ALU.mult).then_inc(s_rp, 1)
                if not left:
                    low_of_gated(g - 1)
                pool.wait_ge(s_xc, 2 * g + 2)
                if not first:
                    pool.wait_ge(s_y, g)
                nc.gpsimd.tensor_tensor(xd[:], xf[:], d_skip[:].unsqueeze(2).broadcast_to([P, NH, HD]),
                                        ALU.mult).then_inc(s_xd, 1)
                pool.wait_ge(s_xs, g + 1)
                pool.wait_ge(s_ed, g + 1)
                if not first:
                    pool.wait_ge(s_st, g)
                nc.gpsimd.tensor_tensor(xdec[:], xs[:], ed[:, 1].unsqueeze(2).broadcast_to([P, NH, HD]),
                                        ALU.mult).then_inc(s_xdec, 1)
                pool.wait_ge(s_yoff, g + 1)
                pool.wait_ge(s_ek, g + 1)
                if not first:
                    pool.wait_ge(s_sa, 2 * g)
                nc.gpsimd.tensor_tensor(state[:], state[:], ek[:].unsqueeze(2).broadcast_to([P, NH, HD]),
                                        ALU.mult).then_inc(s_sd, 1)
                if not first:
                    inverse_deviation(nc, pool, mv[:], rstd[:], const[:], s_mv, s_eps, s_rstd, g)

            def low_of_gated(g):
                pool.wait_ge(s_ghi, g + 1)
                nc.gpsimd.tensor_tensor(g_lo[:], g_f[:], raw(g_hi[:]), ALU.subtract).then_inc(s_glo, 1)

            pool.wait_ge(s_small, 64)
            chunks(pool, step)
            inverse_deviation(nc, pool, mv[:], rstd[:], const[:], s_mv, s_eps, s_rstd, NCH)

        @block.scalar
        def _(act):
            def x_high(g, first=False):
                if not first:
                    act.wait_ge(s_lx, 16 * g)
                    act.wait_ge(s_p2, g)
                nc.scalar.activation(x_hi[:], x_raw[:], ACT.Copy).then_inc(s_xhi, 1)

            def x_copies(g, first=False):
                for i, (bank, sem) in enumerate(((pa, s_p0), (pb, s_p1))):
                    act.wait_ge(sem, g + 1)
                    if i == 0 and not first:
                        act.wait_ge(s_xs, g)
                        act.wait_ge(s_xd, g)
                    nc.scalar.activation(xf[:, i * NH // 2:(i + 1) * NH // 2].rearrange("p h d -> p (h d)"),
                                         bank[:], ACT.Copy).then_inc(s_xc, 1)

            def bc_copy(g, first=False):
                act.wait_ge(s_p2, g + 1)
                if not first:
                    act.wait_ge(s_t2, g)
                    act.wait_ge(s_btok, g)
                nc.scalar.activation(bcd[:], pa[:, 0:BC], ACT.Copy).then_inc(s_bc, 1)

            for i in range(WG):
                if i == 1:
                    x_high(0, True)
                if i >= EARLY:
                    act.wait_ge(s_w[i - EARLY], 16)
                if i == EARLY:
                    act.wait_ge(s_tri, 2)
                    nc.scalar.activation(strict_r[:], cb_m[:], ACT.Copy).then_inc(s_strict, 1)
                    act.wait_ge(s_small, 64)
                    nc.scalar.activation(a_pos[:], a_pos[:], ACT.Exp).then_inc(s_apos, 1)
                if i < IT:
                    nc.scalar.activation(wx_hi[:, i], staging(i), ACT.Copy).then_inc(s_whi, 1)
                else:
                    o = 2 * (i - IT)
                    nc.scalar.activation(wo_hi[:, o:o + 2].rearrange("p k n -> p (k n)"), staging(i),
                                         ACT.Copy).then_inc(s_whi, 1)
            x_copies(0, True)
            bc_copy(0, True)
            x_high(1)

            def g_high(g, first):
                act.wait_ge(s_g, g + 1)
                if not first:
                    act.wait_ge(s_op, g)
                nc.scalar.activation(g_hi[:], g_f[:], ACT.Copy).then_inc(s_ghi, 1)

            def step(g, first, second, left):
                act.wait_ge(s_t2, g + 1)
                if not first:
                    act.wait_ge(s_st, g)
                nc.scalar.activation(bct[:], psm[:, 0:2 * NS], ACT.Copy).then_inc(s_bct, 1)
                nc.scalar.activation(dtT[:], psm[0:NH, 2 * NS:3 * NS], ACT.Copy).then_inc(s_bct, 1)
                act.wait_ge(s_bc, g + 1)
                nc.scalar.activation(b_tok[:], bcd[:, NH:NH + NS], ACT.Copy).then_inc(s_btok, 1)
                act.wait_ge(s_na, g + 1)
                nc.scalar.activation(u[:], na[:], ACT.Exp).then_inc(s_u, 1)
                if not first:
                    g_high(g - 1, second)
                if left:
                    x_copies(g + 1)
                act.wait_ge(s_sum, g + 1)
                if not first:
                    act.wait_ge(s_sd, g)
                    act.wait_ge(s_y, g)
                    act.wait_ge(s_ek, g)
                nc.scalar.activation(ed[:].rearrange("p k h -> p (k h)"), SUM, ACT.Exp).then_inc(s_ed, 1)
                act.wait_ge(s_diff, g + 1)
                if not first:
                    act.wait_ge(s_mix, g)
                nc.scalar.activation(decay[:].rearrange("p h l -> p (h l)"),
                                     pd[:].rearrange("p q n -> p (q n)"), ACT.Exp).then_inc(s_dec, 1)
                if left:
                    bc_copy(g + 1)
                if left == 2:
                    x_high(g + 2)
            chunks(act, step)
            g_high(NCH - 1, False)

        @block.tensor
        def _(pe):
            pieces = ((pa, 0, 512, s_p0), (pb, 512, 512, s_p1), (pa, 2 * 512, BC, s_p2))

            def x_proj_part(piece, kt):
                bank, lo, n, sem = pieces[piece]
                ins = product(pe, bank[:, 0:n], (x_hi[:, kt], x_lo[:, kt]),
                              (wx_hi[:, kt, lo:lo + n], wx_lo[:, kt, lo:lo + n]), kt == 0, kt == IT - 1)
                if kt == IT - 1:
                    ins.then_inc(sem, 1)

            def x_proj(g, piece, first=False, second=False):
                if piece == 0:
                    pe.wait_ge(s_xlo, g + 1)
                if piece == 2:
                    pe.wait_ge(s_xc, 2 * g + 1)
                elif not first:
                    pe.wait_ge(s_bc, g)
                    if not second:
                        pe.wait_ge(s_sa, 2 * (g - 2) + 1 + piece)
                for kt in range(IT):
                    x_proj_part(piece, kt)

            def turn_y(g):
                pe.wait_ge(s_y, g + 1)
                for j in range(IT):
                    ins = pe.transpose(pd[:, j // 4, bass.ts(j % 4, P)],
                                       y[:, 2 * j:2 * j + 2].rearrange("p h d -> p (h d)"), ident[:])
                ins.then_inc(s_yT, 1)

            def out_proj(g, first):
                pe.wait_ge(s_glo, g + 1)
                if not first:
                    pe.wait_ge(s_rr, g)
                for kt in range(IT):
                    ins = product(pe, po[:], (g_hi[:, kt], g_lo[:, kt]), (wo_hi[:, kt], wo_lo[:, kt]),
                                  kt == 0, kt == IT - 1)
                ins.then_inc(s_op, 1)

            def step(g, first, second, left):
                pe.wait_ge(s_bc, g + 1)
                if not first:
                    pe.wait_ge(s_ed, g)
                pe.transpose(psm[:, 0:NS], bcd[:, NH:NH + NS], ident[:])
                pe.transpose(psm[:, NS:2 * NS], bcd[:, NH + NS:BC], ident[:])
                pe.transpose(psm[0:NH, 2 * NS:3 * NS], bcd[:, 0:NH], ident[:]).then_inc(s_t2, 1)
                if left:
                    x_proj(g + 1, 0, second=first)
                if not first and left:
                    turn_y(g - 1)
                pe.wait_ge(s_bct, 2 * g + 2)
                pe.matmul(CB, bct[:, 0:NS], bct[:, NS:2 * NS], start=True, stop=True)
                pe.matmul(DTP, dtT[:], dtw[:], start=True, stop=True).then_inc(s_p3, 1)
                if left:
                    x_proj(g + 1, 1, second=first)
                else:
                    turn_y(g - 1)
                pe.wait_ge(s_a, g + 1)
                pe.wait_ge(s_cbm, g + 1)
                for i, m in enumerate((tri[:], raw(strict_r[:]), ones[:])):
                    ins = pe.matmul(SUM[:, i * NH:(i + 1) * NH], m, a[:], start=True, stop=True)
                ins.then_inc(s_sum, 1)
                if not first and left:
                    out_proj(g - 1, second)
                pe.wait_ge(s_r, g + 1)
                pe.wait_ge(s_rp, g + 1)
                if not first:
                    pe.wait_ge(s_g, g)
                for i in range(4):
                    heads = slice(4 * i, 4 * i + 4)
                    pe.matmul(pd[:, i], strict_r[:], r_hi[:, heads].rearrange("p h l -> p (h l)"),
                              start=True, stop=False)
                    ins = pe.matmul(pd[:, i], strict_r[:], r_lo[:, heads].rearrange("p h l -> p (h l)"),
                                    start=False, stop=True)
                ins.then_inc(s_diff, 1)
                if left:
                    x_proj(g + 1, 2)
                else:
                    out_proj(g - 1, second)
                pe.wait_ge(s_dec, g + 1)
                if not first:
                    pe.wait_ge(s_sa, 2 * g)
                for i in range(2):
                    ins = pe.matmul(pd[:, i], bct[:, NS:2 * NS],
                                    state[:, i * NH // 2:(i + 1) * NH // 2].rearrange("p h d -> p (h d)"),
                                    start=True, stop=True)
                ins.then_inc(s_yoff, 1)
                pe.wait_ge(s_xdec, g + 1)
                if left:
                    pe.wait_ge(s_xc, 2 * g + 4)
                    pe.wait_ge(s_bc, g + 2)
                for i, bank in enumerate((pa, pb)):
                    ins = pe.matmul(bank[:], b_tok[:],
                                    xdec[:, i * NH // 2:(i + 1) * NH // 2].rearrange("p h d -> p (h d)"),
                                    start=True, stop=True)
                ins.then_inc(s_st, 1)
                pe.wait_ge(s_mix, g + 1)
                pe.wait_ge(s_xs, g + 1)
                for h in range(NH):
                    ins = pe.matmul(pd[:, 2 + h // 8, bass.ts(h % 8, HD)], mix[:, h], xs[:, h],
                                    start=True, stop=True)
                ins.then_inc(s_ydiag, 1)

            pe.wait_ge(s_xlo, 1)
            for kt in range(IT):
                pe.wait_ge(s_wlo, kt + 1)
                x_proj_part(0, kt)
                x_proj_part(1, kt)
            x_proj(0, 2, True)
            pe.wait_ge(s_wlo, WG)
            pe.wait_ge(s_const, 6)
            pe.wait_ge(s_tri, 2)
            pe.wait_ge(s_ident, 2)
            pe.wait_ge(s_strict, 1)
            pe.wait_ge(s_small, 64)
            chunks(pe, step)
            turn_y(NCH - 1)
            out_proj(NCH - 1, False)

        @block.vector
        def _(dve):
            chain = Chain(dve, c_dve, 17)
            tt, stt, ts = nc.vector.tensor_tensor, nc.vector.scalar_tensor_tensor, nc.vector.tensor_scalar
            heads = lambda ap, n: ap.unsqueeze(2).broadcast_to([P, ap.shape[1], n])
            flat = lambda ap: ap.rearrange("p h d -> p (h d)")

            def x_low(g):
                dve.wait_ge(s_xhi, g + 1)
                tt(x_lo[:], x_raw[:], raw(x_hi[:]), ALU.subtract).then_inc(s_xlo, 1)

            for i in range(WG):
                if i == 1:
                    x_low(0)
                dve.wait_ge(s_whi, i + 1)
                if i < IT:
                    tt(wx_lo[:, i], staging(i), raw(wx_hi[:, i]), ALU.subtract).then_inc(s_wlo, 1)
                else:
                    o = 2 * (i - IT)
                    tt(flat(wo_lo[:, o:o + 2]), staging(i), raw(flat(wo_hi[:, o:o + 2])),
                       ALU.subtract).then_inc(s_wlo, 1)
            dve.wait_ge(s_wlo, WG)
            dve.wait_ge(s_small, 64)
            dve.wait_ge(s_apos, 1)
            dve.wait_ge(s_tri, 2)
            dve.wait_ge(s_const, 6)
            x_low(1)

            def gate(g, first):
                dve.wait_ge(s_yT, g + 1)
                dve.wait_ge(s_lz, 16 * (g + 1))
                if not first:
                    dve.wait_ge(s_glo, g)
                tt(g_f[:].rearrange("p k n -> p (k n)"), pd[:, 0:2].rearrange("p q n -> p (q n)"),
                   z_raw[:].rearrange("p k n -> p (k n)"), ALU.mult).then_inc(s_g, 1)

            def residual_sum(g, first=False):
                if not first:
                    dve.wait_ge(s_out, 16 * g)
                dve.wait_ge(s_op, g + 1)
                dve.wait_ge(s_lr, 16 * (g + 1))
                tt(rr[:], po[:], res[:], ALU.add).then_inc(s_rr, 1)

            def statistics(g):
                dve.wait_ge(s_rr, g + 1)
                layer_norm_stats(nc, dve, rr[:], stats[:], mv[:], s_bn, s_mv, g + 1, s_tri)

            def normalize(g):
                dve.wait_ge(s_rstd, g + 1)
                ts(rr[:], rr[:], mv[:, 0:1], rstd[:], ALU.subtract, ALU.mult).then_inc(s_x1, 1)
                dve.wait_ge(s_x1, g + 1)

            def step(g, first, second, left):
                chain.round(g)
                if not first and left:
                    gate(g - 1, second)
                dve.wait_ge(s_p3, g + 1)
                tt(cb_m[:], CB, tri[:], ALU.mult).then_inc(s_cbm, 1)
                chain.link(tt(v[:], DTP, dtb[:], ALU.add))
                chain.link(ts(na[:], v[:], -1.0, None, ALU.mult))
                tt(na[:], na[:], v[:], ALU.min).then_inc(s_na, 1)
                dve.wait_ge(s_u, g + 1)
                chain.link(ts(s1[:], u[:], 2.0, None, ALU.add))
                chain.link(nc.vector.reciprocal(s1[:], s1[:]))
                chain.link(tt(s1[:], u[:], s1[:], ALU.mult))
                chain.link(tt(q[:], s1[:], s1[:], ALU.mult))
                chain.link(ts(s2[:], q[:], 1.0 / 13, None, ALU.mult))
                for n in (11, 9, 7, 5, 3):
                    chain.link(stt(out=s2[:], in0=s2[:], scalar=1.0 / n, in1=q[:], op0=ALU.add, op1=ALU.mult))
                chain.link(stt(out=s2[:], in0=s2[:], scalar=1.0, in1=s1[:], op0=ALU.add, op1=ALU.mult))
                chain.link(ts(v[:], v[:], 0.0, None, ALU.max))
                stt(out=dt[:], in0=s2[:], scalar=2.0, in1=v[:], op0=ALU.mult, op1=ALU.add).then_inc(s_dt, 1)
                dve.wait_ge(s_dt, g + 1)
                stt(out=a[:], in0=dt[:], scalar=-1.0, in1=a_pos[:], op0=ALU.mult, op1=ALU.mult).then_inc(s_a, 1)
                dve.wait_ge(s_a, g + 1)
                chain.link(nc.vector.tensor_copy(a_hi[:], a[:]))
                tt(a_lo[:], a[:], raw(a_hi[:]), ALU.subtract).then_inc(s_al, 1)
                if not left:
                    gate(g - 1, second)
                dve.wait_ge(s_al, g + 1)
                half = NH // 2
                tt(r_lo[:, half:NH], tri[:].unsqueeze(1).broadcast_to([P, half, P]), heads(a_lo[:, half:NH], P),
                   ALU.mult)
                tt(r_hi[:], tri[:].unsqueeze(1).broadcast_to([P, NH, P]), heads(raw(a_hi[:]), P),
                   ALU.mult).then_inc(s_r, 1)
                dve.wait_ge(s_xc, 2 * g + 2)
                tt(xs[:], xf[:], heads(dt[:], HD), ALU.mult).then_inc(s_xs, 1)
                dve.wait_ge(s_ed, g + 1)
                ts(ek[:], ed[:, 2], keep[:, bass.ds(g, 1)], None, ALU.mult).then_inc(s_ek, 1)
                dve.wait_ge(s_dec, g + 1)
                tt(mix[:], decay[:], cb_m[:].unsqueeze(1).broadcast_to([P, NH, P]), ALU.mult).then_inc(s_mix, 1)
                if left == 2:
                    x_low(g + 2)
                if not first:
                    residual_sum(g - 1, second)
                dve.wait_ge(s_st, g + 1)
                dve.wait_ge(s_sd, g + 1)
                for i, bank in enumerate((pa, pb)):
                    part = flat(state[:, i * half:(i + 1) * half])
                    stt(out=part, in0=bank[:], scalar=keep[:, bass.ds(g, 1)], in1=part,
                        op0=ALU.mult, op1=ALU.add).then_inc(s_sa, 1)
                if not first:
                    statistics(g - 1)
                dve.wait_ge(s_yoff, g + 1)
                chain.link(tt(y[:], pd[:, 0:2].rearrange("p q (h d) -> p (q h) d", d=HD), heads(ed[:, 0], HD), ALU.mult))
                if not first:
                    normalize(g - 1)
                dve.wait_ge(s_xd, g + 1)
                tt(flat(y[:]), flat(y[:]), flat(xd[:]), ALU.add).then_inc(s_yx, 1)
                dve.wait_ge(s_yx, g + 1)
                dve.wait_ge(s_ydiag, g + 1)
                tt(flat(y[:]), flat(y[:]), pd[:, 2:4].rearrange("p q n -> p (q n)"), ALU.add).then_inc(s_y, 1)
                dve.wait_ge(s_sa, 2 * g + 2)
                chain.close()
            chunks(dve, step)
            chain.round(NCH)
            gate(NCH - 1, False)
            dve.wait_ge(s_ghi, NCH)
            tt(g_lo[:], g_f, raw(g_hi[:]), ALU.subtract).then_inc(s_glo, 1)
            residual_sum(NCH - 1)
            statistics(NCH - 1)
            normalize(NCH - 1)


def inverse_deviations(nc, pool, mv, rstd, minus_half, s_eps, s_rstd, n):
    nc.gpsimd.tensor_scalar(rstd, mv[:, :, 1], EPS, None, ALU.add).then_inc(s_eps, 1)
    pool.wait_ge(s_eps, n)
    nc.gpsimd.tensor_tensor(rstd, rstd, minus_half, ALU.pow).then_inc(s_rstd, 1)


def ffn_phase(nc, t, acc, gated, w_qkv=None):
    with ExitStack() as ctx:
        k = Kit(nc, ctx, "moe" if gated else "ffn")
        TAG = "e_" if gated else "f_"
        UNITS = 8 if gated else 4
        NE = 8 if gated else 16
        NU = 2 if gated else 1
        F = 4
        RING = 4 // NU
        R = 64
        GOLD_C, GOLD_LO, GOLD_HI = 0.36787944117144233, 0.5 - 0.28768207245178085, 0.5

        xc_hi, xc_lo = (k.sb(n, [P, KT, TOK], F32R) for n in ("xc_hi", "xc_lo"))
        up_raw = k.sb("up_raw", [P, NU, F, KT, P])
        dn_raw = k.sb("dn_raw", [P, F, DM])
        up_hi, up_lo = (k.sb(n, [P, NU, F, KT, P], F32R) for n in ("up_hi", "up_lo"))
        dn_hi, dn_lo = (k.sb(n, [P, F, DM], F32R) for n in ("dn_hi", "dn_lo"))
        h_f = k.sb("h_f", [P, 2, SEQ])
        act_f = k.sb("act_f", [P, 2, SEQ]) if gated else None
        h_hi, h_lo = (k.sb(n, [P, F, SEQ], F32R) for n in ("h_hi", "h_lo"))
        wts = k.sb("wts", [P, NCH, NE])
        rw_raw = k.sb("rw_raw", [P, KT, NE])
        rw = k.sb("rw", [P, KT, 2 * NE], F32R)
        rb = k.sb("rb", [P, NE if not gated else 1])
        lower = k.sb("lower", [P, NE, NE])
        GRP = CPB
        lg, pr, sel, gold = (k.sb(n, [P, GRP, NE]) for n in ("lg", "pr", "sel", "gold"))
        sum1, sum2 = k.sb("sum1", [P, GRP]), k.sb("sum2", [P, GRP])
        cmp1, cmp2 = (k.sb(n, [P, GRP, NE, NE]) for n in ("cmp1", "cmp2"))
        ident = k.sb("ident", [P, P])
        minus_half = k.sb("minus_half", [P, CPB])
        stats, mv, rstd = k.sb("stats", [P, CPB, 6]), k.sb("mv", [P, CPB, 2]), k.sb("rstd", [P, CPB])
        if gated:
            la_up, lb_up = k.sb("la_up", [2 * R, DM]), k.sb("lb_up", [2 * R, DM])
            la_dn, lb_dn = k.sb("la_dn", [R, DM]), k.sb("lb_dn", [R, DM])
        pu, pd = k.ps("pu", [P, 4, 512]), k.ps("pd", [P, 4, 512])
        logT = dn_raw[0:2 * NE]
        ORDER = ((0, 2, 1), (1, 0, 2), (3, 3, NE - 3))

        s_x = [k.sem(f"x_loaded{b}") for b in range(NB)]
        s_x0 = [k.sem(f"x_chunk_loaded{c}") for c in range(CPB)]
        s_small = k.sem("small_loaded")
        s_lora = k.sem("lora_loaded")
        s_lu, s_ld = k.sem("up_loaded"), k.sem("down_loaded")
        s_ident, s_mem = k.sem("ident_ready"), k.sem("constants_ready")
        s_xT, s_xhi, s_xlo = k.sem("x_transposed"), k.sem("x_hi_ready"), k.sem("x_lo_ready")
        s_rwhi, s_rwlo = k.sem("router_hi_ready"), k.sem("router_lo_ready")
        s_lg, s_lgc = k.sem("logits_summed"), k.sem("logits_copied")
        s_lgT, s_wts = k.sem("logits_turned"), k.sem("logits_on_tokens")
        s_z, s_e = k.sem("router_to_act"), k.sem("router_from_act")
        s_uhi, s_ulo = k.sem("up_hi_ready"), k.sem("up_lo_ready")
        s_dhi, s_dlo = k.sem("down_hi_ready"), k.sem("down_lo_ready")
        s_delta, s_merged = k.sem("lora_delta_summed"), k.sem("lora_merged")
        s_up = k.sem("hidden_summed")
        s_act, s_hf = k.sem("silu_ready"), k.sem("hidden_ready")
        s_hhi, s_hlo = k.sem("hidden_hi_ready"), k.sem("hidden_lo_ready")
        s_dn, s_acc = k.sem("down_summed"), k.sem("down_added")
        s_bn, s_mv, s_eps, s_rstd = (k.sem(n) for n in ("bn_stats_ready", "mv_ready", "eps_added", "rstd_ready"))
        s_norm, s_out = k.sem("normalized"), k.sem("stored")
        s_wq = k.sem("qkv_weights_loaded")
        c_dve = k.sem("dve_router_steps")
        block = k.block()

        @block.sync
        def _(sp):
            def load_x(b):
                if not gated:
                    sp.dma_start(acc[:, b * CPB:(b + 1) * CPB],
                                 t["x1"][b * SEQ:(b + 1) * SEQ, :].rearrange("(c p) d -> p c d", p=P)).then_inc(s_x[b], 16)

            def lora(e):
                for dst, n in ((la_up, "la_up"), (lb_up, "lb_up"), (la_dn, "la_dn"), (lb_dn, "lb_dn")):
                    sp.dma_start(dst[:], t[n][e]).then_inc(s_lora, 16)

            if not gated:
                for c in range(CPB):
                    sp.dma_start(acc[:, c], t["x1"][c * P:(c + 1) * P, :]).then_inc(s_x0[c], 16)
            sp.dma_start(rw_raw[:], t[TAG + "router"]).then_inc(s_small, 16)
            sp.dma_start(rb[:], t[TAG + "rb"]).then_inc(s_small, 16)
            load_x(1)
            load_x(2)
            sp.dma_start(up_raw[:], t[TAG + "up"][0]).then_inc(s_lu, 16)
            load_x(3)
            if gated:
                lora(0)
            sp.wait_ge(s_wts, 1)
            sp.dma_start(dn_raw[:], t[TAG + "dn"][0]).then_inc(s_ld, 16)

            def unit(u):
                sp.wait_ge(s_small, 32)
                sp.wait_ge(s_ulo, NU * F * u + NU * F)
                sp.dma_start(up_raw[:], t[TAG + "up"][bass.ds(u + 1, 1)].rearrange(
                    "o p n f k c -> (o p) n f k c")).then_inc(s_lu, 16)
                sp.wait_ge(s_small, 32)
                sp.wait_ge(s_dlo, F * u + F)
                sp.dma_start(dn_raw[:], t[TAG + "dn"][bass.ds(u + 1, 1)].rearrange(
                    "o p f d -> (o p) f d")).then_inc(s_ld, 16)
            if not gated:
                sp.dma_start(w_qkv[:], t["qkv_w"]).then_inc(s_wq, 16)
            unit(0)
            if gated:
                sp.wait_ge(s_delta, 12)
                lora(1)
            with sp.Fori(1, UNITS - 1) as u:
                unit(u)
            if not gated:
                sp.wait_ge(s_wq, 16)
            if gated:
                for ch in range(NCH):
                    sp.wait_ge(s_norm, ch + 1)
                    sp.dma_start(t["out"][ch // CPB, bass.ts(ch % CPB, P)], acc[:, ch]).then_inc(s_out, 16)
                sp.wait_ge(s_out, 16 * NCH)

        @block.gpsimd
        def _(pool):
            make_identity(nc, pool, ident[:], s_ident)
            nc.gpsimd.memset(minus_half[:], -0.5).then_inc(s_mem, 1)
            nc.gpsimd.memset(lower[:], 1.0).then_inc(s_mem, 1)
            pool.wait_ge(s_mem, 2)
            nc.gpsimd.affine_select(out=lower[:], in_=lower[:], compare_op=ALU.is_ge, fill=0.0, base=-1,
                                    pattern=[[1, NE], [-1, NE]], channel_multiplier=0).then_inc(s_mem, 1)

            def unit(u, first, last, second=False):
                for tt in range(NB):
                    for f in range(F):
                        m = F * NB * u + F * tt + f
                        pool.wait_ge(s_hhi, m + 1)
                        nc.gpsimd.tensor_tensor(h_lo[:, f], h_f[:, f % 2], raw(h_hi[:, f]),
                                                ALU.subtract).then_inc(s_hlo, 1)
                        if last and tt >= 2 and f == 1:
                            deviations(tt - 1)

            def deviations(n):
                pool.wait_ge(s_mv, CPB * n)
                inverse_deviations(nc, pool, mv[:], rstd[:], minus_half[:], s_eps, s_rstd, n)

            unit(0, True, False)
            unit(1, False, False, True)
            with pool.Fori(2, UNITS - 1) as u:
                unit(u, False, False)
            unit(UNITS - 1, False, True)
            deviations(NB - 1)
            deviations(NB)

        @block.scalar
        def _(act):
            act.wait_ge(s_small, 32)
            nc.scalar.activation(rw[:, :, 0:NE], rw_raw[:], ACT.Copy).then_inc(s_rwhi, 1)

            def turned_logits(b):
                act.wait_ge(s_lg, b + 1)
                nc.scalar.activation(logT[:, b], pu[0:2 * NE, b], ACT.Copy).then_inc(s_lgT, 1)

            for b in range(NB):
                for kt in range(KT):
                    act.wait_ge(s_xT, b * KT + kt + 1)
                    nc.scalar.activation(xc_hi[:, kt, bass.ts(b, SEQ)], pd[:, kt], ACT.Copy).then_inc(s_xhi, 1)
                if b:
                    turned_logits(b - 1)
            turned_logits(NB - 1)

            def up_high(u, f):
                act.wait_ge(s_lu, 16 * u + 16)
                for i in range(NU):
                    nc.scalar.activation(up_hi[:, i, f], up_raw[:, i, f], ACT.Copy).then_inc(s_uhi, 1)

            for f in range(F):
                up_high(0, f)

            def unit(u, first, last, second=False):
                for tt in range(NB):
                    for f in range(F):
                        m = F * NB * u + F * tt + f
                        act.wait_ge(s_up, m + 1)
                        if gated:
                            if not (first and m < 2):
                                act.wait_ge(s_hf, m - 1)
                            nc.scalar.activation(act_f[:, f % 2], pu[:, (f % RING) * NU], ACT.Silu).then_inc(s_act, 1)
                        else:
                            if not (first and m < 2):
                                act.wait_ge(s_hlo, m - 1)
                            nc.scalar.activation(h_f[:, f % 2], pu[:, f], ACT.Gelu).then_inc(s_hf, 1)
                        if tt == NB - 1 and not last:
                            if gated and (first or second):
                                act.wait_ge(s_merged, 12 * u + 8)
                            up_high(u + 1, f)
                        act.wait_ge(s_hf, m + 1)
                        if not (first and tt == 0):
                            act.wait_ge(s_dn, F * (m - F) + F)
                        nc.scalar.activation(h_hi[:, f], h_f[:, f % 2], ACT.Copy).then_inc(s_hhi, 1)
                        if tt == 0:
                            act.wait_ge(s_ld, 16 * u + 16)
                            if gated and second:
                                act.wait_ge(s_merged, 12)
                            elif gated and not first:
                                act.wait_ge(s_merged, 24)
                            nc.scalar.activation(dn_hi[:, f], dn_raw[:, f], ACT.Copy).then_inc(s_dhi, 1)
                        if first:
                            router_functions(tt, f)

            def router_functions(n, part):
                if not gated and part == 0:
                    act.wait_ge(s_z, n + 1)
                    nc.scalar.activation(pr[:], lg[:], ACT.Exp).then_inc(s_e, 1)
                if gated and part == 0:
                    act.wait_ge(s_z, 2 * n + 1)
                    nc.scalar.activation(pr[:], lg[:], ACT.Sigmoid).then_inc(s_e, 1)
                if gated and part == 1:
                    act.wait_ge(s_z, 2 * n + 2)
                    nc.scalar.activation(sel[:], lg[:], ACT.Exp, scale=-1 / 0.1).then_inc(s_e, 1)
                    nc.scalar.activation(pr[:], lg[:], ACT.Exp, scale=-1 / 0.3).then_inc(s_e, 1)

            unit(0, True, False)
            unit(1, False, False, True)
            with act.Fori(2, UNITS - 1) as u:
                unit(u, False, False)
            unit(UNITS - 1, False, True)

        @block.tensor
        def _(pe):
            pe.wait_ge(s_ident, 2)

            def logits(b):
                pe.wait_ge(s_rwlo, 1)
                pe.wait_ge(s_xlo, b * KT + KT)
                for kt in range(KT):
                    x = bass.ts(b, SEQ)
                    pe.matmul(pu[0:2 * NE, b], rw[:, kt], xc_hi[:, kt, x], start=kt == 0, stop=False)
                    ins = pe.matmul(pu[0:NE, b], rw[:, kt, 0:NE], xc_lo[:, kt, x], start=False, stop=kt == KT - 1)
                ins.then_inc(s_lg, 1)

            for c in range(CPB):
                if not gated:
                    pe.wait_ge(s_x0[c], 16)
                for kt in range(KT):
                    ins = pe.transpose(pd[:, kt, bass.ts(c, P)], acc[:, c, bass.ts(kt, P)], ident[:])
                    if c == CPB - 1:
                        ins.then_inc(s_xT, 1)
            for b in range(1, NB):
                if not gated:
                    pe.wait_ge(s_x[b], 16)
                for kt in range(KT):
                    pe.wait_ge(s_xlo, b * KT + kt - KT + 1)
                    for c in range(CPB):
                        ins = pe.transpose(pd[:, kt, bass.ts(c, P)], acc[:, b * CPB + c, bass.ts(kt, P)], ident[:])
                    ins.then_inc(s_xT, 1)
                logits(b - 1)
            logits(NB - 1)
            pe.wait_ge(s_lgT, NB)
            for g in range(NCH):
                ins = pe.transpose(pd[:, 0, bass.ts(g, 2 * NE)], logT[:, g // CPB, bass.ts(g % CPB, P)],
                                   ident[0:2 * NE, 0:2 * NE])
            ins.then_inc(s_wts, 1)

            def merge(e, i, before):
                if i == 0:
                    pe.wait_ge(s_lora, 64 * e + 64)
                    pe.wait_ge(s_lgc, 1)
                if before:
                    pe.wait_ge(s_acc, before)
                if i < 8:
                    rows = slice(R * (i // 4), R * (i // 4) + R)
                    a, b = la_up[rows, bass.ts(i % 4, P)], lb_up[rows, :]
                else:
                    a, b = la_dn[:, bass.ts(i - 8, P)], lb_dn[:]
                pe.matmul(pd[:, 0], a, b, start=True, stop=True).then_inc(s_delta, 1)

            def down(m, f, tt, u, start):
                pe.wait_ge(s_hlo, m + 1)
                pe.wait_ge(s_dlo, F * u + f + 1)
                for c in range(CPB):
                    if not start:
                        pe.wait_ge(s_acc, CPB * (m - 1) + c + 1)
                    ins = product(pe, pd[:, c], (h_hi[:, f, bass.ts(c, P)], h_lo[:, f, bass.ts(c, P)]),
                                  (dn_hi[:, f], dn_lo[:, f]))
                    ins.then_inc(s_dn, 1)

            def unit(u, first, last, second=False):
                for tt in range(NB):
                    for f in range(F):
                        m = F * NB * u + F * tt + f
                        if gated and (first or second) and tt:
                            merge(u, F * (tt - 1) + f, max(0, CPB * (m - F - 1) + 1))
                        if tt == 0:
                            pe.wait_ge(s_ulo, NU * F * u + NU * f + NU)
                        if not (first and m < RING):
                            pe.wait_ge(s_hf, m - RING + 1)
                        for i in range(NU):
                            for kt in range(KT):
                                x = bass.ts(tt, SEQ)
                                ins = product(pe, pu[:, (f % RING) * NU + i], (up_hi[:, i, f, kt], up_lo[:, i, f, kt]),
                                              (xc_hi[:, kt, x], xc_lo[:, kt, x]), kt == 0, kt == KT - 1)
                        ins.then_inc(s_up, 1)
                        if gated and (first or second) and tt:
                            pe.wait_ge(s_merged, 12 * u + F * (tt - 1) + f + 1)
                        if not (first and tt == 0):
                            down(m - F, f, (tt - 1) % NB, u - 1 if tt == 0 else u, first and m == F)

            unit(0, True, False)
            unit(1, False, False, True)
            with pe.Fori(2, UNITS - 1) as u:
                unit(u, False, False)
            unit(UNITS - 1, False, True)
            for f in range(F):
                down(F * NB * UNITS - F + f, f, NB - 1, UNITS - 1, False)

        @block.vector
        def _(dve):
            chain = Chain(dve, c_dve, 0)
            link = chain.link
            tt_, stt, ts = nc.vector.tensor_tensor, nc.vector.scalar_tensor_tensor, nc.vector.tensor_scalar
            red = nc.vector.tensor_reduce
            over = lambda ap, n: ap.unsqueeze(2).broadcast_to([P, ap.shape[1], n])

            for b in range(NB):
                for kt in range(KT):
                    dve.wait_ge(s_xhi, b * KT + kt + 1)
                    x = bass.ts(b, SEQ)
                    tt_(xc_lo[:, kt, x], pd[:, kt], raw(xc_hi[:, kt, x]), ALU.subtract).then_inc(s_xlo, 1)
                if b == 0:
                    dve.wait_ge(s_rwhi, 1)
                    tt_(rw[:, :, NE:2 * NE], rw_raw[:], raw(rw[:, :, 0:NE]), ALU.subtract).then_inc(s_rwlo, 1)

            def merge(e, i):
                dve.wait_ge(s_delta, 12 * e + i + 1)
                if i < 8:
                    dve.wait_ge(s_lu, 16 * e + 32)
                    w, d = up_raw[:, i // 4, :, i % 4], pd[:, 0].rearrange("p (f c) -> p f c", c=P)
                else:
                    dve.wait_ge(s_ld, 16 * e + 32)
                    w, d = dn_raw[:, i - 8], pd[:, 0]
                tt_(w, d, w, ALU.add).then_inc(s_merged, 1)

            def up_low(u, f):
                for i in range(NU):
                    dve.wait_ge(s_uhi, NU * F * u + NU * f + i + 1)
                    tt_(up_lo[:, i, f], up_raw[:, i, f], raw(up_hi[:, i, f]), ALU.subtract).then_inc(s_ulo, 1)

            for f in range(F):
                up_low(0, f)
            dve.wait_ge(s_wts, 1)
            parts = pd[:, 0, 0:NCH * 2 * NE].rearrange("p (c e) -> p c e", c=NCH)
            link(nc.vector.tensor_copy(wts[:], parts[:, :, 0:NE]))
            tt_(wts[:], wts[:], parts[:, :, NE:2 * NE], ALU.add).then_inc(s_lgc, 1)
            dve.wait_ge(s_lgc, 1)

            def ranks(p, part):
                pj = p.unsqueeze(2).broadcast_to([P, GRP, NE, NE])
                pi = p.unsqueeze(3).broadcast_to([P, GRP, NE, NE])
                if part == 0:
                    link(tt_(cmp1[:], pj, pi, ALU.is_gt))
                    link(tt_(cmp2[:], pj, pi, ALU.is_equal))
                else:
                    link(tt_(cmp2[:], cmp2[:], lower[:].unsqueeze(1).broadcast_to([P, GRP, NE, NE]), ALU.mult))
                    link(tt_(cmp1[:], cmp1[:], cmp2[:], ALU.add))

            def router_blocks(n, part):
                w = wts[:, n * GRP:(n + 1) * GRP]
                if part == 0:
                    link(tt_(w, w, rb[:].unsqueeze(1).broadcast_to([P, GRP, NE]), ALU.add))
                    link(red(sum1[:], w, AX_X, ALU.max))
                    tt_(lg[:], w, over(sum1[:], NE), ALU.subtract).then_inc(s_z, 1)
                if part == 1:
                    dve.wait_ge(s_e, n + 1)
                    link(red(sum1[:], pr[:], AX_X, ALU.add))
                    link(nc.vector.reciprocal(sum1[:], sum1[:]))
                    link(tt_(pr[:], pr[:], over(sum1[:], NE), ALU.mult))
                    ranks(pr[:], 0)
                if part == 2:
                    ranks(pr[:], 1)
                if part == 3:
                    link(red(sel[:], cmp1[:], AX_X, ALU.add))
                    link(ts(w, sel[:], 3.5, None, ALU.is_lt))

            def router_golden(n, part):
                w = wts[:, n * GRP:(n + 1) * GRP]
                if part == 0:
                    if n == 0:
                        link(nc.vector.reciprocal(rb[:], rb[:]))
                    ts(lg[:], w, rb[:], None, ALU.mult).then_inc(s_z, 1)
                if part == 1:
                    dve.wait_ge(s_e, 3 * n + 1)
                    link(ts(gold[:], pr[:], GOLD_LO, None, ALU.is_ge))
                    link(ts(cmp1[:, :, 0], pr[:], GOLD_HI, None, ALU.is_le))
                    link(tt_(gold[:], gold[:], cmp1[:, :, 0], ALU.mult))
                    link(ts(lg[:], pr[:], GOLD_C, None, ALU.subtract))
                    link(ts(cmp1[:, :, 0], lg[:], -1.0, None, ALU.mult))
                    tt_(lg[:], lg[:], cmp1[:, :, 0], ALU.max).then_inc(s_z, 1)
                if part == 2:
                    dve.wait_ge(s_e, 3 * n + 2)
                    link(tt_(gold[:], gold[:], sel[:], ALU.mult))
                    dve.wait_ge(s_e, 3 * n + 3)
                    ranks(pr[:], 0)
                    ranks(pr[:], 1)
                if part == 3:
                    link(red(sel[:], cmp1[:], AX_X, ALU.add))
                    link(ts(sel[:], sel[:], 1.5, None, ALU.is_lt))
                    link(tt_(sel[:], sel[:], pr[:], ALU.mult))
                    inverse_of_sum(sel[:])
                    link(tt_(sel[:], sel[:], over(sum1[:], NE), ALU.mult))
                    link(red(sum1[:], gold[:], AX_X, ALU.add))
                    link(ts(sum2[:], sum1[:], 1e-8, None, ALU.is_lt))
                    link(tt_(sel[:], sel[:], over(sum2[:], NE), ALU.mult))
                    link(ts(sum2[:], sum2[:], -1.0, 1.0, ALU.mult, ALU.add))
                    link(tt_(gold[:], gold[:], over(sum2[:], NE), ALU.mult))
                    link(tt_(gold[:], gold[:], sel[:], ALU.add))
                    inverse_of_sum(gold[:])
                    for unit_, expert, size in ORDER:
                        link(tt_(w[:, :, unit_:unit_ + size], gold[:, :, expert:expert + size],
                                 over(sum1[:], size), ALU.mult))

            def inverse_of_sum(v):
                link(red(sum1[:], v, AX_X, ALU.add))
                link(ts(sum1[:], sum1[:], 1e-8, None, ALU.max))
                link(nc.vector.reciprocal(sum1[:], sum1[:]))

            def add_down(m, f, tt, u, stats_after=False):
                for c in range(CPB):
                    n = CPB * m + c
                    ch = tt * CPB + c
                    w = wts[:, ch, bass.ds(u, 1)] if gated else wts[:, ch, bass.ds(F * u + f, 1)]
                    dve.wait_ge(s_dn, n + 1)
                    if not (isinstance(m, int) and m == 0):
                        dve.wait_ge(s_acc, n - CPB + 1)
                    stt(out=acc[:, ch], in0=pd[:, c], scalar=w, in1=acc[:, ch],
                        op0=ALU.mult, op1=ALU.add).then_inc(s_acc, 1)
                    if stats_after:
                        dve.wait_ge(s_acc, n + 1)
                        if c == 0:
                            dve.wait_ge(s_norm, CPB * tt)
                        nc.vector.bn_stats(stats[:, c], acc[:, ch]).then_inc(s_bn, 1)

            def finish(n, part):
                if part == 0:
                    dve.wait_ge(s_acc, CPB * (F * NB * (UNITS - 1) + F * n + F))
                    if n:
                        dve.wait_ge(s_norm, CPB * n)
                    for c in range(CPB):
                        nc.vector.bn_stats(stats[:, c], acc[:, n * CPB + c]).then_inc(s_bn, 1)
                if part == 1:
                    for c in range(CPB):
                        dve.wait_ge(s_bn, CPB * n + c + 1)
                        nc.vector.bn_aggr(mv[:, c], stats[:, c]).then_inc(s_mv, 1)
                if part == 2:
                    dve.wait_ge(s_rstd, n + 1)
                if part >= 2:
                    for c in (2 * part - 4, 2 * part - 3):
                        ch = n * CPB + c
                        ts(acc[:, ch], acc[:, ch], mv[:, c, 0:1], rstd[:, c:c + 1], ALU.subtract,
                           ALU.mult).then_inc(s_norm, 1)

            def unit(u, first, last, second=False):
                for tt in range(NB):
                    for f in range(F):
                        m = F * NB * u + F * tt + f
                        if gated and (first or second) and tt:
                            merge(u, F * (tt - 1) + f)
                        if gated:
                            dve.wait_ge(s_act, m + 1)
                            if not (first and m < 2):
                                dve.wait_ge(s_hlo, m - 1)
                            tt_(h_f[:, f % 2], pu[:, (f % RING) * NU + 1], act_f[:, f % 2], ALU.mult).then_inc(s_hf, 1)
                        if not (first and tt == 0):
                            add_down(m - F, f, (tt - 1) % NB, u - 1 if tt == 0 else u)
                        if tt == NB - 1 and not last:
                            up_low(u + 1, f)
                        if tt == 0:
                            dve.wait_ge(s_dhi, F * u + f + 1)
                            tt_(dn_lo[:, f], dn_raw[:, f], raw(dn_hi[:, f]), ALU.subtract).then_inc(s_dlo, 1)
                        if first and gated:
                            router_golden(tt, f)
                        elif first:
                            router_blocks(tt, f)
                        if last and tt >= 2:
                            finish(tt - 2, f)

            dve.wait_ge(s_small, 32)
            dve.wait_ge(s_mem, 3)
            unit(0, True, False)
            unit(1, False, False, True)
            with dve.Fori(2, UNITS - 1) as u:
                unit(u, False, False)
            unit(UNITS - 1, False, True)
            for f in range(F):
                if f == F - 1:
                    finish(NB - 2, f)
                add_down(F * NB * UNITS - F + f, f, NB - 1, UNITS - 1, stats_after=f == F - 1)
                if f < F - 1:
                    finish(NB - 2, f)
            for part in range(1, 4):
                finish(NB - 1, part)
            dve.wait_ge(s_norm, NCH)


def attn_phase(nc, t, acc, w_qkv):
    with ExitStack() as ctx:
        k = Kit(nc, ctx, "attn")
        AH, AD = 16, 32
        G = DM // P
        HG = AH // G
        VW, OW = P + 1, P + HG
        AEPS = 1e-15
        HALF = KT // 2
        W_CUTS = [(slice(0, HALF), slice(0, DM)), (slice(HALF, KT), slice(0, DM)),
                  (slice(0, KT), slice(DM, 2 * DM)), (slice(0, KT), slice(2 * DM, 3 * DM))]
        wp_raw = k.sb("wp_raw", [P, KT, DM])
        wq_hi, wq_lo = (k.sb(n, [P, KT, 3 * DM], F32R) for n in ("wq_hi", "wq_lo"))
        wp_hi, wp_lo = (k.sb(n, [P, KT, DM], F32R) for n in ("wp_hi", "wp_lo"))
        bias = k.sb("bias", [P, DM])
        xt = k.sb("xt", [P, DM])
        x_hi, x_lo = (k.sb(n, [P, KT, P], F32R) for n in ("x_hi", "x_lo"))
        q, kk = k.sb("q", [P, DM]), k.sb("k", [P, DM])
        vo = k.sb("vo", [P, G, VW])
        qT = k.sb("qT", [P, CPB, G, P])
        bd = k.sb("bd", [P, G, OW])
        same = k.sb("same", [P, HG, AD])
        den = k.sb("den", [P, G, HG])
        o = k.sb("o", [P, G, HG, AD])
        o_hi, o_lo = (k.sb(n, [P, KT, P], F32R) for n in ("o_hi", "o_lo"))
        rr = k.sb("rr", [P, DM])
        ident = k.sb("ident", [P, P])
        stats, mv = k.sb("stats", [P, 6]), k.sb("mv", [P, 2])
        rstd, const = k.sb("rstd", [P, 1]), k.sb("const", [P, 2])
        pt, pq, pk, pv = (k.ps(n, [P, 512]) for n in ("pt", "pq", "pk", "pv"))
        pvk, po = k.ps("pvk", [P, 2, 512]), k.ps("po", [P, 2, 512])

        s_small = k.sem("bias_loaded")
        s_w = k.sem("w_loaded")
        s_whi, s_wlo = k.sem("w_hi_ready"), k.sem("w_lo_ready")
        s_ident, s_mem = k.sem("ident_ready"), k.sem("constants_ready")
        s_xt, s_xT, s_xhi, s_xlo = (k.sem(n) for n in ("x_copied", "x_transposed", "x_hi_ready", "x_lo_ready"))
        s_q, s_k, s_v = k.sem("q_summed"), k.sem("k_summed"), k.sem("v_summed")
        s_qr, s_kr, s_vr = k.sem("q_ready"), k.sem("k_ready"), k.sem("v_ready")
        s_qT, s_qTc = k.sem("q_transposed"), k.sem("q_turned_ready")
        s_vk, s_bd = k.sem("vk_summed"), k.sem("vk_ready")
        s_o, s_od = k.sem("out_summed"), k.sem("out_ready")
        s_oT, s_ohi, s_olo = k.sem("out_transposed"), k.sem("out_hi_ready"), k.sem("out_lo_ready")
        s_p, s_pa, s_rr = k.sem("projected"), k.sem("projection_taken"), k.sem("residual_added")
        s_bn, s_mv, s_eps, s_rstd, s_norm = (k.sem(n) for n in ("bn_stats_ready", "mv_ready", "eps_added",
                                                               "rstd_ready", "normalized"))
        c_dve = k.sem("dve_steps")
        block = k.block()

        def rounds(eng, make, take):
            make(0, True, False)
            with eng.Fori(1, NB - 1) as b:
                make(b, False, False)
            make(NB - 1, False, True)
            take()

        @block.sync
        def _(sp):
            sp.dma_start(bias[:], t["proj_b"]).then_inc(s_small, 16)
            sp.dma_start(wp_raw[:], t["proj_w"]).then_inc(s_w, 16)

        @block.gpsimd
        def _(pool):
            make_identity(nc, pool, ident[:], s_ident)
            nc.gpsimd.memset(const[:, 0:1], EPS).then_inc(s_mem, 1)
            nc.gpsimd.memset(const[:, 1:2], -0.5).then_inc(s_mem, 1)
            nc.gpsimd.memset(vo[:], 1.0).then_inc(s_mem, 1)
            nc.gpsimd.memset(same[:], 1.0).then_inc(s_mem, 1)
            pool.wait_ge(s_mem, 4)
            nc.gpsimd.affine_select(out=same[:], in_=same[:], compare_op=ALU.is_ge, fill=0.0, base=0,
                                    pattern=[[-AD, HG], [0, AD]], channel_multiplier=1).then_inc(s_mem, 1)
            pool.wait_ge(s_mem, 5)
            nc.gpsimd.affine_select(out=same[:], in_=same[:], compare_op=ALU.is_ge, fill=0.0, base=AD - 1,
                                    pattern=[[AD, HG], [0, AD]], channel_multiplier=-1).then_inc(s_mem, 1)

            with pool.Fori(0, NB) as b:
                for c in range(CPB):
                    inverse_deviation(nc, pool, mv[:], rstd[:], const[:], s_mv, s_eps, s_rstd, CPB * b + c + 1)

        @block.scalar
        def _(act):
            def take_x(n):
                if not isinstance(n, int) or n:
                    act.wait_ge(s_xT, n)
                nc.scalar.activation(xt[:].unsqueeze(1), acc[:, bass.ds(n, 1)], ACT.Copy).then_inc(s_xt, 1)

            def cut_x(n):
                act.wait_ge(s_xT, n + 1)
                if not isinstance(n, int) or n:
                    act.wait_ge(s_v, n)
                nc.scalar.activation(x_hi[:].rearrange("p k n -> p (k n)"), pt[:], ACT.Copy).then_inc(s_xhi, 1)

            def cut_out(m):
                act.wait_ge(s_oT, m + 1 + 1)
                act.wait_ge(s_p, m + 1)
                nc.scalar.activation(o_hi[:].rearrange("p k n -> p (k n)"), pk[:], ACT.Copy).then_inc(s_ohi, 1)

            def make(b, first, last):
                for c in range(CPB):
                    n = CPB * b + c
                    act.wait_ge(s_q, n + 1)
                    if not (first and c == 0):
                        act.wait_ge(s_qT, n)
                    nc.scalar.activation(q[:], pq[:], ACT.Relu).then_inc(s_qr, 1)
                    if not (last and c == CPB - 1):
                        take_x(n + 1)
                    act.wait_ge(s_k, n + 1)
                    if not (first and c == 0):
                        act.wait_ge(s_vk, n)
                    nc.scalar.activation(kk[:], pk[:], ACT.Relu).then_inc(s_kr, 1)
                    act.wait_ge(s_qT, n + 1)
                    if not first:
                        act.wait_ge(s_o, n - CPB + 1)
                    nc.scalar.activation(qT[:, c].rearrange("p g n -> p (g n)"), pq[:], ACT.Copy).then_inc(s_qTc, 1)
                    if not first:
                        cut_out(n - CPB)
                    if first and c == 0:
                        act.wait_ge(s_w, 16)
                        nc.scalar.activation(wp_hi[:], wp_raw[:], ACT.Copy).then_inc(s_whi, 1)
                    if not (last and c == CPB - 1):
                        cut_x(n + 1)

            def take():
                for c in range(CPB):
                    cut_out(NCH - CPB + c)

            take_x(0)
            for i, (kt, w) in enumerate(W_CUTS):
                if i == 2:
                    cut_x(0)
                nc.scalar.activation(wq_hi[:, kt, w], w_qkv[:, kt, w], ACT.Copy).then_inc(s_whi, 1)
            rounds(act, make, take)

        @block.tensor
        def _(pe):
            pe.sem_inc(s_oT, 1)
            pe.sem_inc(s_p, 1)
            pe.wait_ge(s_ident, 2)
            pe.wait_ge(s_mem, 6)

            def turn_x(n):
                pe.wait_ge(s_xt, n + 1)
                if not isinstance(n, int) or n:
                    pe.wait_ge(s_xlo, n)
                for kt in range(KT):
                    ins = pe.transpose(pt[:, bass.ts(kt, P)], xt[:, bass.ts(kt, P)], ident[:])
                ins.then_inc(s_xT, 1)

            def qkv(i, sem, cut_first):
                if cut_first:
                    pe.wait_ge(s_wlo, i + 2)
                for kt in range(KT):
                    ins = product(pe, (pq, pk, pv)[i][:], (x_hi[:, kt], x_lo[:, kt]),
                                  (wq_hi[:, kt, bass.ts(i, DM)], wq_lo[:, kt, bass.ts(i, DM)]),
                                  kt == 0, kt == KT - 1)
                ins.then_inc(sem, 1)

            def turn_q(n):
                pe.wait_ge(s_qr, n + 1)
                for g in range(G):
                    ins = pe.transpose(pq[:, bass.ts(g, P)], q[:, bass.ts(g, P)], ident[:])
                ins.then_inc(s_qT, 1)

            def add_vk(n, c):
                pe.wait_ge(s_vr, n + 1)
                for g in range(G):
                    bank = pvk[:, g // 2, (g % 2) * 256:(g % 2) * 256 + VW]
                    ins = pe.matmul(bank, kk[:, bass.ts(g, P)], vo[:, g], start=(c == 0 and g % 2 == 0),
                                    stop=(c == CPB - 1), skip_group_check=True)
                ins.then_inc(s_vk, 1)

            def attend(m, c):
                pe.wait_ge(s_od, m + 1)
                for g in range(G):
                    ins = pe.matmul(po[:, g // 2, (g % 2) * 256:(g % 2) * 256 + OW], qT[:, c, g], bd[:, g],
                                    start=True, stop=True)
                ins.then_inc(s_o, 1)

            def turn_out(m):
                pe.wait_ge(s_od, m + 1 + 1)
                for kt in range(KT):
                    ins = pe.transpose(pk[:, bass.ts(kt, P)], o[:, kt].rearrange("p h d -> p (h d)"), ident[:])
                ins.then_inc(s_oT, 1)

            def project(m, bank):
                pe.wait_ge(s_olo, m + 1 + 1)
                for kt in range(KT):
                    ins = product(pe, bank[:], (o_hi[:, kt], o_lo[:, kt]), (wp_hi[:, kt], wp_lo[:, kt]),
                                  kt == 0, kt == KT - 1)
                ins.then_inc(s_p, 1)

            def make(b, first, last):
                for c in range(CPB):
                    n = CPB * b + c
                    m = n - CPB
                    pe.wait_ge(s_xlo, n + 1)
                    if not (first and c == 0):
                        pe.wait_ge(s_qTc, n)
                    qkv(0, s_q, first and c == 0)
                    if not first:
                        if c == 0:
                            pe.wait_ge(s_bd, b)
                        attend(m, c)
                        pe.wait_ge(s_olo, m + 1)
                    if not (first and c == 0):
                        pe.wait_ge(s_kr, n)
                    qkv(1, s_k, first and c == 0)
                    turn_q(n)
                    if not first:
                        pe.wait_ge(s_pa, m + 1)
                    if not (first and c == 0):
                        pe.wait_ge(s_vr, n)
                    qkv(2, s_v, first and c == 0)
                    pe.wait_ge(s_kr, n + 1)
                    if not first:
                        turn_out(m)
                    if not (last and c == CPB - 1):
                        turn_x(n + 1)
                    add_vk(n, c)
                    if not first:
                        if c == 0:
                            pe.wait_ge(s_wlo, 5)
                        project(m, pv)

            def take():
                pe.wait_ge(s_bd, NB)
                pe.wait_ge(s_qTc, NCH)
                attend(NCH - CPB, 0)
                for c in range(CPB):
                    m = NCH - CPB + c
                    pe.wait_ge(s_olo, m + 1)
                    turn_out(m)
                    if c < CPB - 1:
                        attend(m + 1, c + 1)
                    pe.wait_ge(s_pa, m if c else m + 1)
                    project(m, (pv, pq)[c % 2])

            turn_x(0)
            rounds(pe, make, take)

        @block.vector
        def _(dve):
            tt, ts = nc.vector.tensor_tensor, nc.vector.tensor_scalar
            chain = Chain(dve, c_dve, 2 * CPB)
            flat = lambda ap: ap.rearrange("p k n -> p (k n)")
            for sem in (s_od, s_olo, s_pa, s_norm):
                dve.sem_inc(sem, 1)

            def low_x(n):
                dve.wait_ge(s_xhi, n + 1)
                tt(flat(x_lo[:]), pt[:], raw(flat(x_hi[:])), ALU.subtract).then_inc(s_xlo, 1)

            def norm_in(m, bank):
                dve.wait_ge(s_p, m + 1 + 1)
                dve.wait_ge(s_norm, m + 1)
                tt(rr[:], bank[:], bias[:], ALU.add).then_inc(s_pa, 1)
                dve.wait_ge(s_pa, m + 1 + 1)
                tt(rr[:].unsqueeze(1), rr[:].unsqueeze(1), acc[:, bass.ds(m, 1)], ALU.add).then_inc(s_rr, 1)
                dve.wait_ge(s_rr, m + 1)
                layer_norm_stats(nc, dve, rr[:], stats[:], mv[:], s_bn, s_mv, m + 1, s_small)

            def norm_out(m):
                dve.wait_ge(s_rstd, m + 1)
                ts(acc[:, bass.ds(m, 1)], rr[:].unsqueeze(1), mv[:, 0:1], rstd[:], ALU.subtract,
                   ALU.mult).then_inc(s_norm, 1)

            def divide(m):
                dve.wait_ge(s_o, m + 1)
                outs = po[:].rearrange("p t (g n) -> p (t g) n", g=2)
                chain.link(ts(den[:], outs[:, :, P:OW], AEPS, None, ALU.add))
                chain.link(nc.vector.reciprocal(den[:], den[:]))
                dve.wait_ge(s_oT, m + 1)
                for g in range(G):
                    ins = tt(o[:, g], outs[:, g, 0:P].rearrange("p (h d) -> p h d", h=HG),
                             den[:, g].unsqueeze(2).broadcast_to([P, HG, AD]), ALU.mult)
                ins.then_inc(s_od, 1)

            def low_out(m):
                dve.wait_ge(s_ohi, m + 1)
                tt(flat(o_lo[:]), pk[:], raw(flat(o_hi[:])), ALU.subtract).then_inc(s_olo, 1)

            def mask_vk(b, first):
                dve.wait_ge(s_vk, CPB * b + CPB)
                if not first:
                    dve.wait_ge(s_o, CPB * b)
                for i in range(2):
                    two = pvk[:, i].rearrange("p (g n) -> p g n", g=2)
                    for g in range(2):
                        sums = two[:, g, P:P + 1].broadcast_to([P, HG])
                        tt(bd[:, 2 * i + g, 0:P], two[:, g, 0:P], same[:].rearrange("p h d -> p (h d)"), ALU.mult)
                        ins = tt(bd[:, 2 * i + g, P:OW], sums, same[:, :, 0], ALU.mult)
                ins.then_inc(s_bd, 1)

            def make(b, first, last):
                if not first:
                    chain.round(b - 1)
                for c in range(CPB):
                    n = CPB * b + c
                    m = n - CPB
                    if not first:
                        divide(m)
                    dve.wait_ge(s_v, n + 1)
                    if not (first and c == 0):
                        dve.wait_ge(s_vk, n)
                    nc.vector.tensor_copy(vo[:, :, 0:P], pv[:].rearrange("p (g n) -> p g n", g=G)).then_inc(s_vr, 1)
                    if not first:
                        low_out(m)
                    if not (last and c == CPB - 1):
                        low_x(n + 1)
                    if first and c == 0:
                        dve.wait_ge(s_whi, 5)
                        tt(wp_lo[:], wp_raw[:], raw(wp_hi[:]), ALU.subtract).then_inc(s_wlo, 1)
                    if c == CPB - 1:
                        mask_vk(b, first)
                    if not first and not (last and c == CPB - 1):
                        norm_in(m, pv)
                        norm_out(m)

            def take():
                chain.round(NB - 1)
                for c in range(CPB):
                    m = NCH - CPB + c
                    divide(m)
                    if c:
                        norm_out(m - 2)
                    low_out(m)
                    norm_in(m - 1, (pv, pq)[(c - 1) % 2] if c else pv)
                norm_out(NCH - 2)
                norm_in(NCH - 1, (pv, pq)[(CPB - 1) % 2])
                norm_out(NCH - 1)

            for i, (kt, w) in enumerate(W_CUTS):
                if i == 2:
                    low_x(0)
                dve.wait_ge(s_whi, i + 1)
                tt(wq_lo[:, kt, w], w_qkv[:, kt, w], raw(wq_hi[:, kt, w]), ALU.subtract).then_inc(s_wlo, 1)
            dve.wait_ge(s_mem, 6)
            dve.wait_ge(s_small, 16)
            rounds(dve, make, take)
            dve.wait_ge(s_norm, NCH + 1)


def build(nc, t):
    with nc.sbuf_tensor("pre", [P, TOK * DM // P], F32) as pre, nc.sbuf_tensor("x_raw", [P, IT, P], F32) as x_raw:
        in_proj(nc, t, pre, x_raw)
        ssd_phase(nc, t, pre, x_raw)
    with nc.sbuf_tensor("acc", [P, NCH, DM], F32) as acc:
        with nc.sbuf_tensor("w_qkv", [P, KT, 3 * DM], F32) as w_qkv:
            ffn_phase(nc, t, acc, gated=False, w_qkv=w_qkv)
            attn_phase(nc, t, acc, w_qkv)
        ffn_phase(nc, t, acc, gated=True)


def lay_out(inp):
    import numpy as np

    def cm(w):
        return w.T.reshape(w.shape[1] // P, P, w.shape[0]).transpose(1, 0, 2)

    def rows(v):
        return np.broadcast_to(v, (P, v.shape[0]))

    def up_tiles(w):
        u, n = w.shape[:2]
        return w.reshape(u, n, KT, P, 4, P).transpose(0, 3, 1, 4, 2, 5)

    def down_tiles(w):
        return w.reshape(w.shape[0], 4, P, DM).transpose(0, 2, 1, 3)

    a = {n: np.asarray(v) for n, v in inp.items()}
    w = a["L0_attn_in_proj_w"].reshape(2, IT, P, DM).transpose(1, 0, 2, 3).reshape(2 * DI, DM)
    order = [2, 0, 1] + list(range(3, 8))
    laid = {
        "x": a["L0_attn_x"],
        "x_rows": a["L0_attn_x"].reshape(TOK, DM),
        "in_w": cm(w).reshape(P, KT, 4, 4 * P).transpose(0, 2, 1, 3),
        "conv_w": a["L0_attn_conv_w"].reshape(IT, P, TAPS).transpose(1, 0, 2),
        "conv_b": a["L0_attn_conv_b"].reshape(IT, P).T,
        "x_w": cm(a["L0_attn_x_proj_w"]),
        "out_w": cm(a["L0_attn_out_proj_w"]).reshape(P, IT // 2, 2 * DM),
        "dtw": a["L0_attn_dt_proj_w"].T,
        "dtb": rows(a["L0_attn_dt_proj_b"]),
        "a_log": rows(a["L0_attn_A_log"]),
        "d_skip": rows(a["L0_attn_D"]),
        "f_router": cm(a["L0_ffn_Wr"]),
        "f_rb": rows(a["L0_ffn_br"]),
        "f_up": up_tiles(a["L0_ffn_W1"].T.reshape(DM, 4, 1, DM).transpose(1, 2, 0, 3)),
        "f_dn": down_tiles(a["L0_ffn_W2"].T.reshape(4, DM, DM)),
        "qkv_w": cm(a["L1_attn_w_qkv"]),
        "proj_w": cm(a["L1_attn_w_proj"]),
        "proj_b": rows(a["L1_attn_b_proj"]),
        "e_router": a["L1_ffn_Wr"].reshape(KT, P, 8).transpose(1, 0, 2),
        "e_rb": rows(a["L1_ffn_temperature"]),
        "e_up": up_tiles(np.stack([a["L1_ffn_Wg"], a["L1_ffn_Wu"]], 1))[order],
        "e_dn": down_tiles(a["L1_ffn_Wd"])[order],
        "la_up": np.stack([a["L1_ffn_Ga"], a["L1_ffn_Ua"]], 1).transpose(0, 1, 3, 2).reshape(2, P, DM),
        "lb_up": np.stack([a["L1_ffn_Gb"], a["L1_ffn_Ub"]], 1).reshape(2, P, DM),
        "la_dn": a["L1_ffn_Da"].transpose(0, 2, 1),
        "lb_dn": a["L1_ffn_Db"],
    }
    return {n: np.ascontiguousarray(v) for n, v in laid.items()}


def kernel(**inputs):
    import concourse.bacc as bacc
    from concourse.bass_utils import run_bass_kernel_spmd as run

    laid = lay_out(inputs)
    nc = bacc.Bacc("TRN2", target_bir_lowering=False, num_devices=1)
    t = {n: nc.dram_tensor(f"in_{n}", v.shape, F32, kind="ExternalInput").ap() for n, v in laid.items()}
    for n, shape in (("xb", (IT, P, TOK)), ("zs", (IT, P, TOK)), ("x1", (TOK, DM))):
        t[n] = nc.dram_tensor(n, shape, F32, kind="Internal").ap()
    t["out"] = nc.dram_tensor("out", (NB, SEQ, DM), F32, kind="ExternalOutput").ap()
    build(nc, t)
    r = run(nc, [{f"in_{n}": v for n, v in laid.items()}], core_ids=[0])
    return r.results[0]["out"]
```
